# Optimizing a Trainium2 kernel written in Bass

```python
import numpy as np
import jax
import jax.numpy as jnp

def _softmax(x, axis=-1):
    return jax.nn.softmax(x, axis=axis)

def _gelu(x):
    return jax.nn.gelu(x, approximate=True)

def _silu(x):
    return jax.nn.silu(x)

def _sigmoid(x):
    return jax.nn.sigmoid(x)

def _layernorm(x, axis=-1, eps=1e-05):
    m = jnp.mean(x, axis=axis, keepdims=True)
    v = jnp.var(x, axis=axis, keepdims=True)
    return (x - m) / jnp.sqrt(v + eps)

def _scatter_add(tgt, idx, src, axis=0):
    return tgt.at[idx].add(src)

def _segment_sum(src, seg, n):
    return jax.ops.segment_sum(src, seg, n)
kernel_name = 'mk_recurrent_d2_jaxref_r8_7746d0'

def setup_inputs(seed: int=0):
    np.random.seed(seed)
    _w = jnp.asarray

    def _L0_attn_setup():
        import jax, jax.numpy as jnp
        import numpy as np
        import math
        D_MODEL = 128
        N_HEADS = 16
        D_K = D_MODEL // N_HEADS
        MAX_REL = 128

        def _rel_bias_matrix(rel_bias, seq_len):
            pos = jnp.arange(seq_len)
            rel = pos[:, None] - pos[None, :]
            idx = jnp.clip(rel, -MAX_REL, MAX_REL) + MAX_REL
            return rel_bias[:, idx]
        key = jax.random.key(seed)
        ks = jax.random.split(key, 10)
        B, S = (2, 256)
        std = 1.0 / math.sqrt(D_MODEL)
        inp = {'x': jax.random.normal(ks[0], (B, S, D_MODEL), dtype=jnp.float32), 'Wq': jax.random.normal(ks[1], (D_MODEL, D_MODEL), dtype=jnp.float32) * std, 'bq': jnp.zeros((D_MODEL,), dtype=jnp.float32), 'Wk': jax.random.normal(ks[2], (D_MODEL, D_MODEL), dtype=jnp.float32) * std, 'bk': jnp.zeros((D_MODEL,), dtype=jnp.float32), 'Wv': jax.random.normal(ks[3], (D_MODEL, D_MODEL), dtype=jnp.float32) * std, 'bv': jnp.zeros((D_MODEL,), dtype=jnp.float32), 'Wo': jax.random.normal(ks[4], (D_MODEL, D_MODEL), dtype=jnp.float32) * std, 'bo': jnp.zeros((D_MODEL,), dtype=jnp.float32), 'rel_bias': jax.random.normal(ks[5], (N_HEADS, 2 * MAX_REL + 1), dtype=jnp.float32) * 0.02}
        return inp
    _L0_attn_in = _L0_attn_setup()

    def _L0_ffn_setup():
        import jax, jax.numpy as jnp
        import numpy as np
        B, S, D, E, H, DO = (4, 256, 128, 8, 512, 128)
        TOP_K = 2
        LN_EPS = 1e-05
        key = jax.random.key(seed)
        ks = jax.random.split(key, 9)
        s = 0.02
        return {'x': jax.random.normal(ks[0], (B, S, D), dtype=jnp.float32), 'W1': jax.random.normal(ks[1], (E, D, H), dtype=jnp.float32) * s, 'b1': jnp.zeros((E, H), dtype=jnp.float32), 'W2': jax.random.normal(ks[2], (E, H, DO), dtype=jnp.float32) * s, 'b2': jnp.zeros((E, DO), dtype=jnp.float32), 'gate_W': jax.random.normal(ks[3], (D, E), dtype=jnp.float32) * s, 'shared_W': jax.random.normal(ks[4], (D, DO), dtype=jnp.float32) * s, 'shared_b': jnp.zeros((DO,), dtype=jnp.float32), 'gamma': jnp.ones((DO,), dtype=jnp.float32), 'beta': jnp.zeros((DO,), dtype=jnp.float32)}
    _L0_ffn_in = _L0_ffn_setup()

    def _L1_attn_setup():
        import jax, jax.numpy as jnp
        import numpy as np
        DIM = 128
        DIM_HEADS = 128
        HEADS = 8
        DHEAD = DIM_HEADS // HEADS
        EPS = 1e-06

        def _l2norm(t, axis=-1):
            n = jnp.sqrt(jnp.sum(t * t, axis=axis, keepdims=True))
            return t / jnp.maximum(n, 1e-12)
        key = jax.random.key(seed)
        k1, k2, k3 = jax.random.split(key, 3)
        x = jax.random.normal(k1, (8, 512, DIM), dtype=jnp.float32)
        norm_weight = jnp.ones((DIM,), dtype=jnp.float32)
        w_qkv = jax.random.normal(k2, (3 * DIM_HEADS, DIM), dtype=jnp.float32) * (1.0 / np.sqrt(DIM))
        temperature = jnp.zeros((HEADS, 1, 1), dtype=jnp.float32)
        w_out = jax.random.normal(k3, (DIM, DIM_HEADS), dtype=jnp.float32) * (1.0 / np.sqrt(DIM_HEADS))
        return {'x': x, 'norm_weight': norm_weight, 'w_qkv': w_qkv, 'temperature': temperature, 'w_out': w_out}
    _L1_attn_in = _L1_attn_setup()

    def _L1_ffn_setup():
        import jax, jax.numpy as jnp
        import numpy as np
        key = jax.random.key(seed)
        ks = jax.random.split(key, 6)
        B, L, D, E = (4, 256, 128, 4)
        H = 4 * D
        x = jax.random.normal(ks[0], (B, L, D), dtype=jnp.float32)
        rW1 = jax.random.normal(ks[1], (D, 2 * D), dtype=jnp.float32) * (2.0 / D) ** 0.5
        rb1 = jnp.zeros((2 * D,), dtype=jnp.float32)
        rW2 = jax.random.normal(ks[2], (2 * D, E), dtype=jnp.float32) * (2.0 / (2 * D)) ** 0.5
        rb2 = jnp.zeros((E,), dtype=jnp.float32)
        We1 = jax.random.normal(ks[3], (E, D, H), dtype=jnp.float32) * (2.0 / D) ** 0.5
        be1 = jnp.zeros((E, H), dtype=jnp.float32)
        We2 = jax.random.normal(ks[4], (E, H, D), dtype=jnp.float32) * (2.0 / H) ** 0.5
        be2 = jnp.zeros((E, D), dtype=jnp.float32)
        return {'x': x, 'rW1': rW1, 'rb1': rb1, 'rW2': rW2, 'rb2': rb2, 'We1': We1, 'be1': be1, 'We2': We2, 'be2': be2}
    _L1_ffn_in = _L1_ffn_setup()
    _d = {'L0_attn_x': _L0_attn_in['x'], 'L0_attn_Wq': _L0_attn_in['Wq'], 'L0_attn_bq': _L0_attn_in['bq'], 'L0_attn_Wk': _L0_attn_in['Wk'], 'L0_attn_bk': _L0_attn_in['bk'], 'L0_attn_Wv': _L0_attn_in['Wv'], 'L0_attn_bv': _L0_attn_in['bv'], 'L0_attn_Wo': _L0_attn_in['Wo'], 'L0_attn_bo': _L0_attn_in['bo'], 'L0_attn_rel_bias': _L0_attn_in['rel_bias'], 'L0_ffn_W1': _L0_ffn_in['W1'], 'L0_ffn_b1': _L0_ffn_in['b1'], 'L0_ffn_W2': _L0_ffn_in['W2'], 'L0_ffn_b2': _L0_ffn_in['b2'], 'L0_ffn_gate_W': _L0_ffn_in['gate_W'], 'L0_ffn_shared_W': _L0_ffn_in['shared_W'], 'L0_ffn_shared_b': _L0_ffn_in['shared_b'], 'L0_ffn_gamma': _L0_ffn_in['gamma'], 'L0_ffn_beta': _L0_ffn_in['beta'], 'L1_attn_norm_weight': _L1_attn_in['norm_weight'], 'L1_attn_w_qkv': _L1_attn_in['w_qkv'], 'L1_attn_temperature': _L1_attn_in['temperature'], 'L1_attn_w_out': _L1_attn_in['w_out'], 'L1_ffn_rW1': _L1_ffn_in['rW1'], 'L1_ffn_rb1': _L1_ffn_in['rb1'], 'L1_ffn_rW2': _L1_ffn_in['rW2'], 'L1_ffn_rb2': _L1_ffn_in['rb2'], 'L1_ffn_We1': _L1_ffn_in['We1'], 'L1_ffn_be1': _L1_ffn_in['be1'], 'L1_ffn_We2': _L1_ffn_in['We2'], 'L1_ffn_be2': _L1_ffn_in['be2']}
    _x0 = _d['L0_attn_x']
    _d['L0_attn_x'] = jax.random.normal(jax.random.fold_in(jax.random.key(seed), 1), (16, 256, 128), dtype=_x0.dtype)
    del _x0
    return _d

def reference(L0_attn_x, L0_attn_Wq, L0_attn_bq, L0_attn_Wk, L0_attn_bk, L0_attn_Wv, L0_attn_bv, L0_attn_Wo, L0_attn_bo, L0_attn_rel_bias, L0_ffn_W1, L0_ffn_b1, L0_ffn_W2, L0_ffn_b2, L0_ffn_gate_W, L0_ffn_shared_W, L0_ffn_shared_b, L0_ffn_gamma, L0_ffn_beta, L1_attn_norm_weight, L1_attn_w_qkv, L1_attn_temperature, L1_attn_w_out, L1_ffn_rW1, L1_ffn_rb1, L1_ffn_rW2, L1_ffn_rb2, L1_ffn_We1, L1_ffn_be1, L1_ffn_We2, L1_ffn_be2):

    def _L0_attn_ref(x, Wq, bq, Wk, bk, Wv, bv, Wo, bo, rel_bias):
        import jax, jax.numpy as jnp
        import numpy as np
        import math
        D_MODEL = 128
        N_HEADS = 16
        D_K = D_MODEL // N_HEADS
        MAX_REL = 128

        def _rel_bias_matrix(rel_bias, seq_len):
            pos = jnp.arange(seq_len)
            rel = pos[:, None] - pos[None, :]
            idx = jnp.clip(rel, -MAX_REL, MAX_REL) + MAX_REL
            return rel_bias[:, idx]
        B, S, _ = x.shape

        def proj(W, b):
            y = x @ W.T + b
            return y.reshape(B, S, N_HEADS, D_K).transpose(0, 2, 1, 3)
        Q, K, V = (proj(Wq, bq), proj(Wk, bk), proj(Wv, bv))
        scores = jnp.einsum('bhqd,bhkd->bhqk', Q, K) / math.sqrt(D_K)
        scores = scores + _rel_bias_matrix(rel_bias, S)[None]
        attn = jax.nn.softmax(scores, axis=-1)
        out = jnp.einsum('bhqk,bhkd->bhqd', attn, V)
        out = out.transpose(0, 2, 1, 3).reshape(B, S, D_MODEL)
        return out @ Wo.T + bo

    def _L0_ffn_ref(x, W1, b1, W2, b2, gate_W, shared_W, shared_b, gamma, beta):
        import jax, jax.numpy as jnp
        import numpy as np
        B, S, D, E, H, DO = (4, 256, 128, 8, 512, 128)
        TOP_K = 2
        LN_EPS = 1e-05
        d = x.shape[-1]
        flat = x.reshape(-1, d)
        n_exp = gate_W.shape[-1]
        probs = jax.nn.softmax(flat @ gate_W, axis=-1)
        topk_w, topk_idx = jax.lax.top_k(probs, TOP_K)
        topk_w = topk_w / topk_w.sum(axis=-1, keepdims=True)
        combine = (jax.nn.one_hot(topk_idx, n_exp, dtype=flat.dtype) * topk_w[..., None]).sum(axis=1)
        out = 0.5 * jax.nn.gelu(flat @ shared_W + shared_b, approximate=False)
        for e in range(n_exp):
            h = jax.nn.gelu(flat @ W1[e] + b1[e], approximate=False)
            out = out + combine[:, e:e + 1] * (h @ W2[e] + b2[e])
        mean = out.mean(axis=-1, keepdims=True)
        var = ((out - mean) ** 2).mean(axis=-1, keepdims=True)
        out = (out - mean) * jax.lax.rsqrt(var + LN_EPS) * gamma + beta
        return out.reshape(*x.shape[:-1], out.shape[-1])

    def _L1_attn_ref(x, norm_weight, w_qkv, temperature, w_out):
        import jax, jax.numpy as jnp
        import numpy as np
        DIM = 128
        DIM_HEADS = 128
        HEADS = 8
        DHEAD = DIM_HEADS // HEADS
        EPS = 1e-06

        def _l2norm(t, axis=-1):
            n = jnp.sqrt(jnp.sum(t * t, axis=axis, keepdims=True))
            return t / jnp.maximum(n, 1e-12)
        b, n, _ = x.shape
        ms = jnp.mean(x * x, axis=-1, keepdims=True)
        xn = x * jax.lax.rsqrt(ms + EPS) * norm_weight
        qkv = jnp.einsum('bnc,oc->bno', xn, w_qkv)
        qkv = qkv.reshape(b, n, 3, HEADS, DHEAD).transpose(2, 0, 3, 4, 1)
        q, k, v = (qkv[0], qkv[1], qkv[2])
        q = _l2norm(q)
        k = _l2norm(k)
        q = q * jnp.exp(temperature)
        sim = jnp.einsum('bhin,bhjn->bhij', q, k)
        attn = jax.nn.softmax(sim, axis=-1)
        out = jnp.einsum('bhij,bhjn->bhin', attn, v)
        out = out.transpose(0, 3, 1, 2).reshape(b, n, HEADS * DHEAD)
        return jnp.einsum('bnc,oc->bno', out, w_out)

    def _L1_ffn_ref(x, rW1, rb1, rW2, rb2, We1, be1, We2, be2):
        import jax, jax.numpy as jnp
        import numpy as np
        E = We1.shape[0]
        top_k = min(2, E)
        rh = jax.nn.gelu(x @ rW1 + rb1, approximate=False)
        router_logits = rh @ rW2 + rb2
        router_probs = jax.nn.softmax(router_logits, axis=-1)
        expert_weights, expert_indices = jax.lax.top_k(router_probs, top_k)
        one_hot = jax.nn.one_hot(expert_indices, E, dtype=x.dtype)
        token_mask = one_hot.sum(axis=2)
        combine_w = (one_hot * expert_weights[..., None]).sum(axis=2)
        out = jnp.zeros_like(x)
        for e in range(E):
            xi = x * token_mask[..., e:e + 1]
            h = jax.nn.gelu(xi @ We1[e] + be1[e], approximate=False)
            yo = h @ We2[e] + be2[e]
            out = out + yo * combine_w[..., e:e + 1]
        return out
    x = L0_attn_x
    xn = _layernorm(x, axis=-1)
    s = _L0_attn_ref(xn, L0_attn_Wq, L0_attn_bq, L0_attn_Wk, L0_attn_bk, L0_attn_Wv, L0_attn_bv, L0_attn_Wo, L0_attn_bo, L0_attn_rel_bias)
    g = _silu(_L0_ffn_ref(xn, L0_ffn_W1, L0_ffn_b1, L0_ffn_W2, L0_ffn_b2, L0_ffn_gate_W, L0_ffn_shared_W, L0_ffn_shared_b, L0_ffn_gamma, L0_ffn_beta))
    x = x + s * g
    xn = _layernorm(x, axis=-1)
    s = _L1_attn_ref(xn, L1_attn_norm_weight, L1_attn_w_qkv, L1_attn_temperature, L1_attn_w_out)
    g = _silu(_L1_ffn_ref(xn, L1_ffn_rW1, L1_ffn_rb1, L1_ffn_rW2, L1_ffn_rb2, L1_ffn_We1, L1_ffn_be1, L1_ffn_We2, L1_ffn_be2))
    x = x + s * g
    return x

_drawn_inputs = setup_inputs


def setup_inputs(seed=0):
    import zlib

    import numpy as np

    out = dict(_drawn_inputs(seed))
    spreads = {'L0_attn_bq': (0.0, 0.8),
     'L0_attn_bk': (0.0, 2.0),
     'L0_attn_bv': (0.0, 0.1),
     'L0_attn_bo': (0.0, 0.1),
     'L0_ffn_b1': (0.0, 0.344),
     'L0_ffn_b2': (0.0, 0.1),
     'L0_ffn_shared_b': (0.0, 0.1),
     'L0_ffn_gamma': (1.0, 0.2),
     'L0_ffn_beta': (0.0, 0.537),
     'L1_attn_norm_weight': (1.0, 0.2),
     'L1_attn_temperature': (0.0, 2.0),
     'L1_ffn_rb1': (0.0, 0.457),
     'L1_ffn_rb2': (0.0, 0.406),
     'L1_ffn_be1': (0.0, 0.754),
     'L1_ffn_be2': (0.0, 0.746)}
    factors = {'L0_attn_rel_bias': 28.051}
    for name, (base, spread) in spreads.items():
        noise = np.random.default_rng([zlib.crc32(name.encode()), seed]).standard_normal(out[name].shape)
        drawn = base * np.exp(spread * noise) if base else spread * noise
        out[name] = jnp.asarray(drawn.astype(out[name].dtype))
    for name, factor in factors.items():
        out[name] = (out[name] * factor).astype(out[name].dtype)
    return out
```

```python
import concourse.bass as bass
from concourse import mybir
from contextlib import ExitStack

NB, S, D = 16, 256, 128
P = 128
T = NB * S // P
H0, DK = 16, 8
MAXREL = 128
NREL = 2 * MAXREL + 1
E0, E1, HID = 8, 4, 512
HC = HID // P
H1, DH1 = 8, 16
TS = 256
TOPK = 2
TOK = NB * S
ZBLOCK = 2


def tiles_for(experts):
    n = (TOK * TOPK - experts) // TS + experts
    return n + n % 2


NJ0, NJ1 = tiles_for(E0), tiles_for(E1)
NSLOT = max(NJ0, NJ1) * TS
WROW = HID + HC * D + HC + D
EXT = 2 * S - 1
BW = S + P
LN_EPS, RMS_EPS = 1e-5, 1e-6
QSCALE = float(DK) ** -0.5
OFF = -1e30


class Steps:

    def __init__(self, eng, sem):
        self.eng, self.sem, self.base, self.k, self.it, self.per = eng, sem, 0, 0, None, 0

    def did(self, ins):
        self.k += 1
        return ins.then_inc(self.sem, 1)

    def sync(self):
        at = self.base + self.k
        self.eng.wait_ge(self.sem, at if self.it is None else self.it * self.per + at)

    def link(self, ins):
        self.did(ins)
        self.sync()

    def enter(self, it, per):
        self.base, self.k, self.it, self.per = self.base + self.k, 0, it, per

    def leave(self, turns):
        assert self.k == self.per, (self.k, self.per)
        self.base, self.k, self.it = self.base + turns * self.per, 0, None


def over(ap, n):
    return bass.AP(tensor=ap.tensor, offset=ap.offset, ap=list(ap.ap) + [[0, n]])


def mid(ap, n):
    a = list(ap.ap)
    return bass.AP(tensor=ap.tensor, offset=ap.offset, ap=[a[0], [0, n]] + a[1:])


def build(nc, x, wqT, wkT, wvT, woT, bq, bk, bv, bo, relb, wcat0, gate, shw, shb, gamma, beta,
          nw, wqkT1, wv1, woT1, temp, rw1, rb1, rw2, rb2, wcat1, out):
    fp32, bf16, i32, u32 = mybir.dt.float32, mybir.dt.bfloat16, mybir.dt.int32, mybir.dt.uint32
    ALU, ACT, AX = mybir.AluOpType, mybir.ActivationFunctionType, mybir.AxisListType

    ext_dram = nc.dram_tensor("ext_dram", [H0, EXT], fp32, kind="Internal").ap()
    xg_dram = nc.dram_tensor("xg_dram", [NSLOT, D], fp32, kind="Internal").ap()
    yg_dram = [nc.dram_tensor(f"yg_dram{l}", [(NJ0, NJ1)[l] * TS, D], fp32, kind="Internal").ap() for l in range(2)]

    ctx = ExitStack()
    with ctx:
        def sb(name, shape, dt=fp32):
            return ctx.enter_context(nc.sbuf_tensor(name, shape, dt))

        def sem(name):
            return ctx.enter_context(nc.semaphore(name))

        bufA, bufB, bufC = (sb(f"buf{c}", [P, T, D]) for c in "ABC")
        yy = sb("yy", [P, TOPK, T, D])
        x_sb = s_sb = bufA
        xres = bufB
        sh_sb = bufC
        xn_sb = (bufB, bufC)
        yyf = yy[:, :, :, :].rearrange("p k t d -> p (k t d)")
        strip = yyf[:, 0:H0 * BW].rearrange("p (h u) -> p h u", h=H0)
        xnT = yyf[:, TOK:2 * TOK]
        biasT = sb("biasT", [P, H0, BW])
        biasA = sb("biasA", [P, H0, BW], bf16)
        wqk_sb = sb("wqk_sb", [P, 2 * D])
        wv_sb = sb("wv_sb", [P, D])
        wo_sb = sb("wo_sb", [P, D])
        cols = sb("cols", [P, 8])
        bo_bc = sb("bo_bc", [P, D])
        gate_sb = sb("gate_sb", [P, E0])
        shw_sb = sb("shw_sb", [P, D])
        shb_sb = sb("shb_sb", [1, D])
        gamma_bc = sb("gamma_bc", [P, D])
        beta_bc = sb("beta_bc", [P, D])
        wqk1_sb = sb("wqk1_sb", [P, 2 * D])
        wv1_sb = sb("wv1_sb", [P, D])
        wo1_sb = sb("wo1_sb", [P, D])
        rw1_sb = sb("rw1_sb", [P, 2 * P])
        rb1_sb = sb("rb1_sb", [P, 2])
        rw2_sb = sb("rw2_sb", [P, 2, E1])
        rb2_bc = sb("rb2_bc", [P, E1])
        ext_sb = sb("ext_sb", [H0, EXT])
        ident = sb("ident", [P, P])
        identb = sb("identb", [P, P], bf16)
        flip = sb("flip", [P, P])
        below = sb("below", [P, P])
        ones = sb("ones", [P, P])
        headm = sb("headm", [P, H0])
        selh = sb("selh", [P, H0, P], bf16)
        blockm = sb("blockm", [P, P])
        eidx = sb("eidx", [P, E0])
        jidx = sb("jidx", [P, NSLOT // TS])
        pidx = sb("pidx", [P, 1])
        stats = sb("stats", [P, T, 6])
        mean = sb("mean", [P, T])
        rstd = sb("rstd", [P, T])
        rrms = sb("rrms", [P, T])
        var = sb("var", [P, T])
        tmpa = sb("tmpa", [P, T])
        tmpb = sb("tmpb", [P, T])
        lg = sb("lg", [P, T, E0])
        rt = [sb(f"rt{i}", [P, T * E0]) for i in range(4)]
        hot = [sb(f"hot{k}", [P, T * E0]) for k in range(TOPK)]
        pk = [sb(f"pk{k}", [P, T]) for k in range(TOPK)]
        wk = [sb(f"wk{k}", [P, T]) for k in range(TOPK)]
        slotf = [sb(f"slotf{k}", [P, T]) for k in range(TOPK)]
        sloti = [sb(f"sloti{k}", [P, T], i32) for k in range(TOPK)]
        ecnt = [sb(f"ecnt{i}", [P, E0]) for i in range(4)]
        ecnti = sb("ecnti", [P, E0], i32)
        ejm = sb("ejm", [P, NSLOT // TS * E0])
        ejf = sb("ejf", [P, NSLOT // TS])
        widx = sb("widx", [P, NSLOT // TS], i32)
        widx_cur = [sb(f"widx_cur{u}", [P, 1], i32) for u in range(2)]
        xs = [sb(f"xs{u}", [P, 2, D]) for u in range(2)]
        xT = [sb(f"xT{u}", [P, 2 * P]) for u in range(2)]
        rh = [sb(f"rh{u}", [P, 2, 2 * P]) for u in range(2)]
        work = sb("work", [P, 13312])

        def carve():
            at = [0]

            def take(n, dt=fp32):
                words = n if dt == fp32 else n // 2
                a = work[:, at[0]:at[0] + words]
                at[0] += words
                assert at[0] <= 13312, at
                return a if dt == fp32 else a.bitcast(dt)
            return take

        take = carve()
        qs = [take(S) for _ in range(2)]
        ks = [take(S) for _ in range(2)]
        qm = take(H0 * S).rearrange("p (h s) -> p h s", h=H0)
        qb = take(S, bf16)
        km = take(H0 * S, bf16).rearrange("p (h s) -> p h s", h=H0)
        vaug = [take(2 * H0 * 32).rearrange("p (k h c) -> p k h c", k=2, h=H0) for _ in range(2)]
        nmax = take(2 * H0, bf16).rearrange("p (q h) -> p q h", q=2)
        nmaxT = take(S, bf16)
        scores = [take(2 * S) for _ in range(2)]
        probs = [take(2 * S) for _ in range(2)]
        zero = work[:, 0:13312].rearrange("p (n r) -> p n r", r=1024)[:, ZBLOCK, :]
        oT = take(4 * S).rearrange("p (g s) -> p g s", g=4)
        on = take(2 * D).rearrange("p (q d) -> p q d", q=2)
        onT = take(2 * P)
        rden = take(2 * H0).rearrange("p (q h) -> p q h", q=2)
        take = carve()
        wb = [take(WROW) for _ in range(2)]
        xg = [take(2 * D).rearrange("p (s d) -> p s d", s=2) for _ in range(2)]
        hb = [take(HC * TS).rearrange("p (c s) -> p c s", c=HC) for _ in range(2)]
        yb = [take(2 * D).rearrange("p (s d) -> p s d", s=2) for _ in range(2)]
        take = carve()
        cc = [take(D) for _ in range(2)]
        uu = take(NB * D).rearrange("p (b o) -> p b o", b=NB)
        pr = [take(2 * D) for _ in range(2)]
        x2 = [take(2 * D).rearrange("p (j d) -> p j d", j=2) for _ in range(2)]
        x2T = [take(2 * P) for _ in range(2)]
        nsq = take(2 * NB).rearrange("p (b k) -> p b k", b=NB)
        rin = take(2 * NB).rearrange("p (b k) -> p b k", b=NB)
        nt1, nt2 = take(2 * NB), take(2 * NB)
        gk = [take(D) for _ in range(2)]
        gm = [take(D) for _ in range(2)]
        at1 = [take(D) for _ in range(2)]
        an = [take(D) for _ in range(2)]
        ms = [take(D) for _ in range(2)]
        ps_ = [take(D) for _ in range(2)]
        nm1 = [take(1) for _ in range(2)]
        sm1 = [take(1) for _ in range(2)]
        rs1 = [take(1) for _ in range(2)]

        bank = [ctx.enter_context(nc.psum_tensor(f"bank{i}", [P, 512], fp32)) for i in range(8)]

        bq_c, bk_c, bv_c, nw_c, temp_c, bqs_c, et_c = (cols[:, i:i + 1] for i in range(7))

        s_x, s_w, s_wf = sem("x_loaded"), sem("weights_loaded"), sem("weights_folded")
        s_c, s_cc = sem("constants_made"), sem("constant_steps")
        s_relb, s_edge, s_extd, s_strip = sem("relb_loaded"), sem("edges_filled"), sem("ext_stored"), sem("strip_loaded")
        s_fl, s_fle, s_ba = sem("strip_flipped"), sem("strip_evacuated"), sem("biasA_made")
        s_zero, s_xgz = sem("zero_made"), sem("xg_zeroed")
        s_dve, s_pool, s_act = sem("dve_steps"), sem("pool_steps"), sem("act_steps")

        block = ctx.enter_context(nc.Block())

        def phase_sems(phase, l, names):
            return {n: sem(f"{phase}{l}_{n}") for n in names}

        PRE = ["xs", "xs_saved", "T", "xT", "xT_read", "xT_saved", "gs", "lg", "sh", "rh1", "rhs"]
        pre = [phase_sems("pre", l, PRE) for l in range(2)]
        ROU = ["lgx", "exped", "A", "cum", "routed", "scattered"]
        rou = [phase_sems("route", l, ROU) for l in range(2)]
        MOE = ["W0", "W1", "xg0", "xg1", "T", "xT", "up", "gelu", "down", "y", "st0", "st1", "widx"]
        moe = [phase_sems("experts", l, MOE) for l in range(2)]
        COM = [f"g{i}" for i in range(4)] + ["z", "silu", "x1"]
        com = [phase_sems("combine", l, COM) for l in range(2)]
        s_out, s_x2 = sem("out_stored"), sem("x_back")
        A0 = phase_sems("attend", 0, ["xTs", "qkv", "qk_sb", "v_sb", "qb", "km", "A", "Ared", "mT", "nmT", "B", "S", "E",
                            "PV", "Og", "oTs", "To", "on", "Tn", "onT", "wo", "s", "qm", "s2"])
        A1 = phase_sems("attend", 1, ["x2", "C", "Cs", "U", "Us", "pr", "nn", "nns", "rin",
                            "x2b", "T", "x2T", "G", "gk", "GT", "gm", "mx", "exp", "rs", "an", "M", "Ms", "Pm", "Ps", "F", "s"])

        NW = 22

        @block.sync
        def _(sp):
            sp.dma_start(ext_sb[:, S - 1 - MAXREL:S + MAXREL], relb).then_inc(s_relb, 16)
            xv = x.rearrange("(t p) d -> p t d", p=P)
            for c in range(4):
                sp.dma_start(x_sb[:, c * 8:c * 8 + 8, :], xv[:, c * 8:c * 8 + 8, :]).then_inc(s_x, 16)
            loads = [(wqk_sb[:, 0:D], wqT), (wqk_sb[:, D:2 * D], wkT), (wv_sb[:, :], wvT), (wo_sb[:, :], woT),
                     (bq_c, bq), (bk_c, bk), (bv_c, bv), (nw_c, nw), (temp_c, temp),
                     (bo_bc[:, :], bo.partition_broadcast(P)), (gate_sb[:, :], gate), (shw_sb[:, :], shw),
                     (shb_sb[:, :], shb.unsqueeze(0)), (gamma_bc[:, :], gamma.partition_broadcast(P)),
                     (beta_bc[:, :], beta.partition_broadcast(P)), (wqk1_sb[:, :], wqkT1), (wv1_sb[:, :], wv1),
                     (wo1_sb[:, :], woT1), (rw1_sb[:, :], rw1), (rb1_sb[:, :], rb1), (rw2_sb[:, :, :], rw2),
                     (rb2_bc[:, :], rb2.partition_broadcast(P))]
            assert len(loads) == NW
            for dst, src in loads:
                sp.dma_start(dst, src).then_inc(s_w, 16)
            sp.wait_ge(s_edge, 2)
            sp.dma_start(ext_dram, ext_sb[:, :]).then_inc(s_extd, 16)
            sp.wait_ge(s_extd, 16)
            sp.dma_start(strip, bass.AP(tensor=ext_dram.tensor, offset=0, ap=[[1, P], [EXT, H0], [1, BW]])
                         ).then_inc(s_strip, 16)
            sp.wait_ge(s_zero, 1)
            for c in range(NSLOT * D // (P * 1024)):
                sp.dma_start(xg_dram.rearrange("(c p r) d -> c p (r d)", p=P, r=8)[c], zero).then_inc(s_xgz, 16)
            for l, nj in enumerate((NJ0, NJ1)):
                m = moe[l]
                xgv = xg_dram.rearrange("(j s p) d -> j p s d", s=2, p=P)
                ygv = yg_dram[l].rearrange("(j s p) d -> j p s d", s=2, p=P)

                def load(j, u):
                    sp.wait_ge(m["T"], j + 1)
                    src = xgv[j] if isinstance(j, int) else xgv[bass.ds(j, 1)].rearrange("o p s d -> p (o s) d")
                    sp.dma_start(xg[u], src).then_inc(m[f"xg{u}"], 16)

                def store(j, u):
                    sp.wait_ge(m["y"], j + 3)
                    dst = ygv[j] if isinstance(j, int) else ygv[bass.ds(j, 1)].rearrange("o p s d -> p (o s) d")
                    sp.dma_start(dst, yb[u]).then_inc(m[f"st{u}"], 16)

                sp.wait_ge(rou[l]["scattered"], 16 * TOPK * T)
                if l == 0:
                    sp.dma_start(xres[:, :, :], xv).then_inc(s_x2, 16)
                sp.wait_ge((A0, A1)[l]["s"], NB + (3, 1)[l])
                load(0, 0)
                load(1, 1)
                with sp.Fori(0, nj // 2 - 1) as it:
                    for u in range(2):
                        load(it * 2 + u + 2, u)
                        store(it * 2 + u, u)
                store(nj - 2, 0)
                store(nj - 1, 1)
            ov = out.rearrange("(t p) d -> p t d", p=P)
            for g in range(4):
                sp.wait_ge(com[1]["x1"], g + 1)
                sp.dma_start(ov[:, g * 8:g * 8 + 8, :], yy[:, 0, g * 8:g * 8 + 8, :]).then_inc(s_out, 16)
            sp.wait_ge(s_out, 64)

        @block.gpsimd
        def _(pool):
            g = nc.gpsimd
            st = Steps(pool, s_pool)
            st.did(g.memset(ident[:, :], 0.0))
            st.did(g.memset(flip[:, :], 0.0))
            st.did(g.memset(below[:, :], 1.0))
            st.did(g.memset(headm[:, :], 1.0))
            st.did(g.memset(selh[:, :, :], 0.0))
            st.did(g.memset(blockm[:, :], 0.0))
            st.did(g.iota(widx[:, 0:E0], pattern=[[1, E0]], base=-E0, channel_multiplier=0))
            st.did(g.iota(ejm[:, 0:NSLOT // TS].bitcast(i32), pattern=[[1, NSLOT // TS]], base=0, channel_multiplier=0))
            st.did(g.iota(sloti[0][:, 0:1], pattern=[[1, 1]], base=0, channel_multiplier=1))
            g.memset(ones[:, :], 1.0).then_inc(s_c, 1)
            g.memset(zero, 0.0).then_inc(s_zero, 1)
            st.sync()
            g.affine_select(out=ident[:, :], in_=ident[:, :], compare_op=ALU.not_equal, fill=1.0, base=0,
                            pattern=[[-1, P]], channel_multiplier=1).then_inc(s_c, 1)
            g.affine_select(out=flip[:, :], in_=flip[:, :], compare_op=ALU.not_equal, fill=1.0, base=-(P - 1),
                            pattern=[[1, P]], channel_multiplier=1).then_inc(s_c, 1)
            g.affine_select(out=below[:, :], in_=below[:, :], compare_op=ALU.is_gt, fill=0.0, base=0,
                            pattern=[[1, P]], channel_multiplier=-1).then_inc(s_c, 1)
            g.affine_select(out=selh[:, :, :], in_=selh[:, :, :], compare_op=ALU.not_equal, fill=1.0, base=0,
                            pattern=[[-1, H0], [0, P]], channel_multiplier=1).then_inc(s_c, 1)
            g.tensor_copy(eidx[:, :], widx[:, 0:E0]).then_inc(s_c, 1)
            g.tensor_copy(jidx[:, :], ejm[:, 0:NSLOT // TS].bitcast(i32)).then_inc(s_c, 1)
            g.tensor_copy(pidx[:, :], sloti[0][:, 0:1]).then_inc(s_c, 1)
            bmv = blockm[:, :].rearrange("p (h d) -> p h d", h=H1)
            st.did(g.affine_select(out=headm[:, :], in_=headm[:, :], compare_op=ALU.is_ge, fill=0.0, base=0,
                                   pattern=[[-DK, H0]], channel_multiplier=1))
            st.did(g.affine_select(out=bmv, in_=bmv, compare_op=ALU.is_ge, fill=OFF, base=0,
                                   pattern=[[-DH1, H1], [0, DH1]], channel_multiplier=1))
            st.sync()
            g.affine_select(out=headm[:, :], in_=headm[:, :], compare_op=ALU.is_ge, fill=0.0, base=DK - 1,
                            pattern=[[DK, H0]], channel_multiplier=-1).then_inc(s_c, 1)
            g.affine_select(out=bmv, in_=bmv, compare_op=ALU.is_ge, fill=OFF, base=DH1 - 1,
                            pattern=[[DH1, H1], [0, DH1]], channel_multiplier=-1).then_inc(s_c, 1)
            pool.wait_ge(s_c, 10)
            g.tensor_copy(identb[:, :], ident[:, :]).then_inc(s_c, 1)
            pool.wait_ge(s_strip, 16)
            g.tensor_copy(biasA[:, :, :], bass.AP(tensor=strip.tensor, offset=strip.offset + BW - 1,
                                                  ap=[list(strip.ap)[0], [BW, H0], [-1, BW]])).then_inc(s_ba, 1)

            def save(l):
                m = pre[l]
                with pool.Fori(0, NB // 2) as it:
                    for u in range(2):
                        b = it * 2 + u
                        pool.wait_ge(m["xs"], b + 1)
                        g.tensor_copy(xn_sb[l][:, bass.ds(b * 2, 2), :], xs[u][:, :, :]).then_inc(m["xs_saved"], 1)
                        if l == 0:
                            pool.wait_ge(m["xT"], b + 3)
                            g.tensor_copy(xnT[:, bass.ds(b * S, S)], xT[u][:, :]).then_inc(m["xT_saved"], 1)

            def route_and_scatter(l):
                pool.wait_ge(rou[l]["routed"], 1)
                if l == 0:
                    pool.wait_ge(s_xgz, 16 * (NSLOT * D // (P * 1024)))
                pool.wait_ge(pre[l]["xs_saved"], NB)
                for t in range(T):
                    for k in range(TOPK):
                        g.indirect_dma_start(
                            out=xg_dram, out_offset=bass.IndirectOffsetOnAxis(ap=sloti[k][:, t:t + 1].bitcast(u32), axis=0),
                            in_=xn_sb[l][:, t, :], in_offset=None).then_inc(rou[l]["scattered"], 16)

            def weights(l, nj, wcat):
                m = moe[l]
                with pool.Fori(0, nj // 2) as it:
                    for u in range(2):
                        j = it * 2 + u
                        pool.wait_ge(m["y"], j + 1)
                        g.tensor_copy(widx_cur[u][:, :], widx[:, bass.ds(j, 1)]).then_inc(m["widx"], 1)
                        pool.wait_ge(rou[l]["routed"], 1)
                        pool.wait_ge(m["widx"], j + 1)
                        g.indirect_dma_start(
                            out=wb[u], out_offset=None, in_=wcat,
                            in_offset=bass.IndirectOffsetOnAxis(ap=widx_cur[u][:, 0:1].bitcast(u32), axis=0)
                        ).then_inc(m[f"W{u}"], 16)

            def collect(l, nj):
                m = moe[l]
                for u in range(2):
                    pool.wait_ge(m[f"st{u}"], 16 * (nj // 2 + 1))
                for t in range(T):
                    for k in range(TOPK):
                        g.indirect_dma_start(
                            out=yy[:, k, t, :], out_offset=None, in_=yg_dram[l],
                            in_offset=bass.IndirectOffsetOnAxis(ap=sloti[k][:, t:t + 1].bitcast(u32), axis=0)
                        ).then_inc(com[l][f"g{t // 8}"], 16)

            pool.wait_ge(s_ba, 1)
            save(0)
            route_and_scatter(0)
            pool.wait_ge(pre[0]["sh"], 2 + NB)
            g.tensor_scalar(sh_sb[:, :, :], sh_sb[:, :, :], 0.5, None, ALU.mult).then_inc(com[0]["silu"], 1)
            pool.wait_ge(A0["s"], NB + 3)
            weights(0, NJ0, wcat0)
            collect(0, NJ0)
            save(1)
            route_and_scatter(1)
            pool.wait_ge(A1["s"], NB + 1)
            weights(1, NJ1, wcat1)
            collect(1, NJ1)

        @block.tensor
        def _(pe):
            mm, tr = nc.tensor.matmul, nc.tensor.transpose
            pe.wait_ge(s_c, 11)
            pe.wait_ge(s_w, 16 * NW)

            def pre_pe(l):
                m = pre[l]
                with pe.Fori(0, NB // 2) as it:
                    for u in range(2):
                        b = it * 2 + u
                        pe.wait_ge(m["xs"], b + 1)
                        pe.wait_ge(m["xT"], b + 1)
                        tr(bank[u][:, 0:P], xs[u][:, 0, :], ident[:, :])
                        tr(bank[u][:, P:2 * P], xs[u][:, 1, :], ident[:, :]).then_inc(m["T"], 1)
                        pe.wait_ge(m["xT"], b + 3)
                        if l == 0:
                            pe.wait_ge(m["lg"], b + 1)
                            pe.wait_ge(m["sh"], b + 1)
                            for j in range(2):
                                mm(bank[2 + u][:, j * E0:(j + 1) * E0], xT[u][:, j * P:(j + 1) * P], gate_sb[:, :],
                                   start=True, stop=True)
                                o = bank[4 + u][:, j * D:(j + 1) * D]
                                mm(o, xT[u][:, j * P:(j + 1) * P], shw_sb[:, :], start=True, stop=False)
                                last = mm(o, ones[0:1, :], shb_sb[:, :], start=False, stop=True)
                            last.then_inc(m["gs"], 1)
                        else:
                            pe.wait_ge(m["rhs"], b + 1)
                            for c in range(2):
                                last = mm(bank[4 + u][:, c * S:(c + 1) * S], rw1_sb[:, c * P:(c + 1) * P], xT[u][:, :],
                                          start=True, stop=True)
                            last.then_inc(m["rh1"], 1)
                            pe.wait_ge(m["rhs"], b + 3)
                            pe.wait_ge(m["lg"], b + 1)
                            for j in range(2):
                                for c in range(2):
                                    last = mm(bank[2 + u][:, j * E1:(j + 1) * E1], rh[u][:, c, j * P:(j + 1) * P],
                                              rw2_sb[:, c, :], start=(c == 0), stop=(c == 1))
                            last.then_inc(m["gs"], 1)

            def route_pe(l, ne):
                pe.wait_ge(rou[l]["A"], 1)
                pe.wait_ge(pre[l]["lg"], 2 + NB)
                mm(bank[0][:, 0:T * ne], below[:, :], rt[3][:, 0:T * ne], start=True, stop=True)
                mm(bank[1][:, 0:T * ne], ones[:, :], rt[3][:, 0:T * ne], start=True, stop=True).then_inc(rou[l]["cum"], 1)

            pe.wait_ge(s_strip, 16)
            with pe.Fori(0, H0 // 2) as it:
                for u in range(2):
                    pe.wait_ge(s_fle, it * 2 + u + 1)
                    mm(bank[6 + u][:, 0:BW], flip[:, :], strip[:, bass.ds(it * 2 + u, 1), :].rearrange("p o u -> p (o u)"),
                       start=True, stop=True).then_inc(s_fl, 1)
            pre_pe(0)
            route_pe(0, E0)

            a = A0
            PA, PB, PO, PQ, PV = bank[0:2], bank[2:4], bank[4:6], bank[6], bank[7]
            PVh = PV[:, :].bitcast(bf16)

            def project(n, u):
                pe.wait_ge(a["xTs"], n + 1)
                pe.wait_ge(a["qk_sb"], n + 1)
                pe.wait_ge(a["onT"], n + 1)
                mm(PQ[:, 0:S], wqk_sb[:, 0:D], xT[u][:, :], start=True, stop=True)
                mm(PQ[:, S:2 * S], wqk_sb[:, D:2 * D], xT[u][:, :], start=True, stop=True)
                pe.wait_ge(a["nmT"], n + 1)
                pe.wait_ge(a["s"], n + 1)
                for k in range(2):
                    last = mm(PV[:, k * D:(k + 1) * D], xT[u][:, k * P:(k + 1) * P], wv_sb[:, :], start=True, stop=True)
                last.then_inc(a["qkv"], 1)

            def max_scores(n, i):
                hp, qt = i // 2, i % 2
                o = PA[i % 2]
                pe.wait_ge(a["km"], n * 8 + hp + 1)
                pe.wait_ge(a["Ared"], n * 16 + i + 1)
                if i < 2:
                    pe.wait_ge(a["on"], n * 2 + 2)
                mm(o[:, :], qb[:, qt * P:(qt + 1) * P], km[:, 2 * hp:2 * hp + 2, :], start=True, stop=False)
                v = P * (1 - qt)
                mm(o[:, :], identb[:, :], biasA[:, 2 * hp:2 * hp + 2, v:v + S], start=False, stop=True).then_inc(a["A"], 1)

            def transpose_maxima(n):
                pe.wait_ge(a["Ared"], n * 16 + 18)
                pe.wait_ge(a["v_sb"], n + 2)
                pe.wait_ge(a["s"], n + 2)
                for q in range(2):
                    last = tr(PVh[0:H0, q * P:(q + 1) * P], nmax[:, q, :], identb[:, :])
                last.then_inc(a["mT"], 1)

            def exp_scores(b, u, h):
                o = PB[h % 2]
                pe.wait_ge(a["S"], b * 16 + h + 1)
                pe.wait_ge(a["qm"], b * 16 + h + 1)
                if h == 0:
                    pe.wait_ge(a["nmT"], b + 2)
                for j in range(2):
                    k = 1 - j
                    mm(o[:, j * S:(j + 1) * S], ks[u][:, k * P:(k + 1) * P], qm[:, h, :], start=True, stop=False)
                    last = mm(o[:, j * S:(j + 1) * S], selh[:, h, :], nmaxT[:, :], start=False, stop=True)
                last.then_inc(a["B"], 1)

            def weigh_values(b, u, h):
                gr, i = h // 4, h % 4
                pe.wait_ge(a["E"], b * 16 + h + 3)
                if h == 0:
                    pe.wait_ge(a["v_sb"], b + 2)
                if i == 0:
                    pe.wait_ge(a["oTs"], b * 4 + gr + 1)
                for j in range(2):
                    last = mm(PO[gr % 2][32 * i:32 * i + 32, 0:S], vaug[u][:, 1 - j, h, :], probs[h % 2][:, j * S:(j + 1) * S],
                              start=(j == 0), stop=(j == 1))
                last.then_inc(a["PV"], 1)

            def tail(b, maxima_ahead, projected):
                pe.wait_ge(a["oTs"], b * 4 + 6)
                pe.wait_ge(a["on"], b * 2 + 4)
                pe.wait_ge(a["Ared"], (b + 1 + maxima_ahead) * 16 + 2)
                for q in range(2):
                    for gr in range(4):
                        last = tr(PA[q][:, gr * P:(gr + 1) * P], oT[:, gr, q * P:(q + 1) * P], ident[:, :])
                    last.then_inc(a["To"], 1)
                pe.wait_ge(a["on"], b * 2 + 6)
                pe.wait_ge(a["qk_sb"], b + 2 + projected)
                pe.wait_ge(a["onT"], b + 3)
                for q in range(2):
                    last = tr(PQ[:, q * P:(q + 1) * P], on[:, q, :], ident[:, :])
                last.then_inc(a["Tn"], 1)
                pe.wait_ge(a["onT"], b + 4)
                pe.wait_ge(a["v_sb"], b + 2 + projected)
                pe.wait_ge(a["s"], b + 3)
                pe.wait_ge(a["nmT"], b + 2 + maxima_ahead)
                for q in range(2):
                    last = mm(PV[:, q * D:(q + 1) * D], onT[:, q * P:(q + 1) * P], wo_sb[:, :], start=True, stop=True)
                last.then_inc(a["wo"], 1)

            def attend(b, u, ahead, project_ahead):
                for h in range(H0):
                    exp_scores(b, u, h)
                    if ahead:
                        max_scores(b + 1, h)
                    if h:
                        weigh_values(b, u, h - 1)
                weigh_values(b, u, H0 - 1)
                if ahead:
                    transpose_maxima(b + 1)
                if project_ahead:
                    project(b + 2, u)
                tail(b, int(ahead), 2 * project_ahead if project_ahead else int(ahead))

            pe.wait_ge(s_ba, 1)
            project(0, 0)
            for i in range(H0):
                max_scores(0, i)
            transpose_maxima(0)
            project(1, 1)
            with pe.Fori(0, NB // 2 - 1) as it:
                for u in range(2):
                    attend(it * 2 + u, u, True, True)
            attend(NB - 2, 0, True, False)
            attend(NB - 1, 1, False, False)

            def experts(l, nj):
                m = moe[l]
                XT, HP, YP = bank[0:2], (bank[2:4], bank[4:6]), bank[6:8]

                def transposes(j, u, half):
                    pe.wait_ge(m[f"xg{u}"], half * 16 + 16)
                    pe.wait_ge(m["xT"], j + 1)
                    tr(XT[u][:, 0:P], xg[u][:, 0, :], ident[:, :])
                    tr(XT[u][:, P:2 * P], xg[u][:, 1, :], ident[:, :]).then_inc(m["T"], 1)

                def up(j, u, half):
                    pe.wait_ge(m[f"W{u}"], half * 16 + 16)
                    pe.wait_ge(m["xT"], j + 3)
                    pe.wait_ge(m["gelu"], j * 4 + 4)
                    for c in range(HC):
                        last = mm(HP[u][c // 2][:, (c % 2) * TS:(c % 2 + 1) * TS], wb[u][:, c * P:(c + 1) * P], xT[u][:, :],
                                  start=True, stop=True)
                        if c % 2:
                            last.then_inc(m["up"], 1)

                def down(j, u):
                    pe.wait_ge(m["gelu"], j * 4 + 12)
                    pe.wait_ge(m["y"], j + 1)
                    for s_ in range(2):
                        for c in range(HC):
                            last = mm(YP[u][:, s_ * D:(s_ + 1) * D], hb[u][:, c, s_ * P:(s_ + 1) * P],
                                      wb[u][:, HID + c * D:HID + (c + 1) * D], start=(c == 0), stop=(c == HC - 1))
                    last.then_inc(m["down"], 1)

                transposes(0, 0, 0)
                up(0, 0, 0)
                transposes(1, 1, 0)
                with pe.Fori(0, nj // 2 - 1) as it:
                    for v in range(2):
                        j = it * 2 + (1 + v)
                        up(j, 1 - v, it + v)
                        transposes(j + 1, v, it + 1)
                        down(j - 1, v)
                up(nj - 1, 1, nj // 2 - 1)
                down(nj - 2, 0)
                down(nj - 1, 1)

            experts(0, NJ0)
            pre_pe(1)
            route_pe(1, E1)

            a = A1
            pe.wait_ge(s_wf, 1)
            with pe.Fori(0, NB // 2) as it:
                for u in range(2):
                    b = it * 2 + u
                    pe.wait_ge(a["x2"], b + 1)
                    pe.wait_ge(a["Cs"], b + 1)
                    for j in range(2):
                        last = mm(bank[u][:, 0:D], x2[u][:, j, :], x2[u][:, j, :], start=(j == 0), stop=(j == 1))
                    last.then_inc(a["C"], 1)
                    pe.wait_ge(a["Cs"], b + 3)
                    pe.wait_ge(a["pr"], b + 1)
                    mm(bank[2 + u][:, 0:2 * D], cc[u], wqk1_sb[:, :], start=True, stop=True).then_inc(a["U"], 1)
                    pe.wait_ge(a["pr"], b + 3)
                    pe.wait_ge(a["nns"], b + 1)
                    for k in range(2):
                        last = mm(bank[4 + u][:, k:k + 1], pr[u][:, k * D:(k + 1) * D], ones[:, 0:1], start=True, stop=True)
                    last.then_inc(a["nn"], 1)
            pe.wait_ge(a["nns"], NB + 2)
            with pe.Fori(0, NB // 2) as it:
                for u in range(2):
                    b = it * 2 + u
                    pe.wait_ge(a["x2b"], b + 1)
                    pe.wait_ge(a["x2T"], b + 1)
                    tr(bank[u][:, 0:P], x2[u][:, 0, :], ident[:, :])
                    tr(bank[u][:, P:2 * P], x2[u][:, 1, :], ident[:, :]).then_inc(a["T"], 1)
                    pe.wait_ge(a["gk"], b + 1)
                    mm(bank[2 + u][:, 0:D], wqk1_sb[:, D:2 * D], uu[:, bass.ds(b, 1), 0:D].rearrange("p o d -> p (o d)"),
                       start=True, stop=True).then_inc(a["G"], 1)
                    pe.wait_ge(a["gk"], b + 3)
                    pe.wait_ge(a["gm"], b + 1)
                    tr(bank[4 + u][:, 0:P], gk[u], ident[:, :]).then_inc(a["GT"], 1)
                    pe.wait_ge(a["an"], b + 1)
                    pe.wait_ge(a["Ms"], b + 1)
                    pe.wait_ge(a["Ps"], b + 1)
                    mm(bank[6][:, 0:D], an[u], wo1_sb[:, :], start=True, stop=True).then_inc(a["M"], 1)
                    pe.wait_ge(a["Ms"], b + 2)
                    mm(bank[6][:, 0:D], wv1_sb[:, :], ms[u], start=True, stop=True).then_inc(a["Pm"], 1)
                    pe.wait_ge(a["Ps"], b + 2)
                    pe.wait_ge(a["x2T"], b + 3)
                    pe.wait_ge(a["s"], b + 1)
                    for j in range(2):
                        last = mm(bank[7][:, j * D:(j + 1) * D], x2T[u][:, j * P:(j + 1) * P], ps_[u], start=True, stop=True)
                    last.then_inc(a["F"], 1)
            experts(1, NJ1)

        @block.scalar
        def _(act):
            A = nc.scalar.activation
            for m in pre:
                act.sem_inc(m["xT"], 2)
                act.sem_inc(m["sh"], 2)
                act.sem_inc(m["rhs"], 2)
            act.sem_inc(s_fle, 2)
            for n, c in (("qk_sb", 1), ("v_sb", 1), ("nmT", 1), ("onT", 3), ("E", 2), ("oTs", 2)):
                act.sem_inc(A0[n], c)
            for m in moe:
                act.sem_inc(m["gelu"], 8)
            for n, c in (("Cs", 2), ("x2T", 2), ("Ms", 1), ("Ps", 1)):
                act.sem_inc(A1[n], c)
            act.wait_ge(s_w, 16 * NW)
            A(et_c, temp_c, ACT.Exp).then_inc(s_act, 1)
            with act.Fori(0, H0 // 2) as it:
                for u in range(2):
                    act.wait_ge(s_fl, it * 2 + u + 1)
                    A(biasT[:, bass.ds(it * 2 + u, 1), :].rearrange("p o u -> p (o u)"), bank[6 + u][:, 0:BW], ACT.Copy
                      ).then_inc(s_fle, 1)

            def pre_act(l):
                m = pre[l]
                with act.Fori(0, NB // 2) as it:
                    for u in range(2):
                        b = it * 2 + u
                        act.wait_ge(m["T"], b + 1)
                        if l == 0:
                            act.wait_ge(m["xT_saved"], b + 1)
                            act.wait_ge(m["gs"], b + 1)
                        else:
                            act.wait_ge(m["rh1"], b + 1)
                        A(xT[u][:, :], bank[u][:, 0:2 * P], ACT.Copy).then_inc(m["xT"], 1)
                        if l == 0:
                            act.wait_ge(m["gs"], b + 3)
                            A(sh_sb[:, bass.ds(b * 2, 2), :], bank[4 + u][:, 0:2 * D].rearrange("p (j d) -> p j d", j=2),
                              ACT.Gelu).then_inc(m["sh"], 1)
                        else:
                            act.wait_ge(m["rh1"], b + 3)
                            act.wait_ge(m["gs"], b + 1)
                            A(rh[u][:, 0, :], bank[4 + u][:, 0:S], ACT.Gelu, bias=rb1_sb[:, 0:1])
                            A(rh[u][:, 1, :], bank[4 + u][:, S:2 * S], ACT.Gelu, bias=rb1_sb[:, 1:2]).then_inc(m["rhs"], 1)

            def route_act(l, ne):
                act.wait_ge(rou[l]["lgx"], 1)
                A(rt[0][:, 0:T * ne], rt[0][:, 0:T * ne], ACT.Exp).then_inc(rou[l]["exped"], 1)

            pre_act(0)
            route_act(0, E0)

            a = A0
            PQ, PV, PO = bank[6], bank[7], bank[4:6]

            def evacuate(n, u):
                act.wait_ge(a["qkv"], n + 3)
                act.wait_ge(a["qb"], n + 1)
                act.wait_ge(a["B"], n * 16 + 16)
                A(qs[u], PQ[:, 0:S], ACT.Identity, scale=QSCALE, bias=bqs_c)
                A(ks[u], PQ[:, S:2 * S], ACT.Identity, bias=bk_c).then_inc(a["qk_sb"], 1)
                act.wait_ge(a["PV"], n * 16 + 16)
                A(vaug[u][:, :, :, 0:DK], PV[:, 0:2 * D].rearrange("p (k h d) -> p k h d", k=2, h=H0), ACT.Copy
                  ).then_inc(a["v_sb"], 1)

            def mask_query(n, u, h):
                A(qm[:, h, :], qs[u], ACT.Copy, scale=headm[:, h:h + 1]).then_inc(a["qm"], 1)

            def copy_maxima(n):
                act.wait_ge(a["mT"], n + 2)
                A(nmaxT[0:H0, :], PV[:, :].bitcast(bf16)[0:H0, 0:S], ACT.Copy).then_inc(a["nmT"], 1)

            def attend_act(b, u, ahead, project_ahead):
                for h in range(H0):
                    act.wait_ge(a["S"], b * 16 + h + 3)
                    act.wait_ge(a["PV"], b * 16 + h + 31)
                    A(probs[h % 2], scores[h % 2], ACT.Exp).then_inc(a["E"], 1)
                    if ahead and h:
                        act.wait_ge(a["B"], b * 16 + h + 32)
                        if h == 1:
                            act.wait_ge(a["qk_sb"], b + 3)
                        mask_query(b + 1, 1 - u, h - 1)
                    if h % 4 == 0 and h:
                        copy_group(b, h // 4 - 1)
                if ahead:
                    act.wait_ge(a["B"], b * 16 + 48)
                    mask_query(b + 1, 1 - u, H0 - 1)
                copy_group(b, 3)
                if ahead:
                    copy_maxima(b + 1)
                if project_ahead:
                    evacuate(b + 2, u)
                act.wait_ge(a["Tn"], b + 1)
                A(onT, PQ[:, 0:2 * P], ACT.Identity, bias=bv_c).then_inc(a["onT"], 1)

            def copy_group(b, gr):
                act.wait_ge(a["PV"], b * 16 + 4 * gr + 36)
                A(oT[:, gr, :], PO[gr % 2][:, 0:S], ACT.Copy).then_inc(a["oTs"], 1)

            act.wait_ge(s_wf, 1)
            act.wait_ge(s_c, 11)
            act.wait_ge(s_xgz, 16 * (NSLOT * D // (P * 1024)))
            evacuate(0, 0)
            act.wait_ge(a["qk_sb"], 2)
            for h in range(H0):
                mask_query(0, 0, h)
            copy_maxima(0)
            evacuate(1, 1)
            with act.Fori(0, NB // 2 - 1) as it:
                for u in range(2):
                    attend_act(it * 2 + u, u, True, True)
            attend_act(NB - 2, 0, True, False)
            attend_act(NB - 1, 1, False, False)

            def experts(l, nj):
                m = moe[l]
                with act.Fori(0, nj // 2) as it:
                    for u in range(2):
                        j = it * 2 + u
                        act.wait_ge(m[f"W{u}"], it * 16 + 16)
                        act.wait_ge(m["down"], j + 1)
                        for c in range(HC):
                            if c % 2 == 0:
                                act.wait_ge(m["up"], j * 2 + (5 + c // 2))
                            bc = HID + HC * D + c
                            A(hb[u][:, c, :], bank[2 + 2 * u + c // 2][:, (c % 2) * TS:(c % 2 + 1) * TS], ACT.Gelu,
                              bias=wb[u][:, bc:bc + 1]).then_inc(m["gelu"], 1)

            def silus(l):
                for q in range(4):
                    act.wait_ge(com[l]["z"], q + 1)
                    A(yy[:, 0, q * 8:q * 8 + 8, :], yy[:, 0, q * 8:q * 8 + 8, :], ACT.Silu).then_inc(com[l]["silu"], 1)

            experts(0, NJ0)
            silus(0)
            pre_act(1)
            route_act(1, E1)

            a = A1
            with act.Fori(0, NB // 2) as it:
                for u in range(2):
                    b = it * 2 + u
                    act.wait_ge(a["C"], b + 1)
                    act.wait_ge(a["U"], b + 1)
                    A(cc[u], bank[u][:, 0:D], ACT.Copy).then_inc(a["Cs"], 1)
            with act.Fori(0, NB // 2) as it:
                for u in range(2):
                    b = it * 2 + u
                    act.wait_ge(a["T"], b + 1)
                    act.wait_ge(a["F"], b + 1)
                    A(x2T[u], bank[u][:, 0:2 * P], ACT.Copy).then_inc(a["x2T"], 1)
                    act.wait_ge(a["mx"], b + 1)
                    A(at1[u], gm[u], ACT.Exp, bias=nm1[u], accum_out=sm1[u]).then_inc(a["exp"], 1)
                    act.wait_ge(a["M"], b + 1)
                    A(ms[u], bank[6][:, 0:D], ACT.Copy).then_inc(a["Ms"], 1)
                    act.wait_ge(a["Pm"], b + 1)
                    A(ps_[u], bank[6][:, 0:D], ACT.Copy, scale=nw_c).then_inc(a["Ps"], 1)
            experts(1, NJ1)
            silus(1)

        @block.vector
        def _(dve):
            V = nc.vector
            st = Steps(dve, s_dve)
            for m in pre:
                dve.sem_inc(m["lg"], 2)
                dve.sem_inc(m["xT_saved"], 2)
                dve.sem_inc(m["gs"], 2)
                dve.sem_inc(m["rh1"], 2)
            for n, c in (("on", 4), ("s", 3), ("Ared", 2), ("S", 2), ("qb", 2), ("qkv", 2), ("B", 32), ("PV", 32),
                         ("A", 16), ("mT", 1)):
                dve.sem_inc(A0[n], c)
            for m in moe:
                for n, c in (("xT", 2), ("y", 2), ("T", 2), ("up", 4), ("down", 2), ("st0", 16), ("st1", 16)):
                    dve.sem_inc(m[n], c)
            for n, c in (("pr", 2), ("nns", 2), ("gk", 2), ("gm", 2), ("s", 1), ("U", 2), ("F", 2)):
                dve.sem_inc(A1[n], c)

            def rsqrt(y, v, t1, t2, shape_i=None):
                yi, vi = y.bitcast(i32), v.bitcast(i32)
                st.link(V.tensor_scalar(t1.bitcast(i32), vi, 1, None, ALU.logical_shift_right))
                st.link(V.tensor_scalar(yi, t1.bitcast(i32), -1.0, float(0x5f3759df), ALU.mult, ALU.add))
                for _ in range(4):
                    st.link(V.tensor_tensor(t2, y, y, ALU.mult))
                    st.link(V.tensor_tensor(t1, t2, v, ALU.mult))
                    st.link(V.tensor_scalar(t1, t1, -0.5, 1.5, ALU.mult, ALU.add))
                    st.link(V.tensor_tensor(y, y, t1, ALU.mult))

            def take_stats(src):
                with dve.Fori(0, T // 8) as it:
                    for k in range(8):
                        t = it * 8 + k
                        V.bn_stats(stats[:, bass.ds(t, 1), :], src(t)).then_inc(s_dve, 1)
                st.base += T
                st.sync()

            def finish_stats():
                m0, v0, m1, v1 = (stats[:, :, i] for i in (1, 2, 4, 5))
                st.did(V.tensor_tensor(tmpa[:, :], m0, m1, ALU.add))
                st.did(V.tensor_tensor(tmpb[:, :], m0, m1, ALU.subtract))
                st.link(V.tensor_tensor(var[:, :], v0, v1, ALU.add))
                st.did(V.tensor_scalar(mean[:, :], tmpa[:, :], 0.5, None, ALU.mult))
                st.link(V.tensor_tensor(tmpb[:, :], tmpb[:, :], tmpb[:, :], ALU.mult))
                st.did(V.tensor_scalar(var[:, :], var[:, :], 1.0 / D, None, ALU.mult))
                st.link(V.tensor_scalar(tmpb[:, :], tmpb[:, :], 0.25, None, ALU.mult))
                st.link(V.tensor_tensor(var[:, :], var[:, :], tmpb[:, :], ALU.add))
                st.link(V.tensor_scalar(tmpb[:, :], var[:, :], LN_EPS, None, ALU.add))
                rsqrt(rstd[:, :], tmpb[:, :], tmpa[:, :], rrms[:, :])

            def pre_dve(l, ne):
                m = pre[l]
                src = (x_sb, xres)[l]

                def normalise(b, u, wait):
                    if wait:
                        dve.wait_ge(m["T"], b - 1)
                        dve.wait_ge(m["xs_saved"], b - 1)
                    for j in range(2):
                        t = b * 2 + j
                        last = V.tensor_scalar(xs[u][:, j, :], src[:, bass.ds(t, 1), :].rearrange("p o d -> p (o d)"),
                                               mean[:, bass.ds(t, 1)], rstd[:, bass.ds(t, 1)], ALU.subtract, ALU.mult)
                    last.then_inc(m["xs"], 1)

                def logits(b, u):
                    dve.wait_ge(m["gs"], b + 3)
                    bk = bank[2 + u][:, 0:2 * ne].rearrange("p (j e) -> p j e", j=2)
                    dst = lg[:, bass.ds(b * 2, 2), 0:ne]
                    if l == 0:
                        V.tensor_copy(dst, bk).then_inc(m["lg"], 1)
                    else:
                        V.tensor_tensor(dst, bk, mid(rb2_bc[:, :], 2), ALU.add).then_inc(m["lg"], 1)

                normalise(0, 0, False)
                normalise(1, 1, False)
                with dve.Fori(0, NB // 2 - 1) as it:
                    for u in range(2):
                        b = it * 2 + u
                        normalise(b + 2, u, True)
                        logits(b, u)
                logits(NB - 2, 0)
                logits(NB - 1, 1)

            def route(l, ne, nj, wcat_rows=P):
                r = rou[l]
                n = T * ne
                v3 = lambda t: t[:, 0:n].rearrange("p (t e) -> p t e", e=ne)
                logit = lg[:, :, 0:ne]
                e0, e1, e2, e3 = (v3(x_) for x_ in rt)
                hots = [v3(h) for h in hot]
                dve.wait_ge(pre[l]["lg"], NB + 2)
                st.link(V.reduce_max(tmpa[:, :], logit, AX.X))
                V.tensor_tensor(e0, logit, over(tmpa[:, :], ne), ALU.subtract).then_inc(r["lgx"], 1)
                dve.wait_ge(r["exped"], 1)
                st.link(V.reduce_sum(tmpb[:, :], e0, AX.X))
                st.link(V.reciprocal(tmpb[:, :], tmpb[:, :]))
                st.link(V.tensor_tensor(e0, e0, over(tmpb[:, :], ne), ALU.mult))
                eb = mid(eidx[:, E0 - ne:E0], T)
                for k in range(TOPK):
                    src = logit if k == 0 else e1
                    if k:
                        st.link(V.scalar_tensor_tensor(e1.rearrange("p t e -> p (t e)"), hot[0][:, 0:n], OFF,
                                                       rt[3][:, 0:n], ALU.mult, ALU.add))
                        st.link(V.reduce_max(tmpa[:, :], e1, AX.X))
                    else:
                        st.did(V.tensor_copy(e3, logit))
                    st.link(V.tensor_tensor(e2, src, over(tmpa[:, :], ne), ALU.is_equal))
                    st.link(V.tensor_tensor(e2, e2, eb, ALU.mult))
                    st.link(V.tensor_reduce(tmpb[:, :], e2, AX.X, ALU.min))
                    st.link(V.tensor_tensor(hots[k], eb, over(tmpb[:, :], ne), ALU.is_equal))
                    st.link(V.tensor_tensor(e2, e0, hots[k], ALU.mult))
                    st.link(V.reduce_sum(pk[k][:, :], e2, AX.X))
                V.tensor_tensor(rt[3][:, 0:n], hot[0][:, 0:n], hot[1][:, 0:n], ALU.add).then_inc(r["A"], 1)
                if l == 0:
                    st.link(V.tensor_tensor(tmpa[:, :], pk[0][:, :], pk[1][:, :], ALU.add))
                    st.link(V.reciprocal(tmpa[:, :], tmpa[:, :]))
                    for k in range(TOPK):
                        st.did(V.tensor_tensor(wk[k][:, :], pk[k][:, :], tmpa[:, :], ALU.mult))
                else:
                    for k in range(TOPK):
                        st.did(V.tensor_copy(wk[k][:, :], pk[k][:, :]))
                dve.wait_ge(r["cum"], 1)
                et_ = lambda t: t[:, 0:n].rearrange("p (e t) -> p e t", t=T)
                st.link(V.tensor_copy(et_(rt[1]), bank[1][:, 0:n].rearrange("p (t e) -> p e t", e=ne)))
                st.link(V.memset(rt[2][:, 0:n], 1.0))
                st.link(V.tensor_tensor_scan(rt[0][:, 0:n], rt[2][:, 0:n], rt[1][:, 0:n], 0.0, ALU.mult, ALU.add))
                st.link(V.tensor_tensor(rt[1][:, 0:n], rt[0][:, 0:n], rt[1][:, 0:n], ALU.subtract))
                first = et_(rt[1])[:, :, 0]
                cnt, tend, tmp, off = (e[:, 0:ne] for e in ecnt)
                st.link(V.tensor_tensor(cnt, et_(rt[0])[:, :, T - 1], first, ALU.subtract))
                st.link(V.tensor_scalar(ecnti[:, 0:ne], cnt, float(TS - 1), None, ALU.add))
                st.link(V.tensor_scalar(ecnti[:, 0:ne], ecnti[:, 0:ne], TS.bit_length() - 1, None, ALU.logical_shift_right))
                st.link(V.tensor_copy(cnt, ecnti[:, 0:ne]))
                st.link(V.tensor_tensor_scan(tend, rt[2][:, 0:ne], cnt, 0.0, ALU.mult, ALU.add))
                st.link(V.tensor_tensor(tmp, tend, cnt, ALU.subtract))
                st.link(V.scalar_tensor_tensor(off, tmp, float(TS), first, ALU.mult, ALU.subtract))
                st.link(V.tensor_tensor(e2, v3(bank[0]), et_(rt[1]).rearrange("p e t -> p t e"), ALU.add))
                st.link(V.tensor_tensor(e2, e2, mid(off, T), ALU.add))
                for k in range(TOPK):
                    st.link(V.tensor_tensor(e0, e2, hots[k], ALU.mult))
                    st.link(V.reduce_sum(slotf[k][:, :], e0, AX.X))
                    st.did(V.tensor_copy(sloti[k][:, :], slotf[k][:, :]))
                ej = ejm[:, 0:nj * ne].rearrange("p (j e) -> p j e", e=ne)
                st.link(V.tensor_tensor(ej, mid(tend, nj), over(jidx[:, 0:nj], ne), ALU.is_le))
                st.link(V.reduce_sum(ejf[:, 0:nj], ej, AX.X))
                st.link(V.tensor_scalar(ejf[:, 0:nj], ejf[:, 0:nj], float(ne - 1), float(P), ALU.min, ALU.mult))
                V.tensor_scalar(widx[:, 0:nj], ejf[:, 0:nj], pidx[:, :], None, ALU.add).then_inc(r["routed"], 1)

            dve.wait_ge(s_relb, 16)
            lo, hi = S - 1 - MAXREL, S + MAXREL
            V.tensor_copy(ext_sb[:, 0:lo], ext_sb[:, lo:lo + 1].broadcast_to([H0, lo])).then_inc(s_edge, 1)
            V.tensor_copy(ext_sb[:, hi:EXT], ext_sb[:, hi - 1:hi].broadcast_to([H0, EXT - hi])).then_inc(s_edge, 1)
            dve.wait_ge(s_x, 64)
            take_stats(lambda t: x_sb[:, bass.ds(t, 1), :].rearrange("p o d -> p (o d)"))
            finish_stats()
            pre_dve(0, E0)
            dve.wait_ge(s_c, 11)
            dve.wait_ge(s_w, 16 * NW)
            st.did(V.tensor_scalar(bqs_c, bq_c, QSCALE, None, ALU.mult))
            V.tensor_scalar(wqk1_sb[:, :], wqk1_sb[:, :], nw_c, None, ALU.mult).then_inc(s_wf, 1)
            route(0, E0, NJ0)

            a = A0
            dve.wait_ge(s_xgz, 16 * (NSLOT * D // (P * 1024)))
            dve.wait_ge(pre[0]["xT_saved"], NB + 2)
            for u in range(2):
                st.did(V.memset(vaug[u], 0.0))
            st.did(V.memset(nmaxT, 0.0))
            st.sync()
            for u in range(2):
                st.did(V.memset(vaug[u][:, :, :, DK:DK + 1], 1.0))
            st.sync()

            def fetch_rows(n, u):
                dve.wait_ge(a["qkv"], n + 1)
                V.tensor_copy(xT[u][:, :], xnT[:, n * S:(n + 1) * S] if isinstance(n, int) else xnT[:, bass.ds(n * S, S)]
                              ).then_inc(a["xTs"], 1)

            def mask_keys(u, hp):
                for h in (2 * hp, 2 * hp + 1):
                    last = V.tensor_scalar(km[:, h, :], ks[u], headm[:, h:h + 1], None, ALU.mult)
                last.then_inc(a["km"], 1)

            def start_keys(n, u):
                dve.wait_ge(a["qk_sb"], n + 2)
                dve.wait_ge(a["A"], n * 16 + 16)
                V.tensor_copy(qb, qs[u]).then_inc(a["qb"], 1)
                mask_keys(u, 0)

            def reduce_maxima(n, i):
                hp, qt = i // 2, i % 2
                dve.wait_ge(a["A"], n * 16 + i + 17)
                if i == 0:
                    dve.wait_ge(a["mT"], n + 1)
                V.tensor_reduce(nmax[:, qt, 2 * hp:2 * hp + 2], bank[i % 2][:, :].rearrange("p (h k) -> p h k", h=2),
                                AX.X, ALU.max, negate=True).then_inc(a["Ared"], 1)

            def add_bias(b, h):
                dve.wait_ge(a["B"], b * 16 + h + 33)
                dve.wait_ge(a["E"], b * 16 + h + 1)
                bt = biasT[:, h, 0:S]
                V.tensor_tensor(scores[h % 2].rearrange("p (j q) -> p j q", j=2),
                                bank[2 + h % 2][:, :].rearrange("p (j q) -> p j q", j=2),
                                bass.AP(tensor=bt.tensor, offset=bt.offset, ap=[list(bt.ap)[0], [P, 2], [1, S]]),
                                ALU.add).then_inc(a["S"], 1)

            def attend_dve(b, u, ahead, prepare_ahead):
                for h in range(H0):
                    if ahead:
                        if h % 2 == 0 and h // 2 + 1 < H0 // 2:
                            mask_keys(1 - u, h // 2 + 1)
                        reduce_maxima(b + 1, h)
                    add_bias(b, h)
                    if prepare_ahead and h == 4:
                        fetch_rows(b + 2, u)
                if prepare_ahead:
                    start_keys(b + 2, u)
                for q in range(2):
                    dve.wait_ge(a["To"], b * 2 + (q + 1))
                    o = bank[q][:, :].rearrange("p (h c) -> p h c", c=32)
                    V.reciprocal(rden[:, q, :], o[:, :, DK]).then_inc(a["s2"], 1)
                    dve.wait_ge(a["s2"], b * 2 + (q + 1))
                    V.tensor_tensor(on[:, q, :].rearrange("p (h d) -> p h d", d=DK), o[:, :, 0:DK],
                                    over(rden[:, q, :], DK), ALU.mult).then_inc(a["on"], 1)
                dve.wait_ge(a["wo"], b + 1)
                dst = s_sb[:, 2 * b:2 * b + 2, :] if isinstance(b, int) else s_sb[:, bass.ds(b * 2, 2), :]
                V.tensor_tensor(dst, bank[7][:, 0:2 * D].rearrange("p (q d) -> p q d", q=2), mid(bo_bc[:, :], 2),
                                ALU.add).then_inc(a["s"], 1)

            fetch_rows(0, 0)
            fetch_rows(1, 1)
            start_keys(0, 0)
            for i in range(H0):
                if i % 2 == 0 and i // 2 + 1 < H0 // 2:
                    mask_keys(0, i // 2 + 1)
                reduce_maxima(0, i)
            start_keys(1, 1)
            with dve.Fori(0, NB // 2 - 1) as it:
                for u in range(2):
                    attend_dve(it * 2 + u, u, True, True)
            attend_dve(NB - 2, 0, True, False)
            attend_dve(NB - 1, 1, False, False)

            def experts(l, nj):
                m = moe[l]

                def copy_rows(j, u):
                    dve.wait_ge(m["T"], j + 3)
                    dve.wait_ge(m["up"], j * 2 + 2)
                    V.tensor_copy(xT[u][:, :], bank[u][:, 0:2 * P]).then_inc(m["xT"], 1)

                def outputs(j, u, half):
                    dve.wait_ge(m["down"], j + 3)
                    dve.wait_ge(m[f"st{u}"], half * 16 + 16)
                    V.tensor_tensor(yb[u], bank[6 + u][:, 0:2 * D].rearrange("p (s d) -> p s d", s=2),
                                    mid(wb[u][:, WROW - D:WROW], 2), ALU.add).then_inc(m["y"], 1)

                copy_rows(0, 0)
                copy_rows(1, 1)
                with dve.Fori(0, nj // 2 - 1) as it:
                    for v in range(2):
                        copy_rows(it * 2 + (2 + v), v)
                        outputs(it * 2 + v, v, it)
                outputs(nj - 2, 0, nj // 2 - 1)
                outputs(nj - 1, 1, nj // 2 - 1)

            def combine(l):
                for t in range(T):
                    if t % 8 == 0:
                        dve.wait_ge(com[l][f"g{t // 8}"], 16 * 8 * TOPK)
                    y0, y1 = yy[:, 0, t, :], yy[:, 1, t, :]
                    if l == 0:
                        st.did(V.scalar_tensor_tensor(y0, y0, wk[0][:, t:t + 1], sh_sb[:, t, :], ALU.mult, ALU.add))
                    else:
                        st.did(V.tensor_scalar(y0, y0, wk[0][:, t:t + 1], None, ALU.mult))
                st.sync()
                for t in range(T):
                    y0, y1 = yy[:, 0, t, :], yy[:, 1, t, :]
                    ins = V.scalar_tensor_tensor(y0, y1, wk[1][:, t:t + 1], y0, ALU.mult, ALU.add)
                    if l == 1 and t % 8 == 7:
                        ins.then_inc(com[1]["z"], 1)
                    else:
                        st.did(ins)
                st.sync()

            experts(0, NJ0)
            dve.wait_ge(com[0]["silu"], 1)
            combine(0)
            take_stats(lambda t: yy[:, 0, bass.ds(t, 1), :].rearrange("p o d -> p (o d)"))
            finish_stats()
            for t in range(T):
                st.did(V.tensor_scalar(yy[:, 0, t, :], yy[:, 0, t, :], mean[:, t:t + 1], rstd[:, t:t + 1],
                                       ALU.subtract, ALU.mult))
            st.sync()
            for q in range(4):
                z = yy[:, 0, q * 8:q * 8 + 8, :]
                st.link(V.tensor_tensor(z, z, mid(gamma_bc[:, :], 8), ALU.mult))
                V.tensor_tensor(z, z, mid(beta_bc[:, :], 8), ALU.add).then_inc(com[0]["z"], 1)
            dve.wait_ge(s_x2, 16)
            for q in range(4):
                z, r_, s_ = (b_[:, q * 8:q * 8 + 8, :] for b_ in (yy[:, 0], xres, s_sb))
                dve.wait_ge(com[0]["silu"], q + 2)
                st.link(V.tensor_tensor(z, z, s_, ALU.mult))
                st.did(V.tensor_tensor(r_, r_, z, ALU.add))
            st.sync()
            take_stats(lambda t: xres[:, bass.ds(t, 1), :].rearrange("p o d -> p (o d)"))
            finish_stats()
            st.link(V.tensor_tensor(tmpa[:, :], rstd[:, :], rstd[:, :], ALU.mult))
            st.link(V.tensor_tensor(tmpa[:, :], tmpa[:, :], var[:, :], ALU.mult))
            st.link(V.tensor_scalar(var[:, :], tmpa[:, :], RMS_EPS, None, ALU.add))
            rsqrt(rrms[:, :], var[:, :], tmpa[:, :], tmpb[:, :])
            pre_dve(1, E1)
            route(1, E1, NJ1)

            a = A1
            xn1 = xn_sb[1]
            dve.wait_ge(pre[1]["xs_saved"], NB)
            dve.wait_ge(s_act, 1)

            def scale_rows(b, u, name):
                for j in range(2):
                    t = b * 2 + j
                    last = V.tensor_scalar(x2[u][:, j, :], xn1[:, bass.ds(t, 1), :].rearrange("p o d -> p (o d)"),
                                           rrms[:, bass.ds(t, 1)], None, ALU.mult)
                last.then_inc(a[name], 1)

            with dve.Fori(0, NB // 2) as it:
                for u in range(2):
                    b = it * 2 + u
                    scale_rows(b, u, "x2")
                    dve.wait_ge(a["U"], b + 3)
                    V.tensor_copy(uu[:, bass.ds(b, 1), :].rearrange("p o d -> p (o d)"), bank[2 + u][:, 0:D])
                    V.tensor_tensor(pr[u], bank[2 + u][:, 0:2 * D], wqk1_sb[:, :], ALU.mult).then_inc(a["pr"], 1)
                    dve.wait_ge(a["nn"], b + 1)
                    V.tensor_copy(nsq[:, bass.ds(b, 1), :].rearrange("p o k -> p (o k)"), bank[4 + u][:, 0:2]).then_inc(a["nns"], 1)
            dve.wait_ge(a["nns"], NB + 2)
            nf, rf = nsq.rearrange("p b k -> p (b k)"), rin.rearrange("p b k -> p (b k)")
            st.link(V.tensor_scalar(nf, nf, 1e-24, None, ALU.max))
            rsqrt(rf, nf, nt1, nt2)
            st.link(V.tensor_scalar(rin[:, :, 0], rin[:, :, 0], et_c, None, ALU.mult))
            with dve.Fori(0, NB // 2) as it:
                for u in range(2):
                    b = it * 2 + u
                    scale_rows(b, u, "x2b")
                    dve.wait_ge(a["G"], b + 1)
                    V.tensor_scalar(gk[u], bank[2 + u][:, 0:D], rin[:, bass.ds(b, 1), 1], None, ALU.mult).then_inc(a["gk"], 1)
                    dve.wait_ge(a["GT"], b + 1)
                    V.scalar_tensor_tensor(gm[u], bank[4 + u][:, 0:P], rin[:, bass.ds(b, 1), 0], blockm[:, :], ALU.mult,
                                           ALU.add).then_inc(a["gm"], 1)
                    dve.wait_ge(a["gm"], b + 3)
                    V.tensor_reduce(nm1[u], gm[u], AX.X, ALU.max, negate=True).then_inc(a["mx"], 1)
                    dve.wait_ge(a["exp"], b + 1)
                    V.reciprocal(rs1[u], sm1[u]).then_inc(a["rs"], 1)
                    dve.wait_ge(a["rs"], b + 1)
                    V.tensor_scalar(an[u], at1[u], rs1[u], None, ALU.mult).then_inc(a["an"], 1)
                    dve.wait_ge(a["F"], b + 3)
                    V.tensor_copy(s_sb[:, bass.ds(b * 2, 2), :], bank[7][:, 0:2 * D].rearrange("p (j d) -> p j d", j=2)
                                  ).then_inc(a["s"], 1)
            experts(1, NJ1)
            combine(1)
            for q in range(4):
                z, r_, s_ = (b_[:, q * 8:q * 8 + 8, :] for b_ in (yy[:, 0], xres, s_sb))
                dve.wait_ge(com[1]["silu"], q + 1)
                st.link(V.tensor_tensor(z, z, s_, ALU.mult))
                V.tensor_tensor(z, r_, z, ALU.add).then_inc(com[1]["x1"], 1)


def kernel(**inputs):
    import numpy as _np
    import concourse.bacc as _bacc
    from concourse import mybir as _mybir
    from concourse.bass_utils import run_bass_kernel_spmd as _run

    i = {k: _np.asarray(v) for k, v in inputs.items()}

    def column(v, chunks=1):
        return v.reshape(chunks, P).T

    def expert_rows(w1, b1, w2, b2):
        e = w1.shape[0]
        w2r = w2.reshape(e, HC, P, D).transpose(0, 2, 1, 3).reshape(e, P, HC * D)
        b1r = b1.reshape(e, HC, P).transpose(0, 2, 1)
        b2r = _np.repeat(b2[:, None, :], P, axis=1)
        return _np.concatenate([w1, w2r, b1r, b2r], axis=2).reshape(e * P, WROW)

    wqkv = i["L1_attn_w_qkv"]
    host = [
        ("x", i["L0_attn_x"].reshape(TOK, D)),
        ("wqT", i["L0_attn_Wq"].T), ("wkT", i["L0_attn_Wk"].T), ("wvT", i["L0_attn_Wv"].T), ("woT", i["L0_attn_Wo"].T),
        ("bq", column(i["L0_attn_bq"])), ("bk", column(i["L0_attn_bk"])), ("bv", column(i["L0_attn_bv"])),
        ("bo", i["L0_attn_bo"]), ("relb", i["L0_attn_rel_bias"]),
        ("wcat0", expert_rows(i["L0_ffn_W1"], i["L0_ffn_b1"], i["L0_ffn_W2"], i["L0_ffn_b2"])),
        ("gate", i["L0_ffn_gate_W"]), ("shw", i["L0_ffn_shared_W"]), ("shb", i["L0_ffn_shared_b"]),
        ("gamma", i["L0_ffn_gamma"]), ("beta", i["L0_ffn_beta"]),
        ("nw", column(i["L1_attn_norm_weight"])), ("wqkT1", wqkv[0:2 * D].T), ("wv1", wqkv[2 * D:]),
        ("woT1", i["L1_attn_w_out"].T), ("temp", _np.repeat(i["L1_attn_temperature"].reshape(H1), DH1)[:, None]),
        ("rw1", i["L1_ffn_rW1"]), ("rb1", column(i["L1_ffn_rb1"], 2)),
        ("rw2", i["L1_ffn_rW2"].reshape(2, P, E1).transpose(1, 0, 2)), ("rb2", i["L1_ffn_rb2"]),
        ("wcat1", expert_rows(i["L1_ffn_We1"], i["L1_ffn_be1"], i["L1_ffn_We2"], i["L1_ffn_be2"])),
    ]
    nc = _bacc.Bacc("TRN2", target_bir_lowering=False, num_devices=1)
    arrays, args = {}, []
    for name, a in host:
        a = _np.ascontiguousarray(a)
        arrays[f"in_{name}"] = a
        args.append(nc.dram_tensor(f"in_{name}", a.shape, _mybir.dt.from_np(a.dtype), kind="ExternalInput").ap())
    args.append(nc.dram_tensor("out_x", (TOK, D), _mybir.dt.float32, kind="ExternalOutput").ap())
    build(nc, *args)
    r = _run(nc, [arrays], core_ids=[0])
    return r.results[0]["out_x"].reshape(NB, S, D)
```

```python
import concourse.bass as bass
from concourse import mybir
from contextlib import ExitStack

NB, S, D = 16, 256, 128
P = 128
T = NB * S // P
H0, DK = 16, 8
MAXREL = 128
NREL = 2 * MAXREL + 1
E0, E1, HID = 8, 4, 512
HC = HID // P
H1, DH1 = 8, 16
TS = 256
TOPK = 2
NWB = 4
XW = D + 2
TOK = NB * S
EROWS = 4
NOWHERE = 1e6


def tiles_for(experts):
    n = (TOK * TOPK - experts) // TS + experts
    return -(-n // NWB) * NWB


NJ0, NJ1 = tiles_for(E0), tiles_for(E1)
NSLOT = max(NJ0, NJ1) * TS
WROW = HID + HC * D + HC + D
EXT = 2 * S - 1
QPIECE, KPIECE = (0, 0, 0, 1, 1, 2), (0, 1, 2, 0, 1, 0)
TERMS = len(QPIECE)
STK = TERMS * DK
HALF = P // 2
BW = S + P
LN_EPS, RMS_EPS = 1e-5, 1e-6
QSCALE = float(DK) ** -0.5
OFF = -1e30


class Steps:

    def __init__(self, eng, sem):
        self.eng, self.sem, self.base, self.k, self.it, self.per = eng, sem, 0, 0, None, 0

    def did(self, ins):
        self.k += 1
        return ins.then_inc(self.sem, 1)

    def sync(self):
        at = self.base + self.k
        self.eng.wait_ge(self.sem, at if self.it is None else self.it * self.per + at)

    def link(self, ins):
        self.did(ins)
        self.sync()

    def enter(self, it, per):
        self.base, self.k, self.it, self.per = self.base + self.k, 0, it, per

    def leave(self, turns):
        assert self.k == self.per, (self.k, self.per)
        self.base, self.k, self.it = self.base + turns * self.per, 0, None


def staged(eng, stages):
    head = 2 * -(-max(lag for _, lag in stages) // 2)

    def peeled(i):
        for stage, lag in stages:
            if 0 <= i - lag < NB:
                stage(i - lag, (i - lag) % 2, (i - lag) // 2)

    for i in range(head):
        peeled(i)
    with eng.Fori(0, (NB - head) // 2) as it:
        for v in range(2):
            for stage, lag in stages:
                at = head + v - lag
                stage(it * 2 + at, at % 2, it + at // 2)
    for i in range(NB, NB + max(lag for _, lag in stages)):
        peeled(i)


def some(ap, at, n):
    return ap[:, at:at + n] if isinstance(at, int) else ap[:, bass.ds(at, n)]


def one(ap, at):
    return ap[:, at, :] if isinstance(at, int) else ap[:, bass.ds(at, 1), :].rearrange("p o d -> p (o d)")


def over(ap, n):
    return bass.AP(tensor=ap.tensor, offset=ap.offset, ap=list(ap.ap) + [[0, n]])


def mid(ap, n):
    a = list(ap.ap)
    return bass.AP(tensor=ap.tensor, offset=ap.offset, ap=[a[0], [0, n]] + a[1:])


def build(nc, x, wqT, wkT, wvT, woT, bq, bk, bv, bo, relb, wcat0, gate, shw, shb, gamma, beta,
          nw, wqkT1, wv1, woT1, temp, rw1, rb1, rw2, rb2, wcat1, out):
    fp32, bf16, i32, u32 = mybir.dt.float32, mybir.dt.bfloat16, mybir.dt.int32, mybir.dt.uint32
    ALU, ACT, AX = mybir.AluOpType, mybir.ActivationFunctionType, mybir.AxisListType

    ext_dram = nc.dram_tensor("ext_dram", [2, H0, EXT], fp32, kind="Internal").ap()
    stk_dram = nc.dram_tensor("stk_dram", [NB, 2, H0, STK, S], bf16, kind="Internal").ap()
    xg_dram = [nc.dram_tensor(f"xg_dram{l}", [(NJ0, NJ1)[l] * TS, XW], fp32, kind="Internal").ap() for l in range(2)]
    yg_dram = [nc.dram_tensor(f"yg_dram{l}", [TOPK * TOK + (NJ0, NJ1)[l] * TS, D], fp32, kind="Internal").ap() for l in range(2)]

    ctx = ExitStack()
    with ctx:
        def sb(name, shape, dt=fp32):
            return ctx.enter_context(nc.sbuf_tensor(name, shape, dt))

        def sem(name):
            return ctx.enter_context(nc.semaphore(name))

        bufA = sb("bufA", [P, T, D])
        bufB, bufC = (sb(f"buf{c}", [P, T, XW]) for c in "BC")
        yy = sb("yy", [P, TOPK, T, D])
        x_sb = s_sb = bufA
        xres = bufB[:, :, 0:D]
        sh_sb = bufC[:, :, 0:D]
        xn_sb = (bufB, bufC)
        yyf = yy[:, :, :, :].rearrange("p k t d -> p (k t d)")
        vall = yyf[:, 0:TOK].rearrange("p (t d) -> p t d", d=D)
        biasT = sb("biasT", [P, H0, BW])
        biasA = sb("biasA", [P, H0, BW], bf16)
        wqk_sb = sb("wqk_sb", [P, 2 * D])
        wv_sb = sb("wv_sb", [P, D])
        wo_sb = sb("wo_sb", [P, D])
        cols = sb("cols", [P, 8])
        bo_bc = sb("bo_bc", [P, D])
        gate_sb = sb("gate_sb", [P, E0])
        shw_sb = sb("shw_sb", [P, D])
        shb_sb = sb("shb_sb", [1, D])
        gamma_bc = sb("gamma_bc", [P, D])
        beta_bc = sb("beta_bc", [P, D])
        wqk1_sb = sb("wqk1_sb", [P, 2 * D])
        wv1_sb = sb("wv1_sb", [P, D])
        wo1_sb = sb("wo1_sb", [P, D])
        rw1_sb = sb("rw1_sb", [P, 2 * P])
        rb1_sb = sb("rb1_sb", [P, 2])
        rw2_sb = sb("rw2_sb", [P, 2, E1])
        rb2_bc = sb("rb2_bc", [P, E1])
        ext_sb = sb("ext_sb", [H0, EXT])
        extr_sb = sb("extr_sb", [H0, EXT])
        empty = sb("empty", [P, EROWS * XW])
        ident = sb("ident", [P, P])
        identb = sb("identb", [P, P], bf16)
        below = sb("below", [P, P])
        ones = sb("ones", [P, P])
        selh = sb("selh", [P, H0 // 2, P], bf16)
        blockm = sb("blockm", [P, P])
        eidx = sb("eidx", [P, E0])
        jidx = sb("jidx", [P, NSLOT // TS])
        pidx = sb("pidx", [P, 1])
        spare = sb("spare", [P, NSLOT // P])
        toki, tokf = sb("toki", [P, T], i32), sb("tokf", [P, T])
        stats = sb("stats", [P, T, 6])
        mean = sb("mean", [P, T])
        rstd = sb("rstd", [P, T])
        rrms = sb("rrms", [P, T])
        var = sb("var", [P, T])
        tmpa = sb("tmpa", [P, T])
        tmpb = sb("tmpb", [P, T])
        lg = sb("lg", [P, T, E0])
        rt = [sb(f"rt{i}", [P, T * E0]) for i in range(4)]
        hot = [sb(f"hot{k}", [P, T * E0]) for k in range(TOPK)]
        pk = [sb(f"pk{k}", [P, T]) for k in range(TOPK)]
        wk = [sb(f"wk{k}", [P, T]) for k in range(TOPK)]
        slotf = [sb(f"slotf{k}", [P, T]) for k in range(TOPK)]
        sloti = [sb(f"sloti{k}", [P, T], i32) for k in range(TOPK)]
        ecnt = [sb(f"ecnt{i}", [P, E0]) for i in range(4)]
        ecnti = sb("ecnti", [P, E0], i32)
        ejm = sb("ejm", [P, NSLOT // TS * E0])
        ejf = sb("ejf", [P, NSLOT // TS])
        widx = sb("widx", [P, NSLOT // TS], i32)
        xs = [sb(f"xs{u}", [P, 2, D]) for u in range(2)]
        xT = [sb(f"xT{u}", [P, 2 * P]) for u in range(2)]
        rh = [sb(f"rh{u}", [P, 2, 2 * P]) for u in range(2)]
        work = sb("work", [P, 13312])

        def carve():
            at = [0]

            def take(n, dt=fp32):
                words = n if dt == fp32 else n // 2
                a = work[:, at[0]:at[0] + words]
                at[0] += words
                assert at[0] <= 13312, at
                return a if dt == fp32 else a.bitcast(dt)
            return take

        take = carve()
        qst = [take(H0 // 2 * S, bf16).rearrange("p (t s) -> p t s", s=S) for _ in range(2)]
        kst = [take(H0 * S, bf16).rearrange("p (t e s) -> p t e s", e=2, s=S) for _ in range(2)]
        strip = work[:, 0:H0 * BW].rearrange("p (h u) -> p h u", h=H0)
        vaug = [take(2 * H0 * (DK + 1)).rearrange("p (k h c) -> p k h c", k=2, h=H0) for _ in range(2)]
        nmax = take(2 * H0, bf16).rearrange("p (q h) -> p q h", q=2)
        nmaxT = [take(S, bf16) for _ in range(2)]
        scores = [take(2 * S) for _ in range(2)]
        probs = [take(2 * S) for _ in range(2)]
        oT = take(4 * S).rearrange("p (g s) -> p g s", g=4)
        on = take(2 * D).rearrange("p (q d) -> p q d", q=2)
        onT = take(2 * P)
        rden = take(2 * H0).rearrange("p (q h) -> p q h", q=2)
        qkf = [take(2 * S) for _ in range(2)]
        qkr = take(2 * S)
        pieces = [yyf[:, TOK + u * 3 * S:TOK + (u + 1) * 3 * S].bitcast(bf16).rearrange("p (c s) -> p c s", c=3)
                  for u in range(2)]
        take = carve()
        wb = [take(WROW) for _ in range(NWB)]
        xg = [take(2 * XW).rearrange("p (s w) -> p s w", s=2) for _ in range(2)]
        hb = [take(HC * TS).rearrange("p (c s) -> p c s", c=HC) for _ in range(2)]
        yb = [take(2 * D).rearrange("p (s d) -> p s d", s=2) for _ in range(2)]
        yid = [take(2).bitcast(i32) for _ in range(NWB)]
        yw = [take(2) for _ in range(NWB)]
        take = carve()
        cc = [take(D) for _ in range(2)]
        uu = take(NB * D).rearrange("p (b o) -> p b o", b=NB)
        pr = [take(2 * D) for _ in range(2)]
        x2 = [take(2 * D).rearrange("p (j d) -> p j d", j=2) for _ in range(2)]
        x2T = [take(2 * P) for _ in range(2)]
        nsq = take(2 * NB).rearrange("p (b k) -> p b k", b=NB)
        rin = take(2 * NB).rearrange("p (b k) -> p b k", b=NB)
        nt1, nt2 = take(2 * NB), take(2 * NB)
        gk = [take(D) for _ in range(2)]
        gm = [take(D) for _ in range(2)]
        at1 = [take(D) for _ in range(2)]
        an = [take(D) for _ in range(2)]
        ms = [take(D) for _ in range(2)]
        ps_ = [take(D) for _ in range(2)]
        nm1 = [take(1) for _ in range(2)]
        sm1 = [take(1) for _ in range(2)]
        rs1 = [take(1) for _ in range(2)]

        bank = [ctx.enter_context(nc.psum_tensor(f"bank{i}", [P, 512], fp32)) for i in range(8)]

        bq_c, bk_c, bv_c, nw_c, temp_c, bqs_c, et_c = (cols[:, i:i + 1] for i in range(7))

        s_x, s_w, s_wf = sem("x_loaded"), sem("weights_loaded"), sem("weights_folded")
        s_c, s_cc = sem("constants_made"), sem("constant_steps")
        s_relb, s_edge, s_extd, s_strip = sem("relb_loaded"), sem("edges_filled"), sem("ext_stored"), sem("strip_loaded")
        s_bt, s_ba, s_stk0 = sem("biasT_loaded"), sem("biasA_made"), sem("stacks_zeroed")
        s_zero, s_xgz = sem("zero_made"), sem("xg_zeroed")
        s_dve, s_pool, s_act = sem("dve_steps"), sem("pool_steps"), sem("act_steps")

        block = ctx.enter_context(nc.Block())

        def phase_sems(phase, l, names):
            return {n: sem(f"{phase}{l}_{n}") for n in names}

        PRE = ["xs", "xs_saved", "T", "xT", "gs", "lg"]
        pre = [phase_sems("pre", 0, PRE + ["sh", "shg", "qkv", "qkf", "v", "split", "pieces", "stored0", "stored1"]),
               phase_sems("pre", 1, PRE + ["rh1", "rhs"])]
        ROU = ["lgx", "exped", "A", "cum", "routed", "scattered"]
        rou = [phase_sems("route", l, ROU) for l in range(2)]
        MOE = ["W0", "W1", "W2", "W3", "xg0", "xg1", "T", "xT", "up", "gelu", "down", "yb", "y", "ids",
               "stored0", "stored1"]
        moe = [phase_sems("experts", l, MOE) for l in range(2)]
        COM = [f"g{i}" for i in range(4)] + ["z", "silu", "x1"]
        com = [phase_sems("combine", l, COM) for l in range(2)]
        s_out, s_x2 = sem("out_stored"), sem("x_back")
        A0 = phase_sems("attend", 0, ["init", "stk00", "stk01", "stk10", "stk11", "v_sb", "A", "Ared", "mT", "nmT", "B", "S", "E", "PV", "oTs",
                                      "To", "on", "Tn", "onT", "wo", "s", "s2"])
        A1 = phase_sems("attend", 1, ["x2", "C", "Cs", "U", "pr", "nn", "nns",
                            "x2b", "T", "x2T", "G", "gk", "GT", "gm", "mx", "exp", "rs", "an", "M", "Ms", "Pm", "Ps", "F", "s"])

        NW = 22
        NEMPTY = [nj * TS // (P * EROWS) for nj in (NJ0, NJ1)]

        @block.sync
        def _(sp):
            sp.dma_start(ext_sb[:, S - 1 - MAXREL:S + MAXREL], relb).then_inc(s_relb, 16)
            xv = x.rearrange("(t p) d -> p t d", p=P)
            for c in range(4):
                sp.dma_start(x_sb[:, c * 8:c * 8 + 8, :], xv[:, c * 8:c * 8 + 8, :]).then_inc(s_x, 16)
            loads = [(wqk_sb[:, 0:D], wqT), (wqk_sb[:, D:2 * D], wkT), (wv_sb[:, :], wvT), (wo_sb[:, :], woT),
                     (bq_c, bq), (bk_c, bk), (bv_c, bv), (nw_c, nw), (temp_c, temp),
                     (bo_bc[:, :], bo.partition_broadcast(P)), (gate_sb[:, :], gate), (shw_sb[:, :], shw),
                     (shb_sb[:, :], shb.unsqueeze(0)), (gamma_bc[:, :], gamma.partition_broadcast(P)),
                     (beta_bc[:, :], beta.partition_broadcast(P)), (wqk1_sb[:, :], wqkT1), (wv1_sb[:, :], wv1),
                     (wo1_sb[:, :], woT1), (rw1_sb[:, :], rw1), (rb1_sb[:, :], rb1), (rw2_sb[:, :, :], rw2),
                     (rb2_bc[:, :], rb2.partition_broadcast(P))]
            assert len(loads) == NW
            for dst, src in loads:
                sp.dma_start(dst, src).then_inc(s_w, 16)
            sp.wait_ge(s_edge, 3)
            sp.dma_start(ext_dram[0], ext_sb[:, :]).then_inc(s_extd, 16)
            sp.dma_start(ext_dram[1], extr_sb[:, :]).then_inc(s_extd, 16)
            sp.wait_ge(s_extd, 32)
            sp.dma_start(strip, bass.AP(tensor=ext_dram.tensor, offset=0, ap=[[1, P], [EXT, H0], [1, BW]])
                         ).then_inc(s_strip, 16)
            sp.dma_start(biasT[:, :, :], bass.AP(tensor=ext_dram.tensor, offset=H0 * EXT, ap=[[1, P], [EXT, H0], [1, BW]])
                         ).then_inc(s_bt, 16)

            def store_empty(l):
                xe = xg_dram[l].rearrange("(c p r) w -> c p (r w)", p=P, r=EROWS)
                for c in range(NEMPTY[l]):
                    sp.dma_start(xe[c], empty[:, :]).then_inc(s_xgz, 16)

            sp.wait_ge(s_zero, 1)
            store_empty(0)
            with sp.Fori(0, NB // 2) as it:
                for u in range(2):
                    b = it * 2 + u
                    sp.wait_ge(pre[0]["pieces"], b + 1)
                    for i, piece_of in enumerate((QPIECE, KPIECE)):
                        for r, c in enumerate(piece_of):
                            dst = stk_dram[bass.ds(b, 1), i, :, r * DK:(r + 1) * DK, :].rearrange("o h d s -> (o h) d s")
                            sp.dma_start(dst, pieces[u][:, c, i * S:(i + 1) * S]).then_inc(pre[0][f"stored{u}"], 16)
            for u in range(2):
                sp.wait_ge(pre[0][f"stored{u}"], (NB // 2 + 1) * 2 * TERMS * 16)
            sp.wait_ge(s_stk0, 1)

            def load_stacks(b, u, g):
                for e in range(2):
                    rows = slice(e * HALF, e * HALF + STK)
                    ts = slice(g * 4, g * 4 + 4)

                    def src(i):
                        heads = stk_dram[b, i] if isinstance(b, int) else stk_dram[bass.ds(b, 1), i].rearrange("o h r s -> (o h) r s")
                        return heads.rearrange("(t e) r s -> r t e s", e=2)[:, ts, e, :]
                    sp.dma_start(qst[u][rows, ts, :], src(0)).then_inc(A0[f"stk{u}{g}"], 16)
                    sp.dma_start(kst[u][rows, ts, e, :], src(1)).then_inc(A0[f"stk{u}{g}"], 16)

            for b in range(2):
                for g in range(2):
                    load_stacks(b, b, g)
            with sp.Fori(0, NB // 2 - 1) as it:
                for u in range(2):
                    for g in range(2):
                        b = it * 2 + u
                        sp.wait_ge(A0["B"], b * 16 + (32 + 8 * g + 8))
                        load_stacks(b + 2, u, g)
            store_empty(1)
            for l, nj in enumerate((NJ0, NJ1)):
                m = moe[l]
                xgv = xg_dram[l].rearrange("(j s p) w -> j p s w", s=2, p=P)
                wcat = (wcat0, wcat1)[l]

                def load(j, v):
                    u = v % 2
                    sp.wait_ge(m["T"], j + 1)
                    sp.wait_ge(m["ids"], j + 1)
                    src = xgv[j] if isinstance(j, int) else xgv[bass.ds(j, 1)].rearrange("o p s w -> p (o s) w")
                    sp.dma_start(xg[u], src).then_inc(m[f"xg{u}"], 16)
                    sp.wait_ge(m["y"], j + 1)
                    at = widx[0:1, j:j + 1] if isinstance(j, int) else widx[0:1, bass.ds(j, 1)]
                    row = sp.value_load(at, min_val=0, max_val=((E0, E1)[l] - 1) * P)
                    sp.dma_start(wb[v], wcat[bass.ds(row, P), :]).then_inc(m[f"W{v}"], 16)

                sp.wait_ge(rou[l]["scattered"], 16 * TOPK * T)
                if l == 0:
                    sp.dma_start(xres, xv).then_inc(s_x2, 16)
                sp.wait_ge((A0, A1)[l]["s"], NB + (2, 1)[l])
                with sp.Fori(0, nj // NWB) as it:
                    for v in range(NWB):
                        load(it * NWB + v, v)
                sp.wait_ge(m["stored0"], 16 * nj)
                sp.wait_ge(m["stored1"], 16 * nj)
                yv = yg_dram[l][0:TOPK * TOK, :].rearrange("(k t p) d -> p k t d", k=TOPK, p=P)
                for q in range(4):
                    for k in range(TOPK):
                        sp.dma_start(yy[:, k, q * 8:q * 8 + 8, :], yv[:, k, q * 8:q * 8 + 8, :]).then_inc(com[l][f"g{q}"], 16)
            ov = out.rearrange("(t p) d -> p t d", p=P)
            for g in range(4):
                sp.wait_ge(com[1]["x1"], g + 1)
                sp.dma_start(ov[:, g * 8:g * 8 + 8, :], yy[:, 0, g * 8:g * 8 + 8, :]).then_inc(s_out, 16)
            sp.wait_ge(s_out, 64)

        @block.gpsimd
        def _(pool):
            g = nc.gpsimd
            st = Steps(pool, s_pool)
            st.did(g.memset(ident[:, :], 0.0))
            st.did(g.memset(below[:, :], 1.0))
            st.did(g.memset(selh[:, :, :], 0.0))
            st.did(g.memset(blockm[:, :], 0.0))
            st.did(g.iota(widx[:, 0:E0], pattern=[[1, E0]], base=-E0, channel_multiplier=0))
            st.did(g.iota(ejm[:, 0:NSLOT // TS].bitcast(i32), pattern=[[1, NSLOT // TS]], base=0, channel_multiplier=0))
            st.did(g.iota(sloti[0][:, 0:1], pattern=[[1, 1]], base=0, channel_multiplier=1))
            g.memset(ones[:, :], 1.0).then_inc(s_c, 1)
            st.did(g.memset(empty[:, :], 0.0))
            st.did(g.iota(toki[:, :], pattern=[[P, T]], base=0, channel_multiplier=1))
            st.did(g.iota(ejm[:, P:P + NSLOT // P].bitcast(i32), pattern=[[P, NSLOT // P]], base=TOPK * TOK,
                          channel_multiplier=1))
            st.sync()
            g.memset(empty[:, :].rearrange("p (r c) -> p r c", c=XW)[:, :, D:XW], NOWHERE).then_inc(s_zero, 1)
            g.tensor_copy(tokf[:, :], toki[:, :]).then_inc(s_c, 1)
            g.tensor_copy(spare[:, :], ejm[:, P:P + NSLOT // P].bitcast(i32)).then_inc(s_c, 1)
            g.affine_select(out=ident[:, :], in_=ident[:, :], compare_op=ALU.not_equal, fill=1.0, base=0,
                            pattern=[[-1, P]], channel_multiplier=1).then_inc(s_c, 1)
            g.affine_select(out=below[:, :], in_=below[:, :], compare_op=ALU.is_gt, fill=0.0, base=0,
                            pattern=[[1, P]], channel_multiplier=-1).then_inc(s_c, 1)
            g.affine_select(out=selh[:, :, :], in_=selh[:, :, :], compare_op=ALU.not_equal, fill=1.0, base=0,
                            pattern=[[-1, H0 // 2], [0, P]], channel_multiplier=1).then_inc(s_c, 1)
            g.tensor_copy(eidx[:, :], widx[:, 0:E0]).then_inc(s_c, 1)
            g.tensor_copy(jidx[:, :], ejm[:, 0:NSLOT // TS].bitcast(i32)).then_inc(s_c, 1)
            g.tensor_copy(pidx[:, :], sloti[0][:, 0:1]).then_inc(s_c, 1)
            bmv = blockm[:, :].rearrange("p (h d) -> p h d", h=H1)
            st.did(g.affine_select(out=bmv, in_=bmv, compare_op=ALU.is_ge, fill=OFF, base=0,
                                   pattern=[[-DH1, H1], [0, DH1]], channel_multiplier=1))
            st.sync()
            g.affine_select(out=bmv, in_=bmv, compare_op=ALU.is_ge, fill=OFF, base=DH1 - 1,
                            pattern=[[DH1, H1], [0, DH1]], channel_multiplier=-1).then_inc(s_c, 1)
            pool.wait_ge(s_c, 10)
            g.tensor_copy(identb[:, :], ident[:, :]).then_inc(s_c, 1)

            def save(l):
                m = pre[l]
                with pool.Fori(0, NB // 2) as it:
                    for u in range(2):
                        b = it * 2 + u
                        pool.wait_ge(m["xs"], b + 1)
                        g.tensor_copy(xn_sb[l][:, bass.ds(b * 2, 2), 0:D], xs[u][:, :, :]).then_inc(m["xs_saved"], 1)

            def route_and_scatter(l):
                pool.wait_ge(rou[l]["routed"], 1)
                pool.wait_ge(s_xgz, sum(NEMPTY[:l + 1]) * 16)
                pool.wait_ge(pre[l]["xs_saved"], NB)
                for k in range(TOPK):
                    st.did(g.tensor_scalar(xn_sb[l][:, :, D], tokf[:, :], float(k * TOK), None, ALU.add))
                    st.link(g.tensor_copy(xn_sb[l][:, :, D + 1], wk[k][:, :]))
                    for t in range(T):
                        g.indirect_dma_start(
                            out=xg_dram[l], out_offset=bass.IndirectOffsetOnAxis(ap=sloti[k][:, t:t + 1].bitcast(u32), axis=0),
                            in_=xn_sb[l][:, t, :], in_offset=None).then_inc(rou[l]["scattered"], 16)
                    pool.wait_ge(rou[l]["scattered"], 16 * T * (k + 1))

            def store_outputs(l, nj):
                m = moe[l]
                with pool.Fori(0, nj // NWB) as it:
                    for v in range(NWB):
                        j, u = it * NWB + v, v % 2
                        outputs = pool.to_reg(j + 5)
                        pool.wait_ge(m["ids"], 3 + v)
                        pool.wait_ge(m["y"], outputs)
                        for s_ in range(2):
                            g.indirect_dma_start(
                                out=yg_dram[l], out_offset=bass.IndirectOffsetOnAxis(ap=yid[v][:, s_:s_ + 1].bitcast(u32), axis=0),
                                in_=yb[u][:, s_, :], in_offset=None).then_inc(m[f"stored{u}"], 16)

            for u in range(2):
                g.memset(vaug[u], 1.0).then_inc(A0["init"], 1)
                g.memset(nmaxT[u], 0.0).then_inc(A0["init"], 1)
            save(0)
            pool.wait_ge(s_ba, 1)
            g.memset(work[:, 0:H0 * BW], 0.0).then_inc(s_stk0, 1)
            route_and_scatter(0)
            store_outputs(0, NJ0)
            save(1)
            route_and_scatter(1)
            store_outputs(1, NJ1)

        @block.tensor
        def _(pe):
            mm, tr = nc.tensor.matmul, nc.tensor.transpose
            pe.wait_ge(s_c, 11)
            pe.wait_ge(s_w, 16 * NW)

            def pre_pe(l):
                m = pre[l]

                def transposes(b, u, turn):
                    pe.wait_ge(m["xs"], b + 1)
                    pe.wait_ge(m["xT"], b + 1)
                    tr(bank[u][:, 0:P], xs[u][:, 0, :], ident[:, :])
                    tr(bank[u][:, P:2 * P], xs[u][:, 1, :], ident[:, :]).then_inc(m["T"], 1)

                def project(b, u, turn):
                    pe.wait_ge(m["xT"], b + 3)
                    pe.wait_ge(m["qkf"], b + 1)
                    for i in range(2):
                        last = mm(bank[6 + u][:, i * S:(i + 1) * S], wqk_sb[:, i * D:(i + 1) * D], xT[u][:, :],
                                  start=True, stop=True)
                    last.then_inc(m["qkv"], 1)
                    pe.wait_ge(m["lg"], b + 1)
                    pe.wait_ge(m["v"], b + 1)
                    pe.wait_ge(m["sh"], b + 1)
                    for j in range(2):
                        mm(bank[2 + u][:, S + j * D:S + (j + 1) * D], xT[u][:, j * P:(j + 1) * P], wv_sb[:, :],
                           start=True, stop=True)
                        mm(bank[2 + u][:, j * E0:(j + 1) * E0], xT[u][:, j * P:(j + 1) * P], gate_sb[:, :],
                           start=True, stop=True)
                        o = bank[4 + u][:, j * D:(j + 1) * D]
                        mm(o, xT[u][:, j * P:(j + 1) * P], shw_sb[:, :], start=True, stop=False)
                        last = mm(o, ones[0:1, :], shb_sb[:, :], start=False, stop=True)
                    last.then_inc(m["gs"], 1)

                def router_hidden(b, u, turn):
                    pe.wait_ge(m["xT"], b + 3)
                    pe.wait_ge(m["rhs"], b + 1)
                    for c in range(2):
                        last = mm(bank[4 + u][:, c * S:(c + 1) * S], rw1_sb[:, c * P:(c + 1) * P], xT[u][:, :],
                                  start=True, stop=True)
                    last.then_inc(m["rh1"], 1)

                def router_logits(b, u, turn):
                    pe.wait_ge(m["rhs"], b + 3)
                    pe.wait_ge(m["lg"], b + 1)
                    for j in range(2):
                        for c in range(2):
                            last = mm(bank[2 + u][:, j * E1:(j + 1) * E1], rh[u][:, c, j * P:(j + 1) * P],
                                      rw2_sb[:, c, :], start=(c == 0), stop=(c == 1))
                    last.then_inc(m["gs"], 1)

                if l == 0:
                    staged(pe, [(transposes, 1), (project, 2)])
                else:
                    staged(pe, [(transposes, 1), (router_hidden, 2), (router_logits, 3)])

            def route_pe(l, ne):
                pe.wait_ge(rou[l]["A"], 1)
                pe.wait_ge(pre[l]["lg"], 2 + NB)
                mm(bank[0][:, 0:T * ne], below[:, :], rt[3][:, 0:T * ne], start=True, stop=True)
                mm(bank[1][:, 0:T * ne], ones[:, :], rt[3][:, 0:T * ne], start=True, stop=True).then_inc(rou[l]["cum"], 1)

            pre_pe(0)
            route_pe(0, E0)

            a = A0
            PA, PB, PO, PX, PY = bank[0:2], bank[2:4], bank[4:6], bank[6], bank[7]
            PXh = PX[:, :].bitcast(bf16)

            def max_scores(n, u, pair, i):
                t, qt = i // 2, i % 2
                o = PA[i % 2]
                if i % 8 == 0:
                    pe.wait_ge(a[f"stk{u}{i // 8}"], pair * 64 + 64)
                pe.wait_ge(a["Ared"], n * 16 + (i + 1))
                mm(o[:, :], qst[u][:, t, qt * P:(qt + 1) * P], kst[u][:, t, :, :], start=True, stop=False)
                v = P * (1 - qt)
                mm(o[:, :], identb[:, :], biasA[:, 2 * t:2 * t + 2, v:v + S], start=False, stop=True).then_inc(a["A"], 1)

            def transpose_maxima(n, g):
                pe.wait_ge(a["Ared"], n * 16 + (8 * g + 10))
                for q in range(2):
                    last = tr(PXh[0:H0 // 2, q * P:(q + 1) * P], nmax[:, q, 8 * g:8 * g + 8], identb[:, :])
                last.then_inc(a["mT"], 1)

            def exp_scores(b, u, h):
                o = PB[h % 2]
                if h % 8 == 0:
                    pe.wait_ge(a["nmT"], b * 2 + (h // 8 + 1))
                pe.wait_ge(a["S"], b * 16 + (h + 1))
                for k in range(2):
                    mm(o[:, k * S:(k + 1) * S], kst[u][:, h // 2, h % 2, k * P:(k + 1) * P], qst[u][:, h // 2, :],
                       start=True, stop=False)
                    last = mm(o[:, k * S:(k + 1) * S], selh[:, h % 8, :], nmaxT[h // 8], start=False, stop=True)
                last.then_inc(a["B"], 1)

            def weigh_values(b, u, h):
                gr, i = h // 4, h % 4
                pe.wait_ge(a["E"], b * 16 + (h + 3))
                if h == 0:
                    pe.wait_ge(a["v_sb"], b + 1)
                if i == 0:
                    pe.wait_ge(a["oTs"], b * 4 + (gr + 1))
                for k in range(2):
                    last = mm(PO[gr % 2][32 * i:32 * i + DK + 1, 0:S], vaug[u][:, k, h, :], probs[h % 2][:, k * S:(k + 1) * S],
                              start=(k == 0), stop=(k == 1))
                last.then_inc(a["PV"], 1)

            def transpose_outputs(b):
                pe.wait_ge(a["oTs"], b * 4 + 6)
                pe.wait_ge(a["s"], b + 1)
                for q in range(2):
                    for gr in range(4):
                        last = tr(bank[6 + q][:, gr * P:(gr + 1) * P], oT[:, gr, q * P:(q + 1) * P], ident[:, :])
                    last.then_inc(a["To"], 1)

            def transpose_back(b):
                pe.wait_ge(a["on"], b * 2 + 2)
                for q in range(2):
                    last = tr(PX[:, q * P:(q + 1) * P], on[:, q, :], ident[:, :])
                last.then_inc(a["Tn"], 1)

            def project_out(b):
                pe.wait_ge(a["onT"], b + 1)
                for q in range(2):
                    last = mm(PY[:, q * D:(q + 1) * D], onT[:, q * P:(q + 1) * P], wo_sb[:, :], start=True, stop=True)
                last.then_inc(a["wo"], 1)

            def attend(b, u, pair, first=False, ahead=True):
                for h in range(H0):
                    exp_scores(b, u, h)
                    if ahead:
                        max_scores(b + 1, 1 - u, pair, h)
                    if h:
                        weigh_values(b, u, h - 1)
                    elif not first:
                        weigh_values(b - 1, 1 - u, H0 - 1)
                    if h == 1:
                        transpose_maxima(b, 1)
                    elif h == 4 and not first:
                        pe.wait_ge(a["nmT"], b * 2 + 2)
                        transpose_outputs(b - 1)
                    elif h == 7 and not first:
                        transpose_back(b - 1)
                    elif h == 10 and not first:
                        project_out(b - 1)
                    elif h == 12 and ahead:
                        transpose_maxima(b + 1, 0)

            pe.wait_ge(s_ba, 1)
            pe.wait_ge(a["init"], 6)
            pe.wait_ge(rou[0]["routed"], 1)
            for i in range(H0):
                max_scores(0, 0, 0, i)
            transpose_maxima(0, 0)
            attend(0, 0, 0, first=True)
            with pe.Fori(0, NB // 2 - 1) as it:
                attend(it * 2 + 1, 1, it + 1)
                attend(it * 2 + 2, 0, it + 1)
            attend(NB - 1, 1, 0, ahead=False)
            weigh_values(NB - 1, 1, H0 - 1)
            transpose_outputs(NB - 1)
            transpose_back(NB - 1)
            project_out(NB - 1)

            def experts(l, nj):
                m = moe[l]
                XT, HP, YP = bank[0:2], (bank[2:4], bank[4:6]), bank[6:8]

                def transposes(j, u, half):
                    pe.wait_ge(m[f"xg{u}"], half * 16 + 16)
                    pe.wait_ge(m["xT"], j + 1)
                    tr(XT[u][:, 0:P], xg[u][:, 0, 0:D], ident[:, :])
                    tr(XT[u][:, P:2 * P], xg[u][:, 1, 0:D], ident[:, :]).then_inc(m["T"], 1)

                def up(j, v, fourth):
                    u = v % 2
                    pe.wait_ge(m[f"W{v}"], fourth * 16 + 16)
                    pe.wait_ge(m["xT"], j + 3)
                    pe.wait_ge(m["gelu"], j * 4 + 4)
                    for c in range(HC):
                        last = mm(HP[u][c // 2][:, (c % 2) * TS:(c % 2 + 1) * TS], wb[v][:, c * P:(c + 1) * P], xT[u][:, :],
                                  start=True, stop=True)
                        if c % 2:
                            last.then_inc(m["up"], 1)

                def down(j, v):
                    u = v % 2
                    pe.wait_ge(m["gelu"], j * 4 + 12)
                    pe.wait_ge(m["y"], j + 3)
                    for s_ in range(2):
                        for c in range(HC):
                            last = mm(YP[u][:, s_ * D:(s_ + 1) * D], hb[u][:, c, s_ * P:(s_ + 1) * P],
                                      wb[v][:, HID + c * D:HID + (c + 1) * D], start=(c == 0), stop=(c == HC - 1))
                    last.then_inc(m["down"], 1)

                transposes(0, 0, 0)
                up(0, 0, 0)
                transposes(1, 1, 0)
                for j in range(1, NWB):
                    up(j, j, 0)
                    transposes(j + 1, (j + 1) % 2, (j + 1) // 2)
                    down(j - 1, j - 1)
                with pe.Fori(1, nj // NWB - 1) as it:
                    for v in range(NWB):
                        j = it * NWB + v
                        up(j, v, it)
                        transposes(j + 1, (v + 1) % 2, it * 2 + (v + 1) // 2)
                        down(j - 1, (v - 1) % NWB)
                for j in range(nj - NWB, nj):
                    up(j, j % NWB, j // NWB)
                    if j + 1 < nj:
                        transposes(j + 1, (j + 1) % 2, (j + 1) // 2)
                    down(j - 1, (j - 1) % NWB)
                down(nj - 1, NWB - 1)

            experts(0, NJ0)
            pre_pe(1)
            route_pe(1, E1)

            a = A1
            pe.wait_ge(s_wf, 1)

            def gram(b, u, turn):
                pe.wait_ge(a["x2"], b + 1)
                pe.wait_ge(a["Cs"], b + 1)
                for j in range(2):
                    last = mm(bank[u][:, 0:D], x2[u][:, j, :], x2[u][:, j, :], start=(j == 0), stop=(j == 1))
                last.then_inc(a["C"], 1)

            def gram_times_weights(b, u, turn):
                pe.wait_ge(a["Cs"], b + 3)
                pe.wait_ge(a["pr"], b + 1)
                mm(bank[2 + u][:, 0:2 * D], cc[u], wqk1_sb[:, :], start=True, stop=True).then_inc(a["U"], 1)

            def norms(b, u, turn):
                pe.wait_ge(a["pr"], b + 3)
                pe.wait_ge(a["nns"], b + 1)
                for k in range(2):
                    last = mm(bank[4 + u][:, k:k + 1], pr[u][:, k * D:(k + 1) * D], ones[:, 0:1], start=True, stop=True)
                last.then_inc(a["nn"], 1)

            staged(pe, [(gram, 1), (gram_times_weights, 2), (norms, 3)])
            pe.wait_ge(a["nns"], NB + 2)

            def similarity(b, u, turn):
                pe.wait_ge(a["gk"], b + 1)
                mm(bank[2 + u][:, 0:D], wqk1_sb[:, D:2 * D], one(uu, b), start=True, stop=True).then_inc(a["G"], 1)

            def transpose_similarity(b, u, turn):
                pe.wait_ge(a["gk"], b + 3)
                pe.wait_ge(a["gm"], b + 1)
                tr(bank[4 + u][:, 0:P], gk[u], ident[:, :]).then_inc(a["GT"], 1)

            def weights_times_out(b, u, turn):
                pe.wait_ge(a["an"], b + 3)
                pe.wait_ge(a["Ms"], b + 1)
                mm(bank[6][:, 0:D], an[u], wo1_sb[:, :], start=True, stop=True).then_inc(a["M"], 1)

            def times_values(b, u, turn):
                pe.wait_ge(a["Ms"], b + 2)
                pe.wait_ge(a["Ps"], b + 1)
                mm(bank[1][:, 0:D], wv1_sb[:, :], ms[u], start=True, stop=True).then_inc(a["Pm"], 1)

            def transpose_rows(b, u, turn):
                pe.wait_ge(a["x2b"], b + 1)
                pe.wait_ge(a["x2T"], b + 2)
                tr(bank[0][:, 0:P], x2[u][:, 0, :], ident[:, :])
                tr(bank[0][:, P:2 * P], x2[u][:, 1, :], ident[:, :]).then_inc(a["T"], 1)

            def rows_times_all(b, u, turn):
                pe.wait_ge(a["Ps"], b + 2)
                pe.wait_ge(a["x2T"], b + 3)
                pe.wait_ge(a["s"], b + 1)
                for j in range(2):
                    last = mm(bank[7][:, j * D:(j + 1) * D], x2T[u][:, j * P:(j + 1) * P], ps_[u], start=True, stop=True)
                last.then_inc(a["F"], 1)

            staged(pe, [(similarity, 0), (transpose_similarity, 1), (weights_times_out, 3), (transpose_rows, 4),
                        (times_values, 4), (rows_times_all, 5)])
            experts(1, NJ1)

        @block.scalar
        def _(act):
            A = nc.scalar.activation
            act.sem_inc(pre[0]["xT"], 2)
            act.sem_inc(pre[0]["sh"], 2)
            act.sem_inc(pre[0]["qkf"], 2)
            act.sem_inc(pre[1]["rhs"], 2)
            for n, c in (("E", 2), ("oTs", 2)):
                act.sem_inc(A0[n], c)
            for m in moe:
                act.sem_inc(m["gelu"], 8)
            for n, c in (("Cs", 2), ("x2T", 2), ("Ms", 1), ("Ps", 1)):
                act.sem_inc(A1[n], c)
            act.wait_ge(s_w, 16 * NW)
            A(et_c, temp_c, ACT.Exp).then_inc(s_act, 1)
            act.wait_ge(s_strip, 16)
            A(biasA[:, :, :], bass.AP(tensor=strip.tensor, offset=strip.offset + BW - 1,
                                      ap=[list(strip.ap)[0], [BW, H0], [-1, BW]]), ACT.Copy).then_inc(s_ba, 1)
            act.wait_ge(s_wf, 1)

            def pre_act(l):
                m = pre[l]

                def transposed(b, u, turn):
                    act.wait_ge(m["T"], b + 1)
                    act.wait_ge(m["gs"], b + 1)
                    A(xT[u][:, :], bank[u][:, 0:2 * P], ACT.Copy).then_inc(m["xT"], 1)

                def projected(b, u, turn):
                    act.wait_ge(m["qkv"], b + 1)
                    act.wait_ge(m["split"], b * 3 + 2)
                    A(qkf[u][:, 0:S], bank[6 + u][:, 0:S], ACT.Identity, scale=QSCALE, bias=bqs_c)
                    A(qkf[u][:, S:2 * S], bank[6 + u][:, S:2 * S], ACT.Identity, bias=bk_c).then_inc(m["qkf"], 1)
                    act.wait_ge(m["gs"], b + 3)
                    A(some(sh_sb, b * 2, 2), bank[4 + u][:, 0:2 * D].rearrange("p (j d) -> p j d", j=2), ACT.Copy
                      ).then_inc(m["sh"], 1)

                def hidden(b, u, turn):
                    act.wait_ge(m["rh1"], b + 3)
                    act.wait_ge(m["gs"], b + 1)
                    A(rh[u][:, 0, :], bank[4 + u][:, 0:S], ACT.Gelu, bias=rb1_sb[:, 0:1])
                    A(rh[u][:, 1, :], bank[4 + u][:, S:2 * S], ACT.Gelu, bias=rb1_sb[:, 1:2]).then_inc(m["rhs"], 1)

                if l == 0:
                    staged(act, [(transposed, 1), (projected, 2)])
                    act.wait_ge(m["sh"], NB + 2)
                    A(sh_sb, sh_sb, ACT.Gelu).then_inc(m["shg"], 1)
                else:
                    staged(act, [(hidden, 2)])

            def route_act(l, ne):
                act.wait_ge(rou[l]["lgx"], 1)
                A(rt[0][:, 0:T * ne], rt[0][:, 0:T * ne], ACT.Exp).then_inc(rou[l]["exped"], 1)

            pre_act(0)
            route_act(0, E0)

            a = A0
            PO, PX = bank[4:6], bank[6]

            def fetch_values(n, u):
                act.wait_ge(a["PV"], n * 16 + 16)
                src = vall[:, 2 * n:2 * n + 2, :] if isinstance(n, int) else vall[:, bass.ds(n * 2, 2), :]
                A(vaug[u][:, :, :, 0:DK], src.rearrange("p k (h d) -> p k h d", d=DK), ACT.Copy).then_inc(a["v_sb"], 1)

            def copy_maxima(n, g):
                act.wait_ge(a["mT"], n * 2 + (g + 3))
                act.wait_ge(a["B"], n * 16 + (8 * g + 24))
                A(nmaxT[g][0:H0 // 2, :], PX[:, :].bitcast(bf16)[0:H0 // 2, 0:S], ACT.Copy).then_inc(a["nmT"], 1)

            def copy_group(b, gr, first=False):
                act.wait_ge(a["PV"], b * 16 + (4 * gr + 36))
                if not first:
                    act.wait_ge(a["To"], b * 2)
                A(oT[:, gr, :], PO[gr % 2][:, 0:S], ACT.Copy).then_inc(a["oTs"], 1)

            def add_value_bias(b):
                act.wait_ge(a["Tn"], b + 1)
                A(onT, PX[:, 0:2 * P], ACT.Identity, bias=bv_c).then_inc(a["onT"], 1)

            def attend_act(b, u, first=False, ahead=True):
                for h in range(H0):
                    act.wait_ge(a["S"], b * 16 + (h + 3))
                    act.wait_ge(a["PV"], b * 16 + (h + 31))
                    A(probs[h % 2], scores[h % 2], ACT.Exp).then_inc(a["E"], 1)
                    if h == 1 and not first:
                        copy_group(b - 1, 3)
                    elif h == 2:
                        copy_maxima(b, 1)
                    elif h == 3 and ahead:
                        fetch_values(b + 1, 1 - u)
                    elif h % 4 == 1 and h > 1:
                        copy_group(b, h // 4 - 1, first)
                    elif h == 8 and not first:
                        add_value_bias(b - 1)
                    elif h == 14 and ahead:
                        copy_maxima(b + 1, 0)

            act.wait_ge(s_c, 11)
            act.wait_ge(a["init"], 6)
            act.wait_ge(pre[0]["v"], NB + 2)
            fetch_values(0, 0)
            copy_maxima(0, 0)
            attend_act(0, 0, first=True)
            with act.Fori(0, NB // 2 - 1) as it:
                attend_act(it * 2 + 1, 1)
                attend_act(it * 2 + 2, 0)
            attend_act(NB - 1, 1, ahead=False)
            copy_group(NB - 1, 3)
            add_value_bias(NB - 1)

            def experts(l, nj):
                m = moe[l]
                with act.Fori(0, nj // NWB) as it:
                    for v in range(NWB):
                        j, u = it * NWB + v, v % 2
                        act.wait_ge(m[f"W{v}"], it * 16 + 16)
                        act.wait_ge(m["down"], j + 1)
                        for c in range(HC):
                            if c % 2 == 0:
                                act.wait_ge(m["up"], j * 2 + (5 + c // 2))
                            bc = HID + HC * D + c
                            A(hb[u][:, c, :], bank[2 + 2 * u + c // 2][:, (c % 2) * TS:(c % 2 + 1) * TS], ACT.Gelu,
                              bias=wb[v][:, bc:bc + 1]).then_inc(m["gelu"], 1)

            def silus(l):
                for q in range(4):
                    act.wait_ge(com[l]["z"], q + 1)
                    A(yy[:, 0, q * 8:q * 8 + 8, :], yy[:, 0, q * 8:q * 8 + 8, :], ACT.Silu).then_inc(com[l]["silu"], 1)

            experts(0, NJ0)
            silus(0)
            pre_act(1)
            route_act(1, E1)

            a = A1

            def copy_gram(b, u, turn):
                act.wait_ge(a["C"], b + 3)
                act.wait_ge(a["U"], b + 1)
                A(cc[u], bank[u][:, 0:D], ACT.Copy).then_inc(a["Cs"], 1)

            staged(act, [(copy_gram, 1)])

            def exponents(b, u, turn):
                act.wait_ge(a["mx"], b + 1)
                act.wait_ge(a["an"], b + 1)
                A(at1[u], gm[u], ACT.Exp, bias=nm1[u], accum_out=sm1[u]).then_inc(a["exp"], 1)

            def copy_product(b, u, turn):
                act.wait_ge(a["M"], b + 3)
                act.wait_ge(a["Pm"], b + 1)
                A(ms[u], bank[6][:, 0:D], ACT.Copy).then_inc(a["Ms"], 1)

            def copy_rows(b, u, turn):
                act.wait_ge(a["T"], b + 3)
                act.wait_ge(a["F"], b + 1)
                A(x2T[u], bank[0][:, 0:2 * P], ACT.Copy).then_inc(a["x2T"], 1)

            def scale_product(b, u, turn):
                act.wait_ge(a["Pm"], b + 3)
                A(ps_[u], bank[1][:, 0:D], ACT.Copy, scale=nw_c).then_inc(a["Ps"], 1)

            staged(act, [(exponents, 2), (copy_product, 3), (copy_rows, 4), (scale_product, 4)])
            experts(1, NJ1)
            silus(1)

        @block.vector
        def _(dve):
            V = nc.vector
            st = Steps(dve, s_dve)
            for m in pre:
                dve.sem_inc(m["lg"], 2)
                dve.sem_inc(m["gs"], 2)
            dve.sem_inc(pre[0]["v"], 2)
            dve.sem_inc(pre[0]["split"], 6)
            for u in range(2):
                dve.sem_inc(pre[0][f"stored{u}"], 2 * TERMS * 16)
            dve.sem_inc(pre[1]["rh1"], 2)
            dve.sem_inc(pre[1]["xT"], 2)
            for n, c in (("s", 2), ("Ared", 2), ("S", 2), ("B", 32), ("PV", 32), ("mT", 2)):
                dve.sem_inc(A0[n], c)
            for m in moe:
                for n, c in (("xT", 2), ("y", 4), ("ids", 2), ("T", 2), ("up", 4), ("down", 2)):
                    dve.sem_inc(m[n], c)
            for n, c in (("pr", 2), ("nns", 2), ("gk", 2), ("gm", 2), ("s", 1), ("U", 2), ("F", 2), ("C", 2), ("nn", 2),
                         ("GT", 2), ("exp", 2), ("M", 2), ("an", 2), ("Pm", 2), ("T", 2)):
                dve.sem_inc(A1[n], c)

            def rsqrt(y, v, t1, t2, shape_i=None):
                yi, vi = y.bitcast(i32), v.bitcast(i32)
                st.link(V.tensor_scalar(t1.bitcast(i32), vi, 1, None, ALU.logical_shift_right))
                st.link(V.tensor_scalar(yi, t1.bitcast(i32), -1.0, float(0x5f3759df), ALU.mult, ALU.add))
                for _ in range(4):
                    st.link(V.tensor_tensor(t2, y, y, ALU.mult))
                    st.link(V.tensor_tensor(t1, t2, v, ALU.mult))
                    st.link(V.tensor_scalar(t1, t1, -0.5, 1.5, ALU.mult, ALU.add))
                    st.link(V.tensor_tensor(y, y, t1, ALU.mult))

            def take_stats(src, q):
                for t in range(q * 8, q * 8 + 8):
                    st.did(V.bn_stats(stats[:, t, :], src(t)))

            def finish_stats():
                st.sync()
                m0, v0, m1, v1 = (stats[:, :, i] for i in (1, 2, 4, 5))
                st.did(V.tensor_tensor(tmpa[:, :], m0, m1, ALU.add))
                st.did(V.tensor_tensor(tmpb[:, :], m0, m1, ALU.subtract))
                st.link(V.tensor_tensor(var[:, :], v0, v1, ALU.add))
                st.did(V.tensor_scalar(mean[:, :], tmpa[:, :], 0.5, None, ALU.mult))
                st.link(V.tensor_tensor(tmpb[:, :], tmpb[:, :], tmpb[:, :], ALU.mult))
                st.did(V.tensor_scalar(var[:, :], var[:, :], 1.0 / D, None, ALU.mult))
                st.link(V.tensor_scalar(tmpb[:, :], tmpb[:, :], 0.25, None, ALU.mult))
                st.link(V.tensor_tensor(var[:, :], var[:, :], tmpb[:, :], ALU.add))
                st.link(V.tensor_scalar(tmpb[:, :], var[:, :], LN_EPS, None, ALU.add))
                rsqrt(rstd[:, :], tmpb[:, :], tmpa[:, :], rrms[:, :])

            def pre_dve(l, ne):
                m = pre[l]
                src = (x_sb, xres)[l]

                def normalise(b, u, turn):
                    if not isinstance(b, int) or b >= 2:
                        dve.wait_ge(m["T"], b - 1)
                        dve.wait_ge(m["xs_saved"], b - 1)
                    for j in range(2):
                        t = b * 2 + j
                        last = V.tensor_scalar(xs[u][:, j, :], one(src, t), some(mean, t, 1), some(rstd, t, 1),
                                               ALU.subtract, ALU.mult)
                    last.then_inc(m["xs"], 1)

                def transposed(b, u, turn):
                    dve.wait_ge(m["T"], b + 1)
                    dve.wait_ge(m["rh1"], b + 1)
                    V.tensor_copy(xT[u][:, :], bank[u][:, 0:2 * P]).then_inc(m["xT"], 1)

                def split(b, u, turn):
                    dve.wait_ge(m["qkf"], b + 3)
                    dve.wait_ge(m[f"stored{u}"], turn * (2 * TERMS * 16) + 2 * TERMS * 16)
                    hi, mi, lo = (pieces[u][:, c, :] for c in range(3))
                    V.tensor_copy(hi, qkf[u]).then_inc(m["split"], 1)
                    dve.wait_ge(m["split"], b * 3 + 7)
                    V.tensor_tensor(qkr, qkf[u], hi, ALU.subtract).then_inc(m["split"], 1)
                    dve.wait_ge(m["split"], b * 3 + 8)
                    V.tensor_copy(mi, qkr).then_inc(m["split"], 1)
                    dve.wait_ge(m["split"], b * 3 + 9)
                    V.tensor_tensor(lo, qkr, mi, ALU.subtract).then_inc(m["pieces"], 1)

                def logits(b, u, turn):
                    dve.wait_ge(m["gs"], b + 3)
                    bk = bank[2 + u][:, 0:2 * ne].rearrange("p (j e) -> p j e", j=2)
                    dst = some(lg, b * 2, 2)[:, :, 0:ne]
                    if l == 0:
                        V.tensor_copy(dst, bk).then_inc(m["lg"], 1)
                        V.tensor_copy(some(vall, b * 2, 2), bank[2 + u][:, S:2 * S].rearrange("p (j d) -> p j d", j=2)
                                      ).then_inc(m["v"], 1)
                    else:
                        V.tensor_tensor(dst, bk, mid(rb2_bc[:, :], 2), ALU.add).then_inc(m["lg"], 1)

                if l == 0:
                    staged(dve, [(normalise, 0), (logits, 3), (split, 3)])
                else:
                    staged(dve, [(normalise, 0), (transposed, 1), (logits, 3)])

            def route(l, ne, nj, wcat_rows=P):
                r = rou[l]
                n = T * ne
                v3 = lambda t: t[:, 0:n].rearrange("p (t e) -> p t e", e=ne)
                logit = lg[:, :, 0:ne]
                e0, e1, e2, e3 = (v3(x_) for x_ in rt)
                hots = [v3(h) for h in hot]
                dve.wait_ge(pre[l]["lg"], NB + 2)
                st.link(V.reduce_max(tmpa[:, :], logit, AX.X))
                V.tensor_tensor(e0, logit, over(tmpa[:, :], ne), ALU.subtract).then_inc(r["lgx"], 1)
                dve.wait_ge(r["exped"], 1)
                st.link(V.reduce_sum(tmpb[:, :], e0, AX.X))
                st.link(V.reciprocal(tmpb[:, :], tmpb[:, :]))
                st.link(V.tensor_tensor(e0, e0, over(tmpb[:, :], ne), ALU.mult))
                eb = mid(eidx[:, E0 - ne:E0], T)
                for k in range(TOPK):
                    src = logit if k == 0 else e1
                    if k:
                        st.link(V.scalar_tensor_tensor(e1.rearrange("p t e -> p (t e)"), hot[0][:, 0:n], OFF,
                                                       rt[3][:, 0:n], ALU.mult, ALU.add))
                        st.link(V.reduce_max(tmpa[:, :], e1, AX.X))
                    else:
                        st.did(V.tensor_copy(e3, logit))
                    st.link(V.tensor_tensor(e2, src, over(tmpa[:, :], ne), ALU.is_equal))
                    st.link(V.tensor_tensor(e2, e2, eb, ALU.mult))
                    st.link(V.tensor_reduce(tmpb[:, :], e2, AX.X, ALU.min))
                    st.link(V.tensor_tensor(hots[k], eb, over(tmpb[:, :], ne), ALU.is_equal))
                    st.link(V.tensor_tensor(e2, e0, hots[k], ALU.mult))
                    st.link(V.reduce_sum(pk[k][:, :], e2, AX.X))
                V.tensor_tensor(rt[3][:, 0:n], hot[0][:, 0:n], hot[1][:, 0:n], ALU.add).then_inc(r["A"], 1)
                if l == 0:
                    st.link(V.tensor_tensor(tmpa[:, :], pk[0][:, :], pk[1][:, :], ALU.add))
                    st.link(V.reciprocal(tmpa[:, :], tmpa[:, :]))
                    for k in range(TOPK):
                        st.did(V.tensor_tensor(wk[k][:, :], pk[k][:, :], tmpa[:, :], ALU.mult))
                else:
                    for k in range(TOPK):
                        st.did(V.tensor_copy(wk[k][:, :], pk[k][:, :]))
                dve.wait_ge(r["cum"], 1)
                et_ = lambda t: t[:, 0:n].rearrange("p (e t) -> p e t", t=T)
                st.link(V.tensor_copy(et_(rt[1]), bank[1][:, 0:n].rearrange("p (t e) -> p e t", e=ne)))
                st.link(V.memset(rt[2][:, 0:n], 1.0))
                st.link(V.tensor_tensor_scan(rt[0][:, 0:n], rt[2][:, 0:n], rt[1][:, 0:n], 0.0, ALU.mult, ALU.add))
                st.link(V.tensor_tensor(rt[1][:, 0:n], rt[0][:, 0:n], rt[1][:, 0:n], ALU.subtract))
                first = et_(rt[1])[:, :, 0]
                cnt, tend, tmp, off = (e[:, 0:ne] for e in ecnt)
                st.link(V.tensor_tensor(cnt, et_(rt[0])[:, :, T - 1], first, ALU.subtract))
                st.link(V.tensor_scalar(ecnti[:, 0:ne], cnt, float(TS - 1), None, ALU.add))
                st.link(V.tensor_scalar(ecnti[:, 0:ne], ecnti[:, 0:ne], TS.bit_length() - 1, None, ALU.logical_shift_right))
                st.link(V.tensor_copy(cnt, ecnti[:, 0:ne]))
                st.link(V.tensor_tensor_scan(tend, rt[2][:, 0:ne], cnt, 0.0, ALU.mult, ALU.add))
                st.link(V.tensor_tensor(tmp, tend, cnt, ALU.subtract))
                st.link(V.scalar_tensor_tensor(off, tmp, float(TS), first, ALU.mult, ALU.subtract))
                st.link(V.tensor_tensor(e2, v3(bank[0]), et_(rt[1]).rearrange("p e t -> p t e"), ALU.add))
                st.link(V.tensor_tensor(e2, e2, mid(off, T), ALU.add))
                for k in range(TOPK):
                    st.link(V.tensor_tensor(e0, e2, hots[k], ALU.mult))
                    st.link(V.reduce_sum(slotf[k][:, :], e0, AX.X))
                    st.did(V.tensor_copy(sloti[k][:, :], slotf[k][:, :]))
                ej = ejm[:, 0:nj * ne].rearrange("p (j e) -> p j e", e=ne)
                st.link(V.tensor_tensor(ej, mid(tend, nj), over(jidx[:, 0:nj], ne), ALU.is_le))
                st.link(V.reduce_sum(ejf[:, 0:nj], ej, AX.X))
                st.link(V.tensor_scalar(ejf[:, 0:nj], ejf[:, 0:nj], float(ne - 1), float(P), ALU.min, ALU.mult))
                V.tensor_scalar(widx[:, 0:nj], ejf[:, 0:nj], pidx[:, :], None, ALU.add).then_inc(r["routed"], 1)

            dve.wait_ge(s_relb, 16)
            lo, hi = S - 1 - MAXREL, S + MAXREL
            V.tensor_copy(ext_sb[:, 0:lo], ext_sb[:, lo:lo + 1].broadcast_to([H0, lo])).then_inc(s_edge, 1)
            V.tensor_copy(ext_sb[:, hi:EXT], ext_sb[:, hi - 1:hi].broadcast_to([H0, EXT - hi])).then_inc(s_edge, 1)
            dve.wait_ge(s_edge, 2)
            es = ext_sb[:, :]
            V.tensor_copy(extr_sb[:, :], bass.AP(tensor=es.tensor, offset=es.offset + EXT - 1, ap=[list(es.ap)[0], [-1, EXT]])
                          ).then_inc(s_edge, 1)
            for q in range(4):
                dve.wait_ge(s_x, 64)
                take_stats(lambda t: x_sb[:, t, :], q)
            finish_stats()
            dve.wait_ge(s_w, 16 * NW)
            st.did(V.tensor_scalar(bqs_c, bq_c, QSCALE, None, ALU.mult))
            V.tensor_scalar(wqk1_sb[:, :], wqk1_sb[:, :], nw_c, None, ALU.mult).then_inc(s_wf, 1)
            pre_dve(0, E0)
            dve.wait_ge(s_c, 11)
            dve.wait_ge(pre[0]["sh"], NB + 2)
            for i in (4, 5):
                V.memset(bank[i][:, :], 0.0).then_inc(A0["init"], 1)
            route(0, E0, NJ0)

            a = A0
            dve.wait_ge(s_bt, 16)

            def reduce_maxima(n, i):
                t, qt = i // 2, i % 2
                dve.wait_ge(a["A"], n * 16 + (i + 1))
                if i % 8 == 0:
                    dve.wait_ge(a["mT"], n * 2 + (i // 8 + 1))
                V.tensor_reduce(nmax[:, qt, 2 * t:2 * t + 2], bank[i % 2][:, :].rearrange("p (h k) -> p h k", h=2),
                                AX.X, ALU.max, negate=True).then_inc(a["Ared"], 1)

            def add_bias(b, h):
                dve.wait_ge(a["B"], b * 16 + (h + 33))
                dve.wait_ge(a["E"], b * 16 + (h + 1))
                bt = biasT[:, h, :]
                V.tensor_tensor(scores[h % 2].rearrange("p (j q) -> p j q", j=2),
                                bank[2 + h % 2][:, :].rearrange("p (j q) -> p j q", j=2),
                                bass.AP(tensor=bt.tensor, offset=bt.offset + S - 1, ap=[list(bt.ap)[0], [P, 2], [-1, S]]),
                                ALU.add).then_inc(a["S"], 1)

            def normalise_outputs(b):
                for q in range(2):
                    dve.wait_ge(a["To"], b * 2 + (q + 1))
                    o = bank[6 + q][:, :].rearrange("p (h c) -> p h c", c=32)
                    V.reciprocal(rden[:, q, :], o[:, :, DK]).then_inc(a["s2"], 1)
                for q in range(2):
                    dve.wait_ge(a["s2"], b * 2 + (q + 1))
                    o = bank[6 + q][:, :].rearrange("p (h c) -> p h c", c=32)
                    V.tensor_tensor(on[:, q, :].rearrange("p (h d) -> p h d", d=DK), o[:, :, 0:DK],
                                    over(rden[:, q, :], DK), ALU.mult).then_inc(a["on"], 1)

            def keep_result(b):
                dve.wait_ge(a["wo"], b + 1)
                dst = s_sb[:, 2 * b:2 * b + 2, :] if isinstance(b, int) else s_sb[:, bass.ds(b * 2, 2), :]
                V.tensor_tensor(dst, bank[7][:, 0:2 * D].rearrange("p (q d) -> p q d", q=2), mid(bo_bc[:, :], 2),
                                ALU.add).then_inc(a["s"], 1)

            def attend_dve(b, first=False, ahead=True):
                for h in range(H0):
                    add_bias(b, h)
                    if ahead:
                        reduce_maxima(b + 1, h)
                    if h == 5 and not first:
                        normalise_outputs(b - 1)
                    elif h == 11 and not first:
                        keep_result(b - 1)

            for i in range(H0):
                reduce_maxima(0, i)
            attend_dve(0, first=True)
            with dve.Fori(0, NB // 2 - 1) as it:
                attend_dve(it * 2 + 1)
                attend_dve(it * 2 + 2)
            attend_dve(NB - 1, ahead=False)
            normalise_outputs(NB - 1)
            keep_result(NB - 1)

            def experts(l, nj):
                m = moe[l]

                def copy_rows(j, v, half):
                    u = v % 2
                    dve.wait_ge(m["T"], j + 3)
                    dve.wait_ge(m["up"], j * 2 + 2)
                    V.tensor_copy(xT[u][:, :], bank[u][:, 0:2 * P]).then_inc(m["xT"], 1)
                    if not isinstance(j, int) or j >= NWB:
                        dve.wait_ge(m[f"stored{u}"], half * 32 - 32)
                    V.tensor_tensor(yid[v], xg[u][:, :, D], spare[:, j * 2:j * 2 + 2] if isinstance(j, int) else
                                    spare[:, bass.ds(j * 2, 2)], ALU.min)
                    V.tensor_copy(yw[v], xg[u][:, :, D + 1]).then_inc(m["ids"], 1)

                def outputs(j, v, half):
                    u = v % 2
                    dve.wait_ge(m["down"], j + 3)
                    if not isinstance(j, int) or j >= 2:
                        dve.wait_ge(m[f"stored{u}"], half * 32)
                    V.tensor_tensor(yb[u], bank[6 + u][:, 0:2 * D].rearrange("p (s d) -> p s d", s=2),
                                    mid(wb[v][:, WROW - D:WROW], 2), ALU.add).then_inc(m["yb"], 1)
                    dve.wait_ge(m["yb"], j + 1)
                    V.tensor_tensor(yb[u], yb[u], over(yw[v], D), ALU.mult).then_inc(m["y"], 1)

                copy_rows(0, 0, 0)
                copy_rows(1, 1, 0)
                for j in range(NWB):
                    copy_rows(j + 2, (j + 2) % NWB, (j + 2) // 2)
                    outputs(j, j, j // 2)
                with dve.Fori(1, nj // NWB - 1) as it:
                    for v in range(NWB):
                        copy_rows(it * NWB + (v + 2), (v + 2) % NWB, it * 2 + (v + 2) // 2)
                        outputs(it * NWB + v, v, it * 2 + v // 2)
                for j in range(nj - NWB, nj):
                    if j + 2 < nj:
                        copy_rows(j + 2, (j + 2) % NWB, (j + 2) // 2)
                    outputs(j, j % NWB, j // 2)

            def add_choices(l, q):
                dve.wait_ge(com[l][f"g{q}"], 16 * TOPK)
                y0, y1 = (yy[:, k, q * 8:q * 8 + 8, :] for k in range(TOPK))
                return V.tensor_tensor(y0, y0, y1, ALU.add)

            experts(0, NJ0)
            dve.wait_ge(pre[0]["shg"], 1)
            for q in range(4):
                z, sh = yy[:, 0, q * 8:q * 8 + 8, :], sh_sb[:, q * 8:q * 8 + 8, :]
                st.link(add_choices(0, q))
                st.link(V.scalar_tensor_tensor(z, sh, 0.5, z, ALU.mult, ALU.add))
                take_stats(lambda t: yy[:, 0, t, :], q)
            finish_stats()
            for q in range(4):
                for t in range(q * 8, q * 8 + 8):
                    st.did(V.tensor_scalar(yy[:, 0, t, :], yy[:, 0, t, :], mean[:, t:t + 1], rstd[:, t:t + 1],
                                           ALU.subtract, ALU.mult))
                st.sync()
                z = yy[:, 0, q * 8:q * 8 + 8, :]
                st.link(V.tensor_tensor(z, z, mid(gamma_bc[:, :], 8), ALU.mult))
                V.tensor_tensor(z, z, mid(beta_bc[:, :], 8), ALU.add).then_inc(com[0]["z"], 1)
            dve.wait_ge(s_x2, 16)
            for q in range(4):
                z, r_, s_ = (b_[:, q * 8:q * 8 + 8, :] for b_ in (yy[:, 0], xres, s_sb))
                dve.wait_ge(com[0]["silu"], q + 1)
                st.link(V.tensor_tensor(z, z, s_, ALU.mult))
                st.link(V.tensor_tensor(r_, r_, z, ALU.add))
                take_stats(lambda t: xres[:, t, :], q)
            finish_stats()
            st.link(V.tensor_tensor(tmpa[:, :], rstd[:, :], rstd[:, :], ALU.mult))
            st.link(V.tensor_tensor(tmpa[:, :], tmpa[:, :], var[:, :], ALU.mult))
            st.link(V.tensor_scalar(var[:, :], tmpa[:, :], RMS_EPS, None, ALU.add))
            rsqrt(rrms[:, :], var[:, :], tmpa[:, :], tmpb[:, :])
            pre_dve(1, E1)
            route(1, E1, NJ1)

            a = A1
            xn1 = xn_sb[1]
            dve.wait_ge(pre[1]["xs_saved"], NB)
            dve.wait_ge(s_act, 1)

            def scale_rows(b, u, name, used):
                dve.wait_ge(a[used], b + 1)
                for j in range(2):
                    t = b * 2 + j
                    last = V.tensor_scalar(x2[u][:, j, :], one(xn1, t)[:, 0:D] if isinstance(t, int) else
                                           xn1[:, bass.ds(t, 1), 0:D].rearrange("p o d -> p (o d)"),
                                           some(rrms, t, 1), None, ALU.mult)
                last.then_inc(a[name], 1)

            def products(b, u, turn):
                dve.wait_ge(a["U"], b + 3)
                dve.wait_ge(a["nn"], b + 1)
                V.tensor_copy(one(uu, b), bank[2 + u][:, 0:D])
                V.tensor_tensor(pr[u], bank[2 + u][:, 0:2 * D], wqk1_sb[:, :], ALU.mult).then_inc(a["pr"], 1)

            def keep_norms(b, u, turn):
                dve.wait_ge(a["nn"], b + 3)
                V.tensor_copy(one(nsq, b), bank[4 + u][:, 0:2]).then_inc(a["nns"], 1)

            staged(dve, [(lambda b, u, turn: scale_rows(b, u, "x2", "C"), 0), (products, 2), (keep_norms, 3)])
            dve.wait_ge(a["nns"], NB + 2)
            nf, rf = nsq.rearrange("p b k -> p (b k)"), rin.rearrange("p b k -> p (b k)")
            st.link(V.tensor_scalar(nf, nf, 1e-24, None, ALU.max))
            rsqrt(rf, nf, nt1, nt2)
            st.link(V.tensor_scalar(rin[:, :, 0], rin[:, :, 0], et_c, None, ALU.mult))

            def inverse_norm(b, k):
                return rin[:, b, k:k + 1] if isinstance(b, int) else rin[:, bass.ds(b, 1), k]

            def scale_by_keys(b, u, turn):
                dve.wait_ge(a["G"], b + 1)
                dve.wait_ge(a["GT"], b + 1)
                V.tensor_scalar(gk[u], bank[2 + u][:, 0:D], inverse_norm(b, 1), None, ALU.mult).then_inc(a["gk"], 1)

            def scale_by_queries(b, u, turn):
                dve.wait_ge(a["GT"], b + 3)
                dve.wait_ge(a["exp"], b + 1)
                V.scalar_tensor_tensor(gm[u], bank[4 + u][:, 0:P], inverse_norm(b, 0), blockm[:, :], ALU.mult,
                                       ALU.add).then_inc(a["gm"], 1)
                dve.wait_ge(a["gm"], b + 3)
                V.tensor_reduce(nm1[u], gm[u], AX.X, ALU.max, negate=True).then_inc(a["mx"], 1)

            def normalise_weights(b, u, turn):
                dve.wait_ge(a["exp"], b + 3)
                V.reciprocal(rs1[u], sm1[u]).then_inc(a["rs"], 1)
                dve.wait_ge(a["rs"], b + 1)
                dve.wait_ge(a["M"], b + 1)
                V.tensor_scalar(an[u], at1[u], rs1[u], None, ALU.mult).then_inc(a["an"], 1)

            def keep_result1(b, u, turn):
                dve.wait_ge(a["F"], b + 3)
                V.tensor_copy(some(s_sb, b * 2, 2), bank[7][:, 0:2 * D].rearrange("p (j d) -> p j d", j=2)
                              ).then_inc(a["s"], 1)

            staged(dve, [(scale_by_keys, 0), (scale_by_queries, 1), (normalise_weights, 2),
                         (lambda b, u, turn: scale_rows(b, u, "x2b", "T"), 3), (keep_result1, 5)])
            experts(1, NJ1)
            for q in range(4):
                add_choices(1, q).then_inc(com[1]["z"], 1)
            for q in range(4):
                z, r_, s_ = (b_[:, q * 8:q * 8 + 8, :] for b_ in (yy[:, 0], xres, s_sb))
                dve.wait_ge(com[1]["silu"], q + 1)
                st.link(V.tensor_tensor(z, z, s_, ALU.mult))
                V.tensor_tensor(z, r_, z, ALU.add).then_inc(com[1]["x1"], 1)


def kernel(**inputs):
    import numpy as _np
    import concourse.bacc as _bacc
    from concourse import mybir as _mybir
    from concourse.bass_utils import run_bass_kernel_spmd as _run

    i = {k: _np.asarray(v) for k, v in inputs.items()}

    def column(v, chunks=1):
        return v.reshape(chunks, P).T

    def expert_rows(w1, b1, w2, b2):
        e = w1.shape[0]
        w2r = w2.reshape(e, HC, P, D).transpose(0, 2, 1, 3).reshape(e, P, HC * D)
        b1r = b1.reshape(e, HC, P).transpose(0, 2, 1)
        b2r = _np.repeat(b2[:, None, :], P, axis=1)
        return _np.concatenate([w1, w2r, b1r, b2r], axis=2).reshape(e * P, WROW)

    wqkv = i["L1_attn_w_qkv"]
    host = [
        ("x", i["L0_attn_x"].reshape(TOK, D)),
        ("wqT", i["L0_attn_Wq"].T), ("wkT", i["L0_attn_Wk"].T), ("wvT", i["L0_attn_Wv"].T), ("woT", i["L0_attn_Wo"].T),
        ("bq", column(i["L0_attn_bq"])), ("bk", column(i["L0_attn_bk"])), ("bv", column(i["L0_attn_bv"])),
        ("bo", i["L0_attn_bo"]), ("relb", i["L0_attn_rel_bias"]),
        ("wcat0", expert_rows(i["L0_ffn_W1"], i["L0_ffn_b1"], i["L0_ffn_W2"], i["L0_ffn_b2"])),
        ("gate", i["L0_ffn_gate_W"]), ("shw", i["L0_ffn_shared_W"]), ("shb", i["L0_ffn_shared_b"]),
        ("gamma", i["L0_ffn_gamma"]), ("beta", i["L0_ffn_beta"]),
        ("nw", column(i["L1_attn_norm_weight"])), ("wqkT1", wqkv[0:2 * D].T), ("wv1", wqkv[2 * D:]),
        ("woT1", i["L1_attn_w_out"].T), ("temp", _np.repeat(i["L1_attn_temperature"].reshape(H1), DH1)[:, None]),
        ("rw1", i["L1_ffn_rW1"]), ("rb1", column(i["L1_ffn_rb1"], 2)),
        ("rw2", i["L1_ffn_rW2"].reshape(2, P, E1).transpose(1, 0, 2)), ("rb2", i["L1_ffn_rb2"]),
        ("wcat1", expert_rows(i["L1_ffn_We1"], i["L1_ffn_be1"], i["L1_ffn_We2"], i["L1_ffn_be2"])),
    ]
    nc = _bacc.Bacc("TRN2", target_bir_lowering=False, num_devices=1)
    arrays, args = {}, []
    for name, a in host:
        a = _np.ascontiguousarray(a)
        arrays[f"in_{name}"] = a
        args.append(nc.dram_tensor(f"in_{name}", a.shape, _mybir.dt.from_np(a.dtype), kind="ExternalInput").ap())
    args.append(nc.dram_tensor("out_x", (TOK, D), _mybir.dt.float32, kind="ExternalOutput").ap())
    build(nc, *args)
    r = _run(nc, [arrays], core_ids=[0])
    return r.results[0]["out_x"].reshape(NB, S, D)
```

```python
import concourse.bass as bass
from concourse import mybir
from contextlib import ExitStack

NB, S, D = 16, 256, 128
P = 128
T = NB * S // P
H0, DK = 16, 8
MAXREL = 128
NREL = 2 * MAXREL + 1
E0, E1, HID = 8, 4, 512
HC = HID // P
H1, DH1 = 8, 16
TS = 256
TOPK = 2
NSC = 4
NWB = 4
XW = D + 2
TOK = NB * S
EROWS = 4
NOWHERE = 1e6


def tiles_for(experts):
    n = (TOK * TOPK - experts) // TS + experts
    return -(-n // NWB) * NWB


NJ0, NJ1 = tiles_for(E0), tiles_for(E1)
NSLOT = max(NJ0, NJ1) * TS
WROW = HID + HC * D + HC + D
EXT = 2 * S - 1
RUNS = ((0, 0, 3), (1, 0, 2), (2, 0, 1))
TERMS = sum(n for _, _, n in RUNS)
STK = (TERMS + 1) * DK
STORES = 2 * len(RUNS)
HALF = P // 2
BW = S + P
PACK = (2 * D, D, D, E0, D, 2 * D, D, D, 2 * D, 2, 2 * E1, 5)
WPACK = sum(PACK)
VECTORS = 3 * D + E1
LN_EPS, RMS_EPS = 1e-5, 1e-6
QSCALE = float(DK) ** -0.5
OFF = -1e30


class Steps:

    def __init__(self, eng, sem):
        self.eng, self.sem, self.k = eng, sem, 0

    def did(self, ins):
        self.k += 1
        return ins.then_inc(self.sem, 1)

    def sync(self):
        self.eng.wait_ge(self.sem, self.k)

    def link(self, ins):
        self.did(ins)
        self.sync()


def staged(eng, stages):
    head = 2 * -(-max(lag for _, lag in stages) // 2)

    def peeled(i):
        for stage, lag in stages:
            if 0 <= i - lag < NB:
                stage(i - lag, (i - lag) % 2, (i - lag) // 2)

    for i in range(head):
        peeled(i)
    with eng.Fori(0, (NB - head) // 2) as it:
        for v in range(2):
            for stage, lag in stages:
                at = head + v - lag
                stage(it * 2 + at, at % 2, it + at // 2)
    for i in range(NB, NB + max(lag for _, lag in stages)):
        peeled(i)


def some(ap, at, n):
    return ap[:, at:at + n] if isinstance(at, int) else ap[:, bass.ds(at, n)]


def one(ap, at):
    return ap[:, at, :] if isinstance(at, int) else ap[:, bass.ds(at, 1), :].rearrange("p o d -> p (o d)")


def over(ap, n):
    return bass.AP(tensor=ap.tensor, offset=ap.offset, ap=list(ap.ap) + [[0, n]])


def mid(ap, n):
    a = list(ap.ap)
    return bass.AP(tensor=ap.tensor, offset=ap.offset, ap=[a[0], [0, n]] + a[1:])


def build(nc, x, wpack, vectors, shb, relb, wcat0, wcat1, out):
    fp32, bf16, i32, u32 = mybir.dt.float32, mybir.dt.bfloat16, mybir.dt.int32, mybir.dt.uint32
    ALU, ACT, AX = mybir.AluOpType, mybir.ActivationFunctionType, mybir.AxisListType

    ext_dram = nc.dram_tensor("ext_dram", [2, H0, EXT], fp32, kind="Internal").ap()
    stk_dram = nc.dram_tensor("stk_dram", [2, NB * D, TERMS + 1, S], bf16, kind="Internal").ap()
    xg_dram = [nc.dram_tensor(f"xg_dram{l}", [(NJ0, NJ1)[l] * TS, XW], fp32, kind="Internal").ap() for l in range(2)]
    yg_dram = [nc.dram_tensor(f"yg_dram{l}", [TOPK * TOK + (NJ0, NJ1)[l] * TS, D], fp32, kind="Internal").ap()
               for l in range(2)]

    ctx = ExitStack()
    with ctx:
        def sb(name, shape, dt=fp32):
            return ctx.enter_context(nc.sbuf_tensor(name, shape, dt))

        def sem(name):
            return ctx.enter_context(nc.semaphore(name))

        bufA = sb("bufA", [P, T, D])
        bufB, bufC = (sb(f"buf{c}", [P, T, XW]) for c in "BC")
        yy = sb("yy", [P, TOPK, T, D])
        x_sb = s_sb = bufA
        xres = bufB[:, :, 0:D]
        sh_sb = bufC[:, :, 0:D]
        xn_sb = (bufB, bufC)
        yyf = yy[:, :, :, :].rearrange("p k t d -> p (k t d)")
        vall = yyf[:, 0:TOK].rearrange("p (t d) -> p t d", d=D)
        biasT = sb("biasT", [P, H0, BW])
        biasA = sb("biasA", [P, H0, BW], bf16)
        packed = sb("packed", [P, WPACK])
        at = 0
        parts = []
        for n in PACK:
            parts.append(packed[:, at:at + n])
            at += n
        wqk_sb, wv_sb, wo_sb, gate_sb, shw_sb, wqk1_sb, wv1_sb, wo1_sb, rw1_sb, rb1_sb, rw2_sb, cols = parts
        rw2_sb = rw2_sb.rearrange("p (c e) -> p c e", c=2)
        vec = sb("vec", [P, VECTORS])
        bo_bc, gamma_bc, beta_bc = (vec[:, i * D:(i + 1) * D] for i in range(3))
        rb2_bc = vec[:, 3 * D:VECTORS]
        shb_sb = sb("shb_sb", [1, D])
        more = sb("more", [P, 2])
        ext_sb = sb("ext_sb", [H0, EXT])
        extr_sb = sb("extr_sb", [H0, EXT])
        empty = sb("empty", [P, EROWS * XW])
        fill = sb("fill", [P, 2 * S], bf16)
        ident = sb("ident", [P, P])
        identb = sb("identb", [P, P], bf16)
        below = sb("below", [P, P])
        ones = sb("ones", [P, P])
        blockm = sb("blockm", [P, P])
        eidx = sb("eidx", [P, E0])
        jidx = sb("jidx", [P, NSLOT // TS])
        pidx = sb("pidx", [P, 1])
        spare = sb("spare", [P, NSLOT // P])
        toki, tokf = sb("toki", [P, T], i32), sb("tokf", [P, T])
        stats = sb("stats", [P, T, 6])
        mean = sb("mean", [P, T])
        rstd = sb("rstd", [P, T])
        rrms = sb("rrms", [P, T])
        var = sb("var", [P, T])
        tmpa = sb("tmpa", [P, T])
        tmpb = sb("tmpb", [P, T])
        lg = sb("lg", [P, T, E0])
        rt = [sb(f"rt{i}", [P, T * E0]) for i in range(4)]
        hot = [sb(f"hot{k}", [P, T * E0]) for k in range(TOPK)]
        pk = [sb(f"pk{k}", [P, T]) for k in range(TOPK)]
        wk = [sb(f"wk{k}", [P, T]) for k in range(TOPK)]
        slotf = [sb(f"slotf{k}", [P, T]) for k in range(TOPK)]
        sloti = [sb(f"sloti{k}", [P, T], i32) for k in range(TOPK)]
        ecnt = [sb(f"ecnt{i}", [P, E0]) for i in range(4)]
        ecnti = sb("ecnti", [P, E0], i32)
        ejm = sb("ejm", [P, NSLOT // TS * E0])
        ejf = sb("ejf", [P, NSLOT // TS])
        widx = sb("widx", [P, NSLOT // TS], i32)
        xs = [sb(f"xs{u}", [P, 2, D]) for u in range(2)]
        xT = [sb(f"xT{u}", [P, 2 * P]) for u in range(2)]
        rh = [sb(f"rh{u}", [P, 2, 2 * P]) for u in range(2)]
        work = sb("work", [P, 13312])

        def carve():
            at = [0]

            def take(n, dt=fp32):
                words = n if dt == fp32 else n // 2
                a = work[:, at[0]:at[0] + words]
                at[0] += words
                assert at[0] <= 13312, at
                return a if dt == fp32 else a.bitcast(dt)
            return take

        take = carve()
        qst = [take(H0 // 2 * S, bf16).rearrange("p (t s) -> p t s", s=S) for _ in range(2)]
        kst = [take(H0 * S, bf16).rearrange("p (t e s) -> p t e s", e=2, s=S) for _ in range(2)]
        strip = work[:, 0:H0 * BW].rearrange("p (h u) -> p h u", h=H0)
        vaug = [take(2 * H0 * (DK + 1)).rearrange("p (k h c) -> p k h c", k=2, h=H0) for _ in range(2)]
        nmax = take(2 * H0, bf16).rearrange("p (q h) -> p q h", q=2)
        nmaxT = [take(S, bf16) for _ in range(2)]
        scores = [take(2 * S) for _ in range(NSC)]
        probs = [take(2 * S) for _ in range(NSC)]
        oT = take(4 * S).rearrange("p (g s) -> p g s", g=4)
        on = take(2 * D).rearrange("p (q d) -> p q d", q=2)
        onT = take(2 * P)
        rden = take(2 * H0).rearrange("p (q h) -> p q h", q=2)
        qkf, qkr = scores[0:2], scores[2]
        pieces = [yyf[:, TOK + u * 3 * S:TOK + (u + 1) * 3 * S].bitcast(bf16).rearrange("p (c s) -> p c s", c=3)
                  for u in range(2)]
        take = carve()
        wb = [take(WROW) for _ in range(NWB)]
        xg = [take(2 * XW).rearrange("p (s w) -> p s w", s=2) for _ in range(2)]
        hb = [take(HC * TS).rearrange("p (c s) -> p c s", c=HC) for _ in range(2)]
        yb = [take(2 * D).rearrange("p (s d) -> p s d", s=2) for _ in range(2)]
        yid = [take(2).bitcast(i32) for _ in range(NWB)]
        yw = [take(2) for _ in range(NWB)]
        take = carve()
        cc = [take(D) for _ in range(2)]
        uu = take(NB * D).rearrange("p (b o) -> p b o", b=NB)
        pr = [take(2 * D) for _ in range(2)]
        x2 = [take(2 * D).rearrange("p (j d) -> p j d", j=2) for _ in range(2)]
        x2T = [take(2 * P) for _ in range(2)]
        nsq = take(2 * NB).rearrange("p (b k) -> p b k", b=NB)
        rin = take(2 * NB).rearrange("p (b k) -> p b k", b=NB)
        nt1, nt2 = take(2 * NB), take(2 * NB)
        gk = [take(D) for _ in range(2)]
        gm = [take(D) for _ in range(2)]
        at1 = [take(D) for _ in range(2)]
        an = [take(D) for _ in range(2)]
        ms = [take(D) for _ in range(2)]
        ps_ = [take(D) for _ in range(2)]
        nm1 = [take(1) for _ in range(2)]
        sm1 = [take(1) for _ in range(2)]
        rs1 = [take(1) for _ in range(2)]

        bank = [ctx.enter_context(nc.psum_tensor(f"bank{i}", [P, 512], fp32)) for i in range(8)]

        bq_c, bk_c, bv_c, nw_c, temp_c = (cols[:, i:i + 1] for i in range(5))
        bqs_c, et_c = (more[:, i:i + 1] for i in range(2))

        s_x = [sem(f"x{q}_loaded") for q in range(4)]
        s_w, s_wf = sem("weights_loaded"), sem("weights_folded")
        s_c, s_cc = sem("constants_made"), sem("constant_steps")
        s_relb, s_edge, s_extd, s_strip = sem("relb_loaded"), sem("edges_filled"), sem("ext_stored"), sem("strip_loaded")
        s_bt, s_ba, s_stk0 = sem("biasT_loaded"), sem("biasA_made"), sem("stacks_zeroed")
        s_zero, s_fill = sem("zero_made"), sem("last_rows_stored")
        s_xgz = [sem(f"xg{l}_emptied") for l in range(2)]
        s_dve, s_pool, s_act = sem("dve_steps"), sem("pool_steps"), sem("act_steps")

        block = ctx.enter_context(nc.Block())

        def phase_sems(phase, l, names):
            return {n: sem(f"{phase}{l}_{n}") for n in names.split()}

        pre = [phase_sems("pre", 0, "xs xs_saved T xT gs lg sh shg qkv qkf v split pieces stored0 stored1"),
               phase_sems("pre", 1, "xs xs_saved T xT gs lg rh1 rhs")]
        rou = [phase_sems("route", l, "lgx exped A cum routed scattered") for l in range(2)]
        moe = [phase_sems("experts", l, "W0 W1 W2 W3 xg0 xg1 T xT up gelu down yb y ids stored0 stored1")
               for l in range(2)]
        com = [phase_sems("combine", 0, "g0 g1 g2 g3 stats normed z silu"),
               phase_sems("combine", 1, "g0 g1 g2 g3 z silu x1")]
        s_out, s_x2 = sem("out_stored"), sem("x_back")
        A0 = phase_sems("attend", 0, "init stk00 stk01 stk10 stk11 v_sb A Ared mT nmT M0 M1 B S E PV oTs To on Tn onT wo s s2")
        A1 = phase_sems("attend", 1, "x2 C Cs U pr nn nns x2b T x2T G gk GT gm mx exp rs an M Ms Pm Ps F s")

        NW = 3
        NEMPTY = [nj * TS // (P * EROWS) for nj in (NJ0, NJ1)]

        @block.sync
        def _(sp):
            sp.dma_start(ext_sb[:, S - 1 - MAXREL:S + MAXREL], relb).then_inc(s_relb, 16)
            xv = x.rearrange("(t p) d -> p t d", p=P)
            for c in range(4):
                sp.dma_start(x_sb[:, c * 8:c * 8 + 8, :], xv[:, c * 8:c * 8 + 8, :]).then_inc(s_x[c], 16)
            for dst, src in ((packed[:, :], wpack), (vec[:, :], vectors.partition_broadcast(P)),
                             (shb_sb[:, :], shb.unsqueeze(0))):
                sp.dma_start(dst, src).then_inc(s_w, 16)
            sp.wait_ge(s_edge, 3)
            sp.dma_start(ext_dram[0], ext_sb[:, :]).then_inc(s_extd, 16)
            sp.dma_start(ext_dram[1], extr_sb[:, :]).then_inc(s_extd, 16)
            sp.wait_ge(s_extd, 32)
            sp.dma_start(strip, bass.AP(tensor=ext_dram.tensor, offset=0, ap=[[1, P], [EXT, H0], [1, BW]])
                         ).then_inc(s_strip, 16)

            def store_empty(l):
                xe = xg_dram[l].rearrange("(c p r) w -> c p (r w)", p=P, r=EROWS)
                for c in range(NEMPTY[l]):
                    sp.dma_start(xe[c], empty[:, :]).then_inc(s_xgz[l], 16)

            sp.wait_ge(s_zero, 2)
            for i in range(2):
                sp.dma_start(stk_dram[i].rearrange("(p c) r s -> p c r s", p=P)[:, :, TERMS, :],
                             mid(fill[:, i * S:(i + 1) * S], NB)).then_inc(s_fill, 16)
            with sp.Fori(0, NB // 2) as it:
                for u in range(2):
                    b = it * 2 + u
                    sp.wait_ge(pre[0]["pieces"], b + 1)
                    for i in range(2):
                        r = 0
                        for qp, kp, n in RUNS:
                            dst = stk_dram[i, bass.ds(b * D, D), r:r + n, :]
                            src = pieces[u][:, kp:kp + n, S:2 * S] if i else bass.AP(
                                tensor=pieces[u].tensor, offset=pieces[u].offset + qp * 2 * S,
                                ap=[list(pieces[u].ap)[0], [0, n], [1, S]])
                            sp.dma_start(dst, src).then_inc(pre[0][f"stored{u}"], 16)
                            r += n
            sp.dma_start(biasT[:, :, :], bass.AP(tensor=ext_dram.tensor, offset=H0 * EXT, ap=[[1, P], [EXT, H0], [1, BW]])
                         ).then_inc(s_bt, 16)
            for u in range(2):
                sp.wait_ge(pre[0][f"stored{u}"], (NB // 2 + 1) * STORES * 16)
            sp.wait_ge(s_stk0, 1)
            sp.wait_ge(s_fill, 32)

            def load_stacks(b, u, g):
                for e in range(2):
                    rows = slice(e * HALF, e * HALF + STK)
                    ts = slice(g * 4, g * 4 + 4)

                    def src(i):
                        heads = stk_dram[i, b * D:b * D + D] if isinstance(b, int) else stk_dram[i, bass.ds(b * D, D)]
                        return heads.rearrange("(t e d) r s -> (d r) t e s", e=2, d=DK)[:, ts, e, :]
                    sp.dma_start(qst[u][rows, ts, :], src(0)).then_inc(A0[f"stk{u}{g}"], 16)
                    sp.dma_start(kst[u][rows, ts, e, :], src(1)).then_inc(A0[f"stk{u}{g}"], 16)

            def place_maxima(n, u, g):
                sp.wait_ge(A0["nmT"], n * 2 + (g + 1))
                for e in range(2):
                    sp.dma_start(qst[u][e * HALF + STK - 1:e * HALF + STK, g * 4:g * 4 + 4, :],
                                 nmaxT[g][e:H0 // 2:2, :]).then_inc(A0[f"M{g}"], 16)

            for b in range(2):
                for g in range(2):
                    load_stacks(b, b, g)
            store_empty(0)
            place_maxima(0, 0, 0)
            with sp.Fori(0, NB // 2 - 1) as it:
                for u in range(2):
                    b = it * 2 + u
                    place_maxima(b, u, 1)
                    sp.wait_ge(A0["B"], b * 16 + (32 + 8))
                    load_stacks(b + 2, u, 0)
                    place_maxima(b + 1, 1 - u, 0)
                    sp.wait_ge(A0["B"], b * 16 + (32 + 16))
                    load_stacks(b + 2, u, 1)
            place_maxima(NB - 2, 0, 1)
            place_maxima(NB - 1, 1, 0)
            place_maxima(NB - 1, 1, 1)
            store_empty(1)
            for l, nj in enumerate((NJ0, NJ1)):
                m = moe[l]
                xgv = xg_dram[l].rearrange("(j s p) w -> j p s w", s=2, p=P)
                wcat = (wcat0, wcat1)[l]

                def load(j, v):
                    u = v % 2
                    sp.wait_ge(m["T"], j + 1)
                    sp.wait_ge(m["ids"], j + 1)
                    src = xgv[j] if isinstance(j, int) else xgv[bass.ds(j, 1)].rearrange("o p s w -> p (o s) w")
                    sp.dma_start(xg[u], src).then_inc(m[f"xg{u}"], 16)
                    sp.wait_ge(m["y"], j + 1)
                    at = widx[0:1, j:j + 1] if isinstance(j, int) else widx[0:1, bass.ds(j, 1)]
                    row = sp.value_load(at, min_val=0, max_val=((E0, E1)[l] - 1) * P)
                    sp.dma_start(wb[v], wcat[bass.ds(row, P), :]).then_inc(m[f"W{v}"], 16)

                sp.wait_ge(rou[l]["scattered"], 16 * TOPK * T)
                if l == 0:
                    sp.dma_start(xres, xv).then_inc(s_x2, 16)
                sp.wait_ge((A0, A1)[l]["s"], NB + (2, 1)[l])
                with sp.Fori(0, nj // NWB) as it:
                    for v in range(NWB):
                        load(it * NWB + v, v)
                sp.wait_ge(m["stored0"], 16 * nj)
                sp.wait_ge(m["stored1"], 16 * nj)
                yv = yg_dram[l][0:TOPK * TOK, :].rearrange("(k t p) d -> p k t d", k=TOPK, p=P)
                for q in range(4):
                    for k in range(TOPK):
                        sp.dma_start(yy[:, k, q * 8:q * 8 + 8, :], yv[:, k, q * 8:q * 8 + 8, :]).then_inc(com[l][f"g{q}"], 16)
            ov = out.rearrange("(t p) d -> p t d", p=P)
            for g in range(4):
                sp.wait_ge(com[1]["x1"], g + 1)
                sp.dma_start(ov[:, g * 8:g * 8 + 8, :], yy[:, 0, g * 8:g * 8 + 8, :]).then_inc(s_out, 16)
            sp.wait_ge(s_out, 64)

        @block.gpsimd
        def _(pool):
            g = nc.gpsimd
            st = Steps(pool, s_pool)
            st.did(g.memset(ident[:, :], 0.0))
            st.did(g.memset(below[:, :], 1.0))
            st.did(g.memset(blockm[:, :], 0.0))
            st.did(g.iota(widx[:, 0:E0], pattern=[[1, E0]], base=-E0, channel_multiplier=0))
            st.did(g.iota(ejm[:, 0:NSLOT // TS].bitcast(i32), pattern=[[1, NSLOT // TS]], base=0, channel_multiplier=0))
            st.did(g.iota(sloti[0][:, 0:1], pattern=[[1, 1]], base=0, channel_multiplier=1))
            g.memset(ones[:, :], 1.0).then_inc(s_c, 1)
            st.did(g.memset(empty[:, :], 0.0))
            st.did(g.memset(fill[:, 0:S], 0.0))
            g.memset(fill[:, S:2 * S], 1.0).then_inc(s_zero, 1)
            st.did(g.iota(toki[:, :], pattern=[[P, T]], base=0, channel_multiplier=1))
            st.did(g.iota(ejm[:, P:P + NSLOT // P].bitcast(i32), pattern=[[P, NSLOT // P]], base=TOPK * TOK,
                          channel_multiplier=1))
            st.sync()
            g.memset(empty[:, :].rearrange("p (r c) -> p r c", c=XW)[:, :, D:XW], NOWHERE).then_inc(s_zero, 1)
            g.tensor_copy(tokf[:, :], toki[:, :]).then_inc(s_c, 1)
            g.tensor_copy(spare[:, :], ejm[:, P:P + NSLOT // P].bitcast(i32)).then_inc(s_c, 1)
            g.affine_select(out=ident[:, :], in_=ident[:, :], compare_op=ALU.not_equal, fill=1.0, base=0,
                            pattern=[[-1, P]], channel_multiplier=1).then_inc(s_c, 1)
            g.affine_select(out=below[:, :], in_=below[:, :], compare_op=ALU.is_gt, fill=0.0, base=0,
                            pattern=[[1, P]], channel_multiplier=-1).then_inc(s_c, 1)
            g.tensor_copy(eidx[:, :], widx[:, 0:E0]).then_inc(s_c, 1)
            g.tensor_copy(jidx[:, :], ejm[:, 0:NSLOT // TS].bitcast(i32)).then_inc(s_c, 1)
            g.tensor_copy(pidx[:, :], sloti[0][:, 0:1]).then_inc(s_c, 1)
            bmv = blockm[:, :].rearrange("p (h d) -> p h d", h=H1)
            st.did(g.affine_select(out=bmv, in_=bmv, compare_op=ALU.is_ge, fill=OFF, base=0,
                                   pattern=[[-DH1, H1], [0, DH1]], channel_multiplier=1))
            st.sync()
            g.affine_select(out=bmv, in_=bmv, compare_op=ALU.is_ge, fill=OFF, base=DH1 - 1,
                            pattern=[[DH1, H1], [0, DH1]], channel_multiplier=-1).then_inc(s_c, 1)
            pool.wait_ge(s_c, 9)
            g.tensor_copy(identb[:, :], ident[:, :]).then_inc(s_c, 1)

            def save(l):
                m = pre[l]
                with pool.Fori(0, NB // 2) as it:
                    for u in range(2):
                        b = it * 2 + u
                        pool.wait_ge(m["xs"], b + 1)
                        g.tensor_copy(xn_sb[l][:, bass.ds(b * 2, 2), 0:D], xs[u][:, :, :]).then_inc(m["xs_saved"], 1)

            def route_and_scatter(l):
                pool.wait_ge(rou[l]["routed"], 1)
                pool.wait_ge(s_xgz[l], NEMPTY[l] * 16)
                pool.wait_ge(pre[l]["xs_saved"], NB)
                for k in range(TOPK):
                    st.did(g.tensor_scalar(xn_sb[l][:, :, D], tokf[:, :], float(k * TOK), None, ALU.add))
                    st.link(g.tensor_copy(xn_sb[l][:, :, D + 1], wk[k][:, :]))
                    for t in range(T):
                        g.indirect_dma_start(
                            out=xg_dram[l], out_offset=bass.IndirectOffsetOnAxis(ap=sloti[k][:, t:t + 1].bitcast(u32), axis=0),
                            in_=xn_sb[l][:, t, :], in_offset=None).then_inc(rou[l]["scattered"], 16)
                    pool.wait_ge(rou[l]["scattered"], 16 * T * (k + 1))

            def store_outputs(l, nj):
                m = moe[l]
                with pool.Fori(0, nj // NWB) as it:
                    for v in range(NWB):
                        j, u = it * NWB + v, v % 2
                        outputs = pool.to_reg(j + 5)
                        pool.wait_ge(m["ids"], 3 + v)
                        pool.wait_ge(m["y"], outputs)
                        for s_ in range(2):
                            g.indirect_dma_start(
                                out=yg_dram[l], out_offset=bass.IndirectOffsetOnAxis(ap=yid[v][:, s_:s_ + 1].bitcast(u32), axis=0),
                                in_=yb[u][:, s_, :], in_offset=None).then_inc(m[f"stored{u}"], 16)

            for u in range(2):
                g.memset(vaug[u], 1.0).then_inc(A0["init"], 1)
            save(0)
            pool.wait_ge(s_ba, 1)
            g.memset(work[:, 0:H0 * BW], 0.0).then_inc(s_stk0, 1)
            route_and_scatter(0)
            store_outputs(0, NJ0)
            save(1)
            route_and_scatter(1)
            store_outputs(1, NJ1)

        @block.tensor
        def _(pe):
            mm, tr = nc.tensor.matmul, nc.tensor.transpose
            pe.wait_ge(s_c, 10)
            pe.wait_ge(s_w, 16 * NW)

            def pre_pe(l):
                m = pre[l]

                def transposes(b, u, turn):
                    pe.wait_ge(m["xs"], b + 1)
                    pe.wait_ge(m["xT"], b + 1)
                    tr(bank[u][:, 0:P], xs[u][:, 0, :], ident[:, :])
                    tr(bank[u][:, P:2 * P], xs[u][:, 1, :], ident[:, :]).then_inc(m["T"], 1)

                def project(b, u, turn):
                    pe.wait_ge(m["xT"], b + 3)
                    pe.wait_ge(m["qkf"], b + 1)
                    for i in range(2):
                        last = mm(bank[6 + u][:, i * S:(i + 1) * S], wqk_sb[:, i * D:(i + 1) * D], xT[u][:, :],
                                  start=True, stop=True)
                    last.then_inc(m["qkv"], 1)
                    pe.wait_ge(m["lg"], b + 1)
                    pe.wait_ge(m["v"], b + 1)
                    pe.wait_ge(m["sh"], b + 1)
                    for j in range(2):
                        mm(bank[2 + u][:, S + j * D:S + (j + 1) * D], xT[u][:, j * P:(j + 1) * P], wv_sb[:, :],
                           start=True, stop=True)
                        mm(bank[2 + u][:, j * E0:(j + 1) * E0], xT[u][:, j * P:(j + 1) * P], gate_sb[:, :],
                           start=True, stop=True)
                        o = bank[4 + u][:, j * D:(j + 1) * D]
                        mm(o, xT[u][:, j * P:(j + 1) * P], shw_sb[:, :], start=True, stop=False)
                        last = mm(o, ones[0:1, :], shb_sb[:, :], start=False, stop=True)
                    last.then_inc(m["gs"], 1)

                def router_hidden(b, u, turn):
                    pe.wait_ge(m["xT"], b + 3)
                    pe.wait_ge(m["rhs"], b + 1)
                    for c in range(2):
                        last = mm(bank[4 + u][:, c * S:(c + 1) * S], rw1_sb[:, c * P:(c + 1) * P], xT[u][:, :],
                                  start=True, stop=True)
                    last.then_inc(m["rh1"], 1)

                def router_logits(b, u, turn):
                    pe.wait_ge(m["rhs"], b + 3)
                    pe.wait_ge(m["lg"], b + 1)
                    for j in range(2):
                        for c in range(2):
                            last = mm(bank[2 + u][:, j * E1:(j + 1) * E1], rh[u][:, c, j * P:(j + 1) * P],
                                      rw2_sb[:, c, :], start=(c == 0), stop=(c == 1))
                    last.then_inc(m["gs"], 1)

                if l == 0:
                    staged(pe, [(transposes, 1), (project, 2)])
                else:
                    staged(pe, [(transposes, 1), (router_hidden, 2), (router_logits, 3)])

            def route_pe(l, ne):
                pe.wait_ge(rou[l]["A"], 1)
                pe.wait_ge(pre[l]["lg"], 2 + NB)
                mm(bank[0][:, 0:T * ne], below[:, :], rt[3][:, 0:T * ne], start=True, stop=True)
                mm(bank[1][:, 0:T * ne], ones[:, :], rt[3][:, 0:T * ne], start=True, stop=True).then_inc(rou[l]["cum"], 1)

            pre_pe(0)
            route_pe(0, E0)

            a = A0
            PA, PB, PO, PX, PY = bank[0:2], bank[2:4], bank[4:6], bank[6], bank[7]
            PXh = PX[:, :].bitcast(bf16)

            def max_scores(n, u, pair, i):
                t, qt = i // 2, i % 2
                o = PA[i % 2]
                if i % 8 == 0:
                    pe.wait_ge(a[f"stk{u}{i // 8}"], pair * 64 + 64)
                pe.wait_ge(a["Ared"], n * 16 + (i + 1))
                mm(o[:, :], qst[u][:, t, qt * P:(qt + 1) * P], kst[u][:, t, :, :], start=True, stop=False)
                v = P * (1 - qt)
                mm(o[:, :], identb[:, :], biasA[:, 2 * t:2 * t + 2, v:v + S], start=False, stop=True).then_inc(a["A"], 1)

            def transpose_maxima(n, g):
                pe.wait_ge(a["Ared"], n * 16 + (8 * g + 10))
                for q in range(2):
                    last = tr(PXh[0:H0 // 2, q * P:(q + 1) * P], nmax[:, q, 8 * g:8 * g + 8], identb[:, :])
                last.then_inc(a["mT"], 1)

            def exp_scores(b, u, h):
                o = PB[h % 2]
                if h % 8 == 0:
                    pe.wait_ge(a[f"M{h // 8}"], b * 32 + 32)
                pe.wait_ge(a["S"], b * 16 + (h + 1))
                for k in range(2):
                    last = mm(o[:, k * S:(k + 1) * S], kst[u][:, h // 2, h % 2, k * P:(k + 1) * P], qst[u][:, h // 2, :],
                              start=True, stop=True)
                last.then_inc(a["B"], 1)

            def weigh_values(b, u, h):
                gr, i = h // 4, h % 4
                pe.wait_ge(a["E"], b * 16 + (h + 1 + NSC))
                if h == 0:
                    pe.wait_ge(a["v_sb"], b + 1)
                if i == 0:
                    pe.wait_ge(a["oTs"], b * 4 + (gr + 1))
                for k in range(2):
                    last = mm(PO[gr % 2][32 * i:32 * i + DK + 1, 0:S], vaug[u][:, k, h, :], probs[h % NSC][:, k * S:(k + 1) * S],
                              start=(k == 0), stop=(k == 1))
                last.then_inc(a["PV"], 1)

            def transpose_outputs(b, q):
                pe.wait_ge(a["oTs"], b * 4 + 6)
                pe.wait_ge(a["s"], b + 1)
                for gr in range(4):
                    last = tr(bank[6 + q][:, gr * P:(gr + 1) * P], oT[:, gr, q * P:(q + 1) * P], ident[:, :])
                last.then_inc(a["To"], 1)

            def transpose_back(b):
                pe.wait_ge(a["on"], b * 2 + 2)
                for q in range(2):
                    last = tr(PX[:, q * P:(q + 1) * P], on[:, q, :], ident[:, :])
                last.then_inc(a["Tn"], 1)

            def project_out(b):
                pe.wait_ge(a["onT"], b + 1)
                for q in range(2):
                    last = mm(PY[:, q * D:(q + 1) * D], onT[:, q * P:(q + 1) * P], wo_sb[:, :], start=True, stop=True)
                last.then_inc(a["wo"], 1)

            def attend(b, u, pair, first=False, ahead=True):
                for h in range(H0):
                    exp_scores(b, u, h)
                    if ahead:
                        max_scores(b + 1, 1 - u, pair, h)
                    if h > 1:
                        weigh_values(b, u, h - 2)
                    elif not first:
                        weigh_values(b - 1, 1 - u, H0 - 2 + h)
                    if h == 1:
                        transpose_maxima(b, 1)
                    elif h in (5, 6) and not first:
                        pe.wait_ge(a["nmT"], b * 2 + 2)
                        transpose_outputs(b - 1, h - 5)
                    elif h == 8 and not first:
                        transpose_back(b - 1)
                    elif h == 12 and not first:
                        project_out(b - 1)
                    elif h == 10 and ahead:
                        if not first:
                            pe.wait_ge(a["onT"], b)
                        transpose_maxima(b + 1, 0)

            pe.wait_ge(s_ba, 1)
            pe.wait_ge(a["init"], 4)
            pe.wait_ge(rou[0]["routed"], 1)
            for i in range(H0):
                max_scores(0, 0, 0, i)
            transpose_maxima(0, 0)
            attend(0, 0, 0, first=True)
            with pe.Fori(0, NB // 2 - 1) as it:
                attend(it * 2 + 1, 1, it + 1)
                attend(it * 2 + 2, 0, it + 1)
            attend(NB - 1, 1, 0, ahead=False)
            for h in (H0 - 2, H0 - 1):
                weigh_values(NB - 1, 1, h)
            for q in range(2):
                transpose_outputs(NB - 1, q)
            transpose_back(NB - 1)
            project_out(NB - 1)

            def experts(l, nj):
                m = moe[l]
                XT, HP, YP = bank[0:2], (bank[2:4], bank[4:6]), bank[6:8]

                def transposes(j, u, half):
                    pe.wait_ge(m[f"xg{u}"], half * 16 + 16)
                    pe.wait_ge(m["xT"], j + 1)
                    tr(XT[u][:, 0:P], xg[u][:, 0, 0:D], ident[:, :])
                    tr(XT[u][:, P:2 * P], xg[u][:, 1, 0:D], ident[:, :]).then_inc(m["T"], 1)

                def up(j, v, fourth):
                    u = v % 2
                    pe.wait_ge(m[f"W{v}"], fourth * 16 + 16)
                    pe.wait_ge(m["xT"], j + 3)
                    pe.wait_ge(m["gelu"], j * 4 + 4)
                    for c in range(HC):
                        last = mm(HP[u][c // 2][:, (c % 2) * TS:(c % 2 + 1) * TS], wb[v][:, c * P:(c + 1) * P], xT[u][:, :],
                                  start=True, stop=True)
                        if c % 2:
                            last.then_inc(m["up"], 1)

                def down(j, v):
                    u = v % 2
                    pe.wait_ge(m["gelu"], j * 4 + 12)
                    pe.wait_ge(m["y"], j + 3)
                    for s_ in range(2):
                        for c in range(HC):
                            last = mm(YP[u][:, s_ * D:(s_ + 1) * D], hb[u][:, c, s_ * P:(s_ + 1) * P],
                                      wb[v][:, HID + c * D:HID + (c + 1) * D], start=(c == 0), stop=(c == HC - 1))
                    last.then_inc(m["down"], 1)

                transposes(0, 0, 0)
                up(0, 0, 0)
                transposes(1, 1, 0)
                for j in range(1, NWB):
                    up(j, j, 0)
                    transposes(j + 1, (j + 1) % 2, (j + 1) // 2)
                    down(j - 1, j - 1)
                with pe.Fori(1, nj // NWB - 1) as it:
                    for v in range(NWB):
                        j = it * NWB + v
                        up(j, v, it)
                        transposes(j + 1, (v + 1) % 2, it * 2 + (v + 1) // 2)
                        down(j - 1, (v - 1) % NWB)
                for j in range(nj - NWB, nj):
                    up(j, j % NWB, j // NWB)
                    if j + 1 < nj:
                        transposes(j + 1, (j + 1) % 2, (j + 1) // 2)
                    down(j - 1, (j - 1) % NWB)
                down(nj - 1, NWB - 1)

            experts(0, NJ0)
            pre_pe(1)
            route_pe(1, E1)

            a = A1
            pe.wait_ge(s_wf, 1)

            def gram(b, u, turn):
                pe.wait_ge(a["x2"], b + 1)
                pe.wait_ge(a["Cs"], b + 1)
                for j in range(2):
                    last = mm(bank[u][:, 0:D], x2[u][:, j, :], x2[u][:, j, :], start=(j == 0), stop=(j == 1))
                last.then_inc(a["C"], 1)

            def gram_times_weights(b, u, turn):
                pe.wait_ge(a["Cs"], b + 3)
                pe.wait_ge(a["pr"], b + 1)
                mm(bank[2 + u][:, 0:2 * D], cc[u], wqk1_sb[:, :], start=True, stop=True).then_inc(a["U"], 1)

            def norms(b, u, turn):
                pe.wait_ge(a["pr"], b + 3)
                pe.wait_ge(a["nns"], b + 1)
                for k in range(2):
                    last = mm(bank[4 + u][:, k:k + 1], pr[u][:, k * D:(k + 1) * D], ones[:, 0:1], start=True, stop=True)
                last.then_inc(a["nn"], 1)

            staged(pe, [(gram, 1), (gram_times_weights, 2), (norms, 3)])
            pe.wait_ge(a["nns"], NB + 2)

            def similarity(b, u, turn):
                pe.wait_ge(a["gk"], b + 1)
                mm(bank[2 + u][:, 0:D], wqk1_sb[:, D:2 * D], one(uu, b), start=True, stop=True).then_inc(a["G"], 1)

            def transpose_similarity(b, u, turn):
                pe.wait_ge(a["gk"], b + 3)
                pe.wait_ge(a["gm"], b + 1)
                tr(bank[4 + u][:, 0:P], gk[u], ident[:, :]).then_inc(a["GT"], 1)

            def weights_times_out(b, u, turn):
                pe.wait_ge(a["an"], b + 3)
                pe.wait_ge(a["Ms"], b + 1)
                mm(bank[6][:, 0:D], an[u], wo1_sb[:, :], start=True, stop=True).then_inc(a["M"], 1)

            def times_values(b, u, turn):
                pe.wait_ge(a["Ms"], b + 2)
                pe.wait_ge(a["Ps"], b + 1)
                mm(bank[1][:, 0:D], wv1_sb[:, :], ms[u], start=True, stop=True).then_inc(a["Pm"], 1)

            def transpose_rows(b, u, turn):
                pe.wait_ge(a["x2b"], b + 1)
                pe.wait_ge(a["x2T"], b + 2)
                tr(bank[0][:, 0:P], x2[u][:, 0, :], ident[:, :])
                tr(bank[0][:, P:2 * P], x2[u][:, 1, :], ident[:, :]).then_inc(a["T"], 1)

            def rows_times_all(b, u, turn):
                pe.wait_ge(a["Ps"], b + 2)
                pe.wait_ge(a["x2T"], b + 3)
                pe.wait_ge(a["s"], b + 1)
                for j in range(2):
                    last = mm(bank[7][:, j * D:(j + 1) * D], x2T[u][:, j * P:(j + 1) * P], ps_[u], start=True, stop=True)
                last.then_inc(a["F"], 1)

            staged(pe, [(similarity, 0), (transpose_similarity, 1), (weights_times_out, 3), (transpose_rows, 4),
                        (times_values, 4), (rows_times_all, 5)])
            experts(1, NJ1)

        @block.scalar
        def _(act):
            A = nc.scalar.activation
            act.sem_inc(pre[0]["xT"], 2)
            act.sem_inc(pre[0]["sh"], 2)
            act.sem_inc(pre[0]["qkf"], 2)
            act.sem_inc(pre[1]["rhs"], 2)
            for n, c in (("E", NSC), ("oTs", 2)):
                act.sem_inc(A0[n], c)
            for m in moe:
                act.sem_inc(m["gelu"], 8)
            for n, c in (("Cs", 2), ("x2T", 2), ("Ms", 1), ("Ps", 1)):
                act.sem_inc(A1[n], c)
            act.wait_ge(s_w, 16 * NW)
            A(et_c, temp_c, ACT.Exp).then_inc(s_act, 1)
            act.wait_ge(s_wf, 1)

            def pre_act(l):
                m = pre[l]

                def transposed(b, u, turn):
                    act.wait_ge(m["T"], b + 1)
                    act.wait_ge(m["gs"], b + 1)
                    A(xT[u][:, :], bank[u][:, 0:2 * P], ACT.Copy).then_inc(m["xT"], 1)

                def projected(b, u, turn):
                    act.wait_ge(m["qkv"], b + 1)
                    act.wait_ge(m["split"], b * 3 + 2)
                    A(qkf[u][:, 0:S], bank[6 + u][:, 0:S], ACT.Identity, scale=QSCALE, bias=bqs_c)
                    A(qkf[u][:, S:2 * S], bank[6 + u][:, S:2 * S], ACT.Identity, bias=bk_c).then_inc(m["qkf"], 1)
                    act.wait_ge(m["gs"], b + 3)
                    A(some(sh_sb, b * 2, 2), bank[4 + u][:, 0:2 * D].rearrange("p (j d) -> p j d", j=2), ACT.Copy
                      ).then_inc(m["sh"], 1)

                def hidden(b, u, turn):
                    act.wait_ge(m["rh1"], b + 3)
                    act.wait_ge(m["gs"], b + 1)
                    A(rh[u][:, 0, :], bank[4 + u][:, 0:S], ACT.Gelu, bias=rb1_sb[:, 0:1])
                    A(rh[u][:, 1, :], bank[4 + u][:, S:2 * S], ACT.Gelu, bias=rb1_sb[:, 1:2]).then_inc(m["rhs"], 1)

                if l == 0:
                    staged(act, [(transposed, 1), (projected, 2)])
                    act.wait_ge(s_strip, 16)
                    A(biasA[:, :, :], bass.AP(tensor=strip.tensor, offset=strip.offset + BW - 1,
                                              ap=[list(strip.ap)[0], [BW, H0], [-1, BW]]), ACT.Copy).then_inc(s_ba, 1)
                    act.wait_ge(m["sh"], NB + 2)
                    A(sh_sb, sh_sb, ACT.Gelu).then_inc(m["shg"], 1)
                else:
                    staged(act, [(hidden, 2)])

            def route_act(l, ne):
                act.wait_ge(rou[l]["lgx"], 1)
                A(rt[0][:, 0:T * ne], rt[0][:, 0:T * ne], ACT.Exp).then_inc(rou[l]["exped"], 1)

            pre_act(0)
            route_act(0, E0)

            a = A0
            PO, PX = bank[4:6], bank[6]

            def fetch_values(n, u):
                act.wait_ge(a["PV"], n * 16 + 16)
                src = vall[:, 2 * n:2 * n + 2, :] if isinstance(n, int) else vall[:, bass.ds(n * 2, 2), :]
                A(vaug[u][:, :, :, 0:DK], src.rearrange("p k (h d) -> p k h d", d=DK), ACT.Copy).then_inc(a["v_sb"], 1)

            def copy_maxima(n, g):
                act.wait_ge(a["mT"], n * 2 + (g + 3))
                if not isinstance(n, int) or n:
                    act.wait_ge(a[f"M{g}"], n * 32)
                A(nmaxT[g][0:H0 // 2, :], PX[:, :].bitcast(bf16)[0:H0 // 2, 0:S], ACT.Copy).then_inc(a["nmT"], 1)

            def copy_group(b, gr, first=False):
                act.wait_ge(a["PV"], b * 16 + (4 * gr + 36))
                if not first:
                    act.wait_ge(a["To"], b * 2)
                A(oT[:, gr, :], PO[gr % 2][:, 0:S], ACT.Copy).then_inc(a["oTs"], 1)

            def add_value_bias(b):
                act.wait_ge(a["Tn"], b + 1)
                A(onT, PX[:, 0:2 * P], ACT.Identity, bias=bv_c).then_inc(a["onT"], 1)

            def attend_act(b, u, first=False, ahead=True):
                for h in range(H0):
                    act.wait_ge(a["S"], b * 16 + (h + 3))
                    act.wait_ge(a["PV"], b * 16 + (h + 33 - NSC))
                    A(probs[h % NSC], scores[h % NSC], ACT.Exp).then_inc(a["E"], 1)
                    if h == 2:
                        copy_maxima(b, 1)
                    elif h == 3 and not first:
                        copy_group(b - 1, 3)
                    elif h == 4 and ahead:
                        fetch_values(b + 1, 1 - u)
                    elif h % 4 == 3 and h > 3:
                        copy_group(b, h // 4 - 1, first)
                    elif h == 9 and not first:
                        add_value_bias(b - 1)
                    elif h == 12 and ahead:
                        copy_maxima(b + 1, 0)

            act.wait_ge(s_c, 10)
            act.wait_ge(a["init"], 4)
            act.wait_ge(pre[0]["v"], NB + 2)
            fetch_values(0, 0)
            copy_maxima(0, 0)
            attend_act(0, 0, first=True)
            with act.Fori(0, NB // 2 - 1) as it:
                attend_act(it * 2 + 1, 1)
                attend_act(it * 2 + 2, 0)
            attend_act(NB - 1, 1, ahead=False)
            copy_group(NB - 1, 3)
            add_value_bias(NB - 1)

            def experts(l, nj):
                m = moe[l]
                with act.Fori(0, nj // NWB) as it:
                    for v in range(NWB):
                        j, u = it * NWB + v, v % 2
                        act.wait_ge(m[f"W{v}"], it * 16 + 16)
                        act.wait_ge(m["down"], j + 1)
                        for c in range(HC):
                            if c % 2 == 0:
                                act.wait_ge(m["up"], j * 2 + (5 + c // 2))
                            bc = HID + HC * D + c
                            A(hb[u][:, c, :], bank[2 + 2 * u + c // 2][:, (c % 2) * TS:(c % 2 + 1) * TS], ACT.Gelu,
                              bias=wb[v][:, bc:bc + 1]).then_inc(m["gelu"], 1)

            def silus(l):
                for q in range(4):
                    act.wait_ge(com[l]["z"], q + 1)
                    A(yy[:, 0, q * 8:q * 8 + 8, :], yy[:, 0, q * 8:q * 8 + 8, :], ACT.Silu).then_inc(com[l]["silu"], 1)

            experts(0, NJ0)
            act.wait_ge(com[0]["stats"], 1)
            for t in range(8, T):
                ins = A(yy[:, 0, t, :], yy[:, 0, t, :], ACT.Identity, scale=rstd[:, t:t + 1], bias=var[:, t:t + 1])
                if t % 8 == 7:
                    ins.then_inc(com[0]["normed"], 1)
            silus(0)
            pre_act(1)
            route_act(1, E1)

            a = A1

            def copy_gram(b, u, turn):
                act.wait_ge(a["C"], b + 3)
                act.wait_ge(a["U"], b + 1)
                A(cc[u], bank[u][:, 0:D], ACT.Copy).then_inc(a["Cs"], 1)

            staged(act, [(copy_gram, 1)])

            def exponents(b, u, turn):
                act.wait_ge(a["mx"], b + 1)
                act.wait_ge(a["an"], b + 1)
                A(at1[u], gm[u], ACT.Exp, bias=nm1[u], accum_out=sm1[u]).then_inc(a["exp"], 1)

            def copy_product(b, u, turn):
                act.wait_ge(a["M"], b + 3)
                act.wait_ge(a["Pm"], b + 1)
                A(ms[u], bank[6][:, 0:D], ACT.Copy).then_inc(a["Ms"], 1)

            def copy_rows(b, u, turn):
                act.wait_ge(a["T"], b + 3)
                act.wait_ge(a["F"], b + 1)
                A(x2T[u], bank[0][:, 0:2 * P], ACT.Copy).then_inc(a["x2T"], 1)

            def scale_product(b, u, turn):
                act.wait_ge(a["Pm"], b + 3)
                A(ps_[u], bank[1][:, 0:D], ACT.Copy, scale=nw_c).then_inc(a["Ps"], 1)

            staged(act, [(exponents, 2), (copy_product, 3), (copy_rows, 4), (scale_product, 4)])
            experts(1, NJ1)
            silus(1)

        @block.vector
        def _(dve):
            V = nc.vector
            st = Steps(dve, s_dve)
            for m in pre:
                dve.sem_inc(m["lg"], 2)
                dve.sem_inc(m["gs"], 2)
            dve.sem_inc(pre[0]["v"], 2)
            dve.sem_inc(pre[0]["split"], 6)
            for u in range(2):
                dve.sem_inc(pre[0][f"stored{u}"], STORES * 16)
            dve.sem_inc(pre[1]["rh1"], 2)
            dve.sem_inc(pre[1]["xT"], 2)
            for n, c in (("s", 2), ("Ared", 2), ("S", 2), ("B", 32), ("PV", 32), ("mT", 2)):
                dve.sem_inc(A0[n], c)
            for m in moe:
                for n, c in (("xT", 2), ("y", 4), ("ids", 2), ("T", 2), ("up", 4), ("down", 2)):
                    dve.sem_inc(m[n], c)
            for n, c in (("pr", 2), ("nns", 2), ("gk", 2), ("gm", 2), ("s", 1), ("U", 2), ("F", 2), ("C", 2), ("nn", 2),
                         ("GT", 2), ("exp", 2), ("M", 2), ("an", 2), ("Pm", 2), ("T", 2)):
                dve.sem_inc(A1[n], c)

            def rsqrt(y, v, t1, t2):
                yi, vi = y.bitcast(i32), v.bitcast(i32)
                st.link(V.tensor_scalar(t1.bitcast(i32), vi, 1, None, ALU.logical_shift_right))
                st.link(V.tensor_scalar(yi, t1.bitcast(i32), -1.0, float(0x5f3759df), ALU.mult, ALU.add))
                for _ in range(3):
                    st.link(V.tensor_tensor(t2, y, y, ALU.mult))
                    st.link(V.tensor_tensor(t1, t2, v, ALU.mult))
                    st.link(V.tensor_scalar(t1, t1, -0.5, 1.5, ALU.mult, ALU.add))
                    st.link(V.tensor_tensor(y, y, t1, ALU.mult))

            def take_stats(src, q):
                for t in range(q * 8, q * 8 + 8):
                    st.did(V.bn_stats(stats[:, t, :], src(t)))

            def finish_stats():
                st.sync()
                m0, v0, m1, v1 = (stats[:, :, i] for i in (1, 2, 4, 5))
                st.did(V.tensor_tensor(tmpa[:, :], m0, m1, ALU.add))
                st.did(V.tensor_tensor(tmpb[:, :], m0, m1, ALU.subtract))
                st.link(V.tensor_tensor(var[:, :], v0, v1, ALU.add))
                st.did(V.tensor_scalar(mean[:, :], tmpa[:, :], 0.5, None, ALU.mult))
                st.link(V.tensor_tensor(tmpb[:, :], tmpb[:, :], tmpb[:, :], ALU.mult))
                st.did(V.tensor_scalar(var[:, :], var[:, :], 1.0 / D, None, ALU.mult))
                st.link(V.tensor_scalar(tmpb[:, :], tmpb[:, :], 0.25, None, ALU.mult))
                st.link(V.tensor_tensor(var[:, :], var[:, :], tmpb[:, :], ALU.add))
                st.link(V.tensor_scalar(tmpb[:, :], var[:, :], LN_EPS, None, ALU.add))
                rsqrt(rstd[:, :], tmpb[:, :], tmpa[:, :], rrms[:, :])

            def pre_dve(l, ne):
                m = pre[l]
                src = (x_sb, xres)[l]

                def normalise(b, u, turn):
                    if not isinstance(b, int) or b >= 2:
                        dve.wait_ge(m["T"], b - 1)
                        dve.wait_ge(m["xs_saved"], b - 1)
                    for j in range(2):
                        t = b * 2 + j
                        last = V.tensor_scalar(xs[u][:, j, :], one(src, t), some(mean, t, 1), some(rstd, t, 1),
                                               ALU.subtract, ALU.mult)
                    last.then_inc(m["xs"], 1)

                def transposed(b, u, turn):
                    dve.wait_ge(m["T"], b + 1)
                    dve.wait_ge(m["rh1"], b + 1)
                    V.tensor_copy(xT[u][:, :], bank[u][:, 0:2 * P]).then_inc(m["xT"], 1)

                def split(b, u, turn):
                    dve.wait_ge(m["qkf"], b + 3)
                    dve.wait_ge(m[f"stored{u}"], turn * (STORES * 16) + STORES * 16)
                    hi, mi, lo = (pieces[u][:, c, :] for c in range(3))
                    V.tensor_copy(hi, qkf[u]).then_inc(m["split"], 1)
                    dve.wait_ge(m["split"], b * 3 + 7)
                    V.tensor_tensor(qkr, qkf[u], hi, ALU.subtract).then_inc(m["split"], 1)
                    dve.wait_ge(m["split"], b * 3 + 8)
                    V.tensor_copy(mi, qkr).then_inc(m["split"], 1)
                    dve.wait_ge(m["split"], b * 3 + 9)
                    V.tensor_tensor(lo, qkr, mi, ALU.subtract).then_inc(m["pieces"], 1)

                def logits(b, u, turn):
                    dve.wait_ge(m["gs"], b + 3)
                    bk = bank[2 + u][:, 0:2 * ne].rearrange("p (j e) -> p j e", j=2)
                    dst = some(lg, b * 2, 2)[:, :, 0:ne]
                    if l == 0:
                        V.tensor_copy(dst, bk).then_inc(m["lg"], 1)
                        V.tensor_copy(some(vall, b * 2, 2), bank[2 + u][:, S:2 * S].rearrange("p (j d) -> p j d", j=2)
                                      ).then_inc(m["v"], 1)
                    else:
                        V.tensor_tensor(dst, bk, mid(rb2_bc[:, :], 2), ALU.add).then_inc(m["lg"], 1)

                if l == 0:
                    staged(dve, [(normalise, 0), (logits, 3), (split, 3)])
                else:
                    staged(dve, [(normalise, 0), (transposed, 1), (logits, 3)])

            def route(l, ne, nj):
                r = rou[l]
                n = T * ne
                v3 = lambda t: t[:, 0:n].rearrange("p (t e) -> p t e", e=ne)
                logit = lg[:, :, 0:ne]
                e0, e1, e2, e3 = (v3(x_) for x_ in rt)
                hots = [v3(h) for h in hot]
                dve.wait_ge(pre[l]["lg"], NB + 2)
                st.link(V.reduce_max(tmpa[:, :], logit, AX.X))
                V.tensor_tensor(e0, logit, over(tmpa[:, :], ne), ALU.subtract).then_inc(r["lgx"], 1)
                dve.wait_ge(r["exped"], 1)
                st.link(V.reduce_sum(tmpb[:, :], e0, AX.X))
                st.link(V.reciprocal(tmpb[:, :], tmpb[:, :]))
                st.link(V.tensor_tensor(e0, e0, over(tmpb[:, :], ne), ALU.mult))
                eb = mid(eidx[:, E0 - ne:E0], T)
                for k in range(TOPK):
                    src = logit if k == 0 else e1
                    if k:
                        st.link(V.scalar_tensor_tensor(e1.rearrange("p t e -> p (t e)"), hot[0][:, 0:n], OFF,
                                                       rt[3][:, 0:n], ALU.mult, ALU.add))
                        st.link(V.reduce_max(tmpa[:, :], e1, AX.X))
                    else:
                        st.did(V.tensor_copy(e3, logit))
                    st.link(V.tensor_tensor(e2, src, over(tmpa[:, :], ne), ALU.is_equal))
                    st.link(V.tensor_tensor(e2, e2, eb, ALU.mult))
                    st.link(V.tensor_reduce(tmpb[:, :], e2, AX.X, ALU.min))
                    st.link(V.tensor_tensor(hots[k], eb, over(tmpb[:, :], ne), ALU.is_equal))
                    st.link(V.tensor_tensor(e2, e0, hots[k], ALU.mult))
                    st.link(V.reduce_sum(pk[k][:, :], e2, AX.X))
                V.tensor_tensor(rt[3][:, 0:n], hot[0][:, 0:n], hot[1][:, 0:n], ALU.add).then_inc(r["A"], 1)
                if l == 0:
                    st.link(V.tensor_tensor(tmpa[:, :], pk[0][:, :], pk[1][:, :], ALU.add))
                    st.link(V.reciprocal(tmpa[:, :], tmpa[:, :]))
                    for k in range(TOPK):
                        st.did(V.tensor_tensor(wk[k][:, :], pk[k][:, :], tmpa[:, :], ALU.mult))
                else:
                    for k in range(TOPK):
                        st.did(V.tensor_copy(wk[k][:, :], pk[k][:, :]))
                dve.wait_ge(r["cum"], 1)
                et_ = lambda t: t[:, 0:n].rearrange("p (e t) -> p e t", t=T)
                st.link(V.tensor_copy(et_(rt[1]), bank[1][:, 0:n].rearrange("p (t e) -> p e t", e=ne)))
                st.link(V.memset(rt[2][:, 0:n], 1.0))
                st.link(V.tensor_tensor_scan(rt[0][:, 0:n], rt[2][:, 0:n], rt[1][:, 0:n], 0.0, ALU.mult, ALU.add))
                st.link(V.tensor_tensor(rt[1][:, 0:n], rt[0][:, 0:n], rt[1][:, 0:n], ALU.subtract))
                first = et_(rt[1])[:, :, 0]
                cnt, tend, tmp, off = (e[:, 0:ne] for e in ecnt)
                st.link(V.tensor_tensor(cnt, et_(rt[0])[:, :, T - 1], first, ALU.subtract))
                st.link(V.tensor_scalar(ecnti[:, 0:ne], cnt, float(TS - 1), None, ALU.add))
                st.link(V.tensor_scalar(ecnti[:, 0:ne], ecnti[:, 0:ne], TS.bit_length() - 1, None, ALU.logical_shift_right))
                st.link(V.tensor_copy(cnt, ecnti[:, 0:ne]))
                st.link(V.tensor_tensor_scan(tend, rt[2][:, 0:ne], cnt, 0.0, ALU.mult, ALU.add))
                st.link(V.tensor_tensor(tmp, tend, cnt, ALU.subtract))
                st.link(V.scalar_tensor_tensor(off, tmp, float(TS), first, ALU.mult, ALU.subtract))
                st.link(V.tensor_tensor(e2, v3(bank[0]), et_(rt[1]).rearrange("p e t -> p t e"), ALU.add))
                st.link(V.tensor_tensor(e2, e2, mid(off, T), ALU.add))
                for k in range(TOPK):
                    st.link(V.tensor_tensor(e0, e2, hots[k], ALU.mult))
                    st.link(V.reduce_sum(slotf[k][:, :], e0, AX.X))
                    st.did(V.tensor_copy(sloti[k][:, :], slotf[k][:, :]))
                ej = ejm[:, 0:nj * ne].rearrange("p (j e) -> p j e", e=ne)
                st.link(V.tensor_tensor(ej, mid(tend, nj), over(jidx[:, 0:nj], ne), ALU.is_le))
                st.link(V.reduce_sum(ejf[:, 0:nj], ej, AX.X))
                st.link(V.tensor_scalar(ejf[:, 0:nj], ejf[:, 0:nj], float(ne - 1), float(P), ALU.min, ALU.mult))
                V.tensor_scalar(widx[:, 0:nj], ejf[:, 0:nj], pidx[:, :], None, ALU.add).then_inc(r["routed"], 1)

            dve.wait_ge(s_relb, 16)
            lo, hi = S - 1 - MAXREL, S + MAXREL
            V.tensor_copy(ext_sb[:, 0:lo], ext_sb[:, lo:lo + 1].broadcast_to([H0, lo])).then_inc(s_edge, 1)
            V.tensor_copy(ext_sb[:, hi:EXT], ext_sb[:, hi - 1:hi].broadcast_to([H0, EXT - hi])).then_inc(s_edge, 1)
            dve.wait_ge(s_edge, 2)
            es = ext_sb[:, :]
            V.tensor_copy(extr_sb[:, :], bass.AP(tensor=es.tensor, offset=es.offset + EXT - 1, ap=[list(es.ap)[0], [-1, EXT]])
                          ).then_inc(s_edge, 1)
            for q in range(4):
                dve.wait_ge(s_x[q], 16)
                take_stats(lambda t: x_sb[:, t, :], q)
            finish_stats()
            dve.wait_ge(s_w, 16 * NW)
            st.did(V.tensor_scalar(bqs_c, bq_c, QSCALE, None, ALU.mult))
            V.tensor_scalar(wqk1_sb[:, :], wqk1_sb[:, :], nw_c, None, ALU.mult).then_inc(s_wf, 1)
            pre_dve(0, E0)
            dve.wait_ge(s_c, 10)
            dve.wait_ge(pre[0]["sh"], NB + 2)
            for i in (4, 5):
                V.memset(bank[i][:, :], 0.0).then_inc(A0["init"], 1)
            route(0, E0, NJ0)

            a = A0
            dve.wait_ge(s_bt, 16)

            def reduce_maxima(n, i):
                t, qt = i // 2, i % 2
                dve.wait_ge(a["A"], n * 16 + (i + 1))
                if i % 8 == 0:
                    dve.wait_ge(a["mT"], n * 2 + (i // 8 + 1))
                V.tensor_reduce(nmax[:, qt, 2 * t:2 * t + 2], bank[i % 2][:, :].rearrange("p (h k) -> p h k", h=2),
                                AX.X, ALU.max, negate=True).then_inc(a["Ared"], 1)

            def add_bias(b, h):
                dve.wait_ge(a["B"], b * 16 + (h + 33))
                dve.wait_ge(a["E"], b * 16 + (h + 1))
                bt = biasT[:, h, :]
                V.tensor_tensor(scores[h % NSC].rearrange("p (j q) -> p j q", j=2),
                                bank[2 + h % 2][:, :].rearrange("p (j q) -> p j q", j=2),
                                bass.AP(tensor=bt.tensor, offset=bt.offset + S - 1, ap=[list(bt.ap)[0], [P, 2], [-1, S]]),
                                ALU.add).then_inc(a["S"], 1)

            def normalise_outputs(b, q):
                dve.wait_ge(a["To"], b * 2 + (q + 1))
                o = bank[6 + q][:, :].rearrange("p (h c) -> p h c", c=32)
                V.reciprocal(rden[:, q, :], o[:, :, DK]).then_inc(a["s2"], 1)
                dve.wait_ge(a["s2"], b * 2 + (q + 1))
                V.tensor_tensor(on[:, q, :].rearrange("p (h d) -> p h d", d=DK), o[:, :, 0:DK],
                                over(rden[:, q, :], DK), ALU.mult).then_inc(a["on"], 1)

            def keep_result(b):
                dve.wait_ge(a["wo"], b + 1)
                dst = s_sb[:, 2 * b:2 * b + 2, :] if isinstance(b, int) else s_sb[:, bass.ds(b * 2, 2), :]
                V.tensor_tensor(dst, bank[7][:, 0:2 * D].rearrange("p (q d) -> p q d", q=2), mid(bo_bc[:, :], 2),
                                ALU.add).then_inc(a["s"], 1)

            def attend_dve(b, first=False, ahead=True):
                for h in range(H0):
                    add_bias(b, h)
                    if ahead:
                        reduce_maxima(b + 1, h)
                    if h in (6, 7) and not first:
                        normalise_outputs(b - 1, h - 6)
                    elif h == 13 and not first:
                        keep_result(b - 1)

            for i in range(H0):
                reduce_maxima(0, i)
            attend_dve(0, first=True)
            with dve.Fori(0, NB // 2 - 1) as it:
                attend_dve(it * 2 + 1)
                attend_dve(it * 2 + 2)
            attend_dve(NB - 1, ahead=False)
            for q in range(2):
                normalise_outputs(NB - 1, q)
            keep_result(NB - 1)

            def experts(l, nj):
                m = moe[l]

                def copy_rows(j, v, half):
                    u = v % 2
                    dve.wait_ge(m["T"], j + 3)
                    dve.wait_ge(m["up"], j * 2 + 2)
                    V.tensor_copy(xT[u][:, :], bank[u][:, 0:2 * P]).then_inc(m["xT"], 1)
                    if not isinstance(j, int) or j >= NWB:
                        dve.wait_ge(m[f"stored{u}"], half * 32 - 32)
                    V.tensor_tensor(yid[v], xg[u][:, :, D], spare[:, j * 2:j * 2 + 2] if isinstance(j, int) else
                                    spare[:, bass.ds(j * 2, 2)], ALU.min)
                    V.tensor_copy(yw[v], xg[u][:, :, D + 1]).then_inc(m["ids"], 1)

                def outputs(j, v, half):
                    u = v % 2
                    dve.wait_ge(m["down"], j + 3)
                    if not isinstance(j, int) or j >= 2:
                        dve.wait_ge(m[f"stored{u}"], half * 32)
                    V.tensor_tensor(yb[u], bank[6 + u][:, 0:2 * D].rearrange("p (s d) -> p s d", s=2),
                                    mid(wb[v][:, WROW - D:WROW], 2), ALU.add).then_inc(m["yb"], 1)
                    dve.wait_ge(m["yb"], j + 1)
                    V.tensor_tensor(yb[u], yb[u], over(yw[v], D), ALU.mult).then_inc(m["y"], 1)

                copy_rows(0, 0, 0)
                copy_rows(1, 1, 0)
                for j in range(NWB):
                    copy_rows(j + 2, (j + 2) % NWB, (j + 2) // 2)
                    outputs(j, j, j // 2)
                with dve.Fori(1, nj // NWB - 1) as it:
                    for v in range(NWB):
                        copy_rows(it * NWB + (v + 2), (v + 2) % NWB, it * 2 + (v + 2) // 2)
                        outputs(it * NWB + v, v, it * 2 + v // 2)
                for j in range(nj - NWB, nj):
                    if j + 2 < nj:
                        copy_rows(j + 2, (j + 2) % NWB, (j + 2) // 2)
                    outputs(j, j % NWB, j // 2)

            def add_choices(l, q):
                dve.wait_ge(com[l][f"g{q}"], 16 * TOPK)
                y0, y1 = (yy[:, k, q * 8:q * 8 + 8, :] for k in range(TOPK))
                return V.tensor_tensor(y0, y0, y1, ALU.add)

            experts(0, NJ0)
            dve.wait_ge(pre[0]["shg"], 1)
            for q in range(4):
                z, sh = yy[:, 0, q * 8:q * 8 + 8, :], sh_sb[:, q * 8:q * 8 + 8, :]
                st.link(add_choices(0, q))
                st.link(V.scalar_tensor_tensor(z, sh, 0.5, z, ALU.mult, ALU.add))
                take_stats(lambda t: yy[:, 0, t, :], q)
            finish_stats()
            st.link(V.tensor_tensor(var[:, :], mean[:, :], rstd[:, :], ALU.mult))
            V.tensor_scalar(var[:, :], var[:, :], -1.0, None, ALU.mult).then_inc(com[0]["stats"], 1)
            for q in range(4):
                if q == 0:
                    for t in range(8):
                        st.did(V.tensor_scalar(yy[:, 0, t, :], yy[:, 0, t, :], mean[:, t:t + 1], rstd[:, t:t + 1],
                                               ALU.subtract, ALU.mult))
                    st.sync()
                else:
                    dve.wait_ge(com[0]["normed"], q)
                z = yy[:, 0, q * 8:q * 8 + 8, :]
                st.link(V.tensor_tensor(z, z, mid(gamma_bc[:, :], 8), ALU.mult))
                V.tensor_tensor(z, z, mid(beta_bc[:, :], 8), ALU.add).then_inc(com[0]["z"], 1)
            dve.wait_ge(s_x2, 16)
            for q in range(4):
                z, r_, s_ = (b_[:, q * 8:q * 8 + 8, :] for b_ in (yy[:, 0], xres, s_sb))
                dve.wait_ge(com[0]["silu"], q + 1)
                st.link(V.tensor_tensor(z, z, s_, ALU.mult))
                st.link(V.tensor_tensor(r_, r_, z, ALU.add))
                take_stats(lambda t: xres[:, t, :], q)
            finish_stats()
            st.link(V.tensor_tensor(tmpa[:, :], rstd[:, :], rstd[:, :], ALU.mult))
            st.link(V.tensor_tensor(tmpa[:, :], tmpa[:, :], var[:, :], ALU.mult))
            st.link(V.tensor_scalar(var[:, :], tmpa[:, :], RMS_EPS, None, ALU.add))
            rsqrt(rrms[:, :], var[:, :], tmpa[:, :], tmpb[:, :])
            pre_dve(1, E1)
            route(1, E1, NJ1)

            a = A1
            xn1 = xn_sb[1]
            dve.wait_ge(pre[1]["xs_saved"], NB)
            dve.wait_ge(s_act, 1)

            def scale_rows(b, u, name, used):
                dve.wait_ge(a[used], b + 1)
                for j in range(2):
                    t = b * 2 + j
                    last = V.tensor_scalar(x2[u][:, j, :], one(xn1, t)[:, 0:D] if isinstance(t, int) else
                                           xn1[:, bass.ds(t, 1), 0:D].rearrange("p o d -> p (o d)"),
                                           some(rrms, t, 1), None, ALU.mult)
                last.then_inc(a[name], 1)

            def products(b, u, turn):
                dve.wait_ge(a["U"], b + 3)
                dve.wait_ge(a["nn"], b + 1)
                V.tensor_copy(one(uu, b), bank[2 + u][:, 0:D])
                V.tensor_tensor(pr[u], bank[2 + u][:, 0:2 * D], wqk1_sb[:, :], ALU.mult).then_inc(a["pr"], 1)

            def keep_norms(b, u, turn):
                dve.wait_ge(a["nn"], b + 3)
                V.tensor_copy(one(nsq, b), bank[4 + u][:, 0:2]).then_inc(a["nns"], 1)

            staged(dve, [(lambda b, u, turn: scale_rows(b, u, "x2", "C"), 0), (products, 2), (keep_norms, 3)])
            dve.wait_ge(a["nns"], NB + 2)
            nf, rf = nsq.rearrange("p b k -> p (b k)"), rin.rearrange("p b k -> p (b k)")
            st.link(V.tensor_scalar(nf, nf, 1e-24, None, ALU.max))
            rsqrt(rf, nf, nt1, nt2)
            st.link(V.tensor_scalar(rin[:, :, 0], rin[:, :, 0], et_c, None, ALU.mult))

            def inverse_norm(b, k):
                return rin[:, b, k:k + 1] if isinstance(b, int) else rin[:, bass.ds(b, 1), k]

            def scale_by_keys(b, u, turn):
                dve.wait_ge(a["G"], b + 1)
                dve.wait_ge(a["GT"], b + 1)
                V.tensor_scalar(gk[u], bank[2 + u][:, 0:D], inverse_norm(b, 1), None, ALU.mult).then_inc(a["gk"], 1)

            def scale_by_queries(b, u, turn):
                dve.wait_ge(a["GT"], b + 3)
                dve.wait_ge(a["exp"], b + 1)
                V.scalar_tensor_tensor(gm[u], bank[4 + u][:, 0:P], inverse_norm(b, 0), blockm[:, :], ALU.mult,
                                       ALU.add).then_inc(a["gm"], 1)
                dve.wait_ge(a["gm"], b + 3)
                V.tensor_reduce(nm1[u], gm[u], AX.X, ALU.max, negate=True).then_inc(a["mx"], 1)

            def normalise_weights(b, u, turn):
                dve.wait_ge(a["exp"], b + 3)
                V.reciprocal(rs1[u], sm1[u]).then_inc(a["rs"], 1)
                dve.wait_ge(a["rs"], b + 1)
                dve.wait_ge(a["M"], b + 1)
                V.tensor_scalar(an[u], at1[u], rs1[u], None, ALU.mult).then_inc(a["an"], 1)

            def keep_result1(b, u, turn):
                dve.wait_ge(a["F"], b + 3)
                V.tensor_copy(some(s_sb, b * 2, 2), bank[7][:, 0:2 * D].rearrange("p (j d) -> p j d", j=2)
                              ).then_inc(a["s"], 1)

            staged(dve, [(scale_by_keys, 0), (scale_by_queries, 1), (normalise_weights, 2),
                         (lambda b, u, turn: scale_rows(b, u, "x2b", "T"), 3), (keep_result1, 5)])
            experts(1, NJ1)
            for q in range(4):
                add_choices(1, q).then_inc(com[1]["z"], 1)
            for q in range(4):
                z, r_, s_ = (b_[:, q * 8:q * 8 + 8, :] for b_ in (yy[:, 0], xres, s_sb))
                dve.wait_ge(com[1]["silu"], q + 1)
                st.link(V.tensor_tensor(z, z, s_, ALU.mult))
                V.tensor_tensor(z, r_, z, ALU.add).then_inc(com[1]["x1"], 1)


def kernel(**inputs):
    import numpy as _np
    import concourse.bacc as _bacc
    from concourse import mybir as _mybir
    from concourse.bass_utils import run_bass_kernel_spmd as _run

    i = {k: _np.asarray(v) for k, v in inputs.items()}

    def column(v, chunks=1):
        return v.reshape(chunks, P).T

    def expert_rows(w1, b1, w2, b2):
        e = w1.shape[0]
        w2r = w2.reshape(e, HC, P, D).transpose(0, 2, 1, 3).reshape(e, P, HC * D)
        b1r = b1.reshape(e, HC, P).transpose(0, 2, 1)
        b2r = _np.repeat(b2[:, None, :], P, axis=1)
        return _np.concatenate([w1, w2r, b1r, b2r], axis=2).reshape(e * P, WROW)

    wqkv = i["L1_attn_w_qkv"]
    pack = [i["L0_attn_Wq"].T, i["L0_attn_Wk"].T, i["L0_attn_Wv"].T, i["L0_attn_Wo"].T, i["L0_ffn_gate_W"],
            i["L0_ffn_shared_W"], wqkv[0:2 * D].T, wqkv[2 * D:], i["L1_attn_w_out"].T, i["L1_ffn_rW1"],
            column(i["L1_ffn_rb1"], 2), i["L1_ffn_rW2"].reshape(2, P, E1).transpose(1, 0, 2).reshape(P, 2 * E1),
            column(i["L0_attn_bq"]), column(i["L0_attn_bk"]), column(i["L0_attn_bv"]), column(i["L1_attn_norm_weight"]),
            _np.repeat(i["L1_attn_temperature"].reshape(H1), DH1)[:, None]]
    host = [
        ("x", i["L0_attn_x"].reshape(TOK, D)),
        ("wpack", _np.concatenate(pack, axis=1)),
        ("vectors", _np.concatenate([i["L0_attn_bo"], i["L0_ffn_gamma"], i["L0_ffn_beta"], i["L1_ffn_rb2"]])),
        ("shb", i["L0_ffn_shared_b"]), ("relb", i["L0_attn_rel_bias"]),
        ("wcat0", expert_rows(i["L0_ffn_W1"], i["L0_ffn_b1"], i["L0_ffn_W2"], i["L0_ffn_b2"])),
        ("wcat1", expert_rows(i["L1_ffn_We1"], i["L1_ffn_be1"], i["L1_ffn_We2"], i["L1_ffn_be2"])),
    ]
    nc = _bacc.Bacc("TRN2", target_bir_lowering=False, num_devices=1)
    arrays, args = {}, []
    for name, a in host:
        a = _np.ascontiguousarray(a)
        arrays[f"in_{name}"] = a
        args.append(nc.dram_tensor(f"in_{name}", a.shape, _mybir.dt.from_np(a.dtype), kind="ExternalInput").ap())
    args.append(nc.dram_tensor("out_x", (TOK, D), _mybir.dt.float32, kind="ExternalOutput").ap())
    build(nc, *args)
    r = _run(nc, [arrays], core_ids=[0])
    return r.results[0]["out_x"].reshape(NB, S, D)
```
